# Optimizing a Trainium2 kernel written in Bass

```python
import numpy as np
import jax
import jax.numpy as jnp

def _softmax(x, axis=-1):
    return jax.nn.softmax(x, axis=axis)

def _gelu(x):
    return jax.nn.gelu(x, approximate=True)

def _silu(x):
    return jax.nn.silu(x)

def _sigmoid(x):
    return jax.nn.sigmoid(x)

def _layernorm(x, axis=-1, eps=1e-05):
    m = jnp.mean(x, axis=axis, keepdims=True)
    v = jnp.var(x, axis=axis, keepdims=True)
    return (x - m) / jnp.sqrt(v + eps)

def _scatter_add(tgt, idx, src, axis=0):
    return tgt.at[idx].add(src)

def _segment_sum(src, seg, n):
    return jax.ops.segment_sum(src, seg, n)
kernel_name = 'mk_prb_d2_jaxref_r8_37a456'

def setup_inputs(seed: int=0):
    np.random.seed(seed)
    _w = jnp.asarray

    def _L0_attn_setup():
        import math
        import jax, jax.numpy as jnp
        import numpy as np

        def get_alibi_slopes(n_heads: int) -> jnp.ndarray:

            def _pow2_slopes(n):
                i = jnp.arange(1, n + 1, dtype=jnp.float32)
                return jnp.power(2.0, -8.0 * i / n)
            if n_heads & n_heads - 1 == 0:
                return _pow2_slopes(n_heads)
            nearest = 2 ** math.ceil(math.log2(n_heads))
            full = _pow2_slopes(nearest)
            half = nearest // 2
            half_slopes = _pow2_slopes(half)
            extra = full[jnp.arange(half) * 2 + 1]
            return jnp.concatenate([half_slopes, extra])[:n_heads]

        def build_alibi_bias(n_heads: int, T: int, causal: bool=True) -> jnp.ndarray:
            slopes = get_alibi_slopes(n_heads)
            idx = jnp.arange(T)
            rel = jnp.abs(idx[:, None] - idx[None, :]).astype(jnp.float32)
            bias = -slopes[:, None, None] * rel[None]
            if causal:
                future = idx[None, :] > idx[:, None]
                bias = jnp.where(future[None], -jnp.inf, bias)
            return bias
        key = jax.random.key(seed)
        ks = jax.random.split(key, 5)
        B, T, C = (2, 256, 128)
        s = 0.02
        return {'x': jax.random.normal(ks[0], (B, T, C), dtype=jnp.float32), 'Wq': jax.random.normal(ks[1], (C, C), dtype=jnp.float32) * s, 'Wk': jax.random.normal(ks[2], (C, C), dtype=jnp.float32) * s, 'Wv': jax.random.normal(ks[3], (C, C), dtype=jnp.float32) * s, 'Wo': jax.random.normal(ks[4], (C, C), dtype=jnp.float32) * s}
    _L0_attn_in = _L0_attn_setup()

    def _L0_ffn_setup():
        import jax, jax.numpy as jnp
        import numpy as np
        B, S, D = (2, 256, 128)
        DFF = 256
        E_FFN = 8
        E_ZERO = 4
        E_TOT = E_FFN + E_ZERO
        TOP_K = 2
        key = jax.random.key(seed)
        k1, k2, k3, k4 = jax.random.split(key, 4)
        x = jax.random.normal(k1, (B, S, D), dtype=jnp.float32)
        gate_w = jax.random.normal(k2, (E_TOT, D), dtype=jnp.float32) * (1.0 / np.sqrt(D))
        expert_bias = jnp.zeros((E_TOT,), dtype=jnp.float32)
        w1 = jax.random.normal(k3, (E_FFN, DFF, D), dtype=jnp.float32) * (1.0 / np.sqrt(D))
        w2 = jax.random.normal(k4, (E_FFN, D, DFF), dtype=jnp.float32) * (1.0 / np.sqrt(DFF))
        return {'x': x, 'gate_w': gate_w, 'expert_bias': expert_bias, 'w1': w1, 'w2': w2}
    _L0_ffn_in = _L0_ffn_setup()

    def _L1_attn_setup():
        import jax, jax.numpy as jnp
        import numpy as np
        L, D, F, H = (4, 128, 256, 8)
        DH = D // H
        EPS = 1e-05

        def _layer_norm(x, scale, bias):
            mu = x.mean(-1, keepdims=True)
            var = x.var(-1, keepdims=True)
            return (x - mu) * jax.lax.rsqrt(var + EPS) * scale + bias

        def _rotate(x, cos, sin):
            x1, x2 = (x[..., 0::2], x[..., 1::2])
            r1 = x1 * cos - x2 * sin
            r2 = x1 * sin + x2 * cos
            return jnp.stack([r1, r2], axis=-1).reshape(x.shape)

        def _decay_matrix(S):
            gammas = 1.0 - jnp.exp(jnp.linspace(np.log(1 / 32), np.log(1 / 64), H)).astype(jnp.float32)
            n = jnp.arange(S)
            diff = (n[:, None] - n[None, :]).astype(jnp.float32)
            pw = jnp.exp(jnp.clip(diff, 0.0)[None] * jnp.log(gammas)[:, None, None])
            return jnp.where(diff[None] >= 0, pw, 0.0)

        def _retention(x, Wq, Wk, Wv, Wg, Wo, gn_s, gn_b, Dm, cos, sin):
            B, S, _ = x.shape
            Q = (x @ Wq).reshape(B, S, H, DH)
            K = (x @ Wk).reshape(B, S, H, DH)
            V = (x @ Wv).reshape(B, S, H, DH)
            Q = _rotate(Q, cos, sin)
            K = _rotate(K, cos, -sin)
            att = jnp.einsum('bnhd,bmhd->bhnm', Q, K) * Dm
            Y = jnp.einsum('bhnm,bmhd->bnhd', att, V)
            mu = Y.mean(-1, keepdims=True)
            var = Y.var(-1, keepdims=True)
            Y = (Y - mu) * jax.lax.rsqrt(var + EPS)
            Y = Y.reshape(B, S, D) * gn_s + gn_b
            G = jax.nn.swish(x @ Wg)
            return G * Y @ Wo
        key = jax.random.key(seed)
        ks = jax.random.split(key, 8)
        B, S = (4, 128)
        sd = 1.0 / np.sqrt(D)
        sf = 1.0 / np.sqrt(F)
        return {'X': jax.random.normal(ks[0], (B, S, D), jnp.float32), 'Wq': jax.random.normal(ks[1], (L, D, D), jnp.float32) * sd, 'Wk': jax.random.normal(ks[2], (L, D, D), jnp.float32) * sd, 'Wv': jax.random.normal(ks[3], (L, D, D), jnp.float32) * sd, 'Wg': jax.random.normal(ks[4], (L, D, D), jnp.float32) * sd, 'Wo': jax.random.normal(ks[5], (L, D, D), jnp.float32) * sd, 'W1': jax.random.normal(ks[6], (L, D, F), jnp.float32) * sd, 'W2': jax.random.normal(ks[7], (L, F, D), jnp.float32) * sf, 'ln_scale': jnp.ones((D,), jnp.float32), 'ln_bias': jnp.zeros((D,), jnp.float32), 'gn_scale': jnp.ones((L, D), jnp.float32), 'gn_bias': jnp.zeros((L, D), jnp.float32)}
    _L1_attn_in = _L1_attn_setup()

    def _L1_ffn_setup():
        import jax, jax.numpy as jnp
        import numpy as np
        B, T, D = (4, 512, 128)
        E = 8
        TOP_K = 2
        FFN = 384
        HALF = FFN // 2

        def _kaiming_uniform(key, shape, fan_in):
            bound = 1.0 / np.sqrt(fan_in)
            return jax.random.uniform(key, shape, jnp.float32, -bound, bound)
        key = jax.random.key(seed)
        ks = jax.random.split(key, 7)
        x = jax.random.normal(ks[0], (B, T, D), jnp.float32)
        gate_w = _kaiming_uniform(ks[1], (E, D), D) * 0.01
        w_up = _kaiming_uniform(ks[2], (E, FFN, D), D)
        w_down = _kaiming_uniform(ks[3], (E, D, HALF), HALF)
        sg_gate = _kaiming_uniform(ks[4], (HALF, D), D)
        sg_up = _kaiming_uniform(ks[5], (HALF, D), D)
        sg_down = _kaiming_uniform(ks[6], (D, HALF), HALF)
        return {'x': x, 'gate_w': gate_w, 'w_up': w_up, 'w_down': w_down, 'sg_gate': sg_gate, 'sg_up': sg_up, 'sg_down': sg_down}
    _L1_ffn_in = _L1_ffn_setup()
    _d = {'L0_attn_x': _L0_attn_in['x'], 'L0_attn_Wq': _L0_attn_in['Wq'], 'L0_attn_Wk': _L0_attn_in['Wk'], 'L0_attn_Wv': _L0_attn_in['Wv'], 'L0_attn_Wo': _L0_attn_in['Wo'], 'L0_ffn_gate_w': _L0_ffn_in['gate_w'], 'L0_ffn_expert_bias': _L0_ffn_in['expert_bias'], 'L0_ffn_w1': _L0_ffn_in['w1'], 'L0_ffn_w2': _L0_ffn_in['w2'], 'L1_attn_Wq': _L1_attn_in['Wq'], 'L1_attn_Wk': _L1_attn_in['Wk'], 'L1_attn_Wv': _L1_attn_in['Wv'], 'L1_attn_Wg': _L1_attn_in['Wg'], 'L1_attn_Wo': _L1_attn_in['Wo'], 'L1_attn_W1': _L1_attn_in['W1'], 'L1_attn_W2': _L1_attn_in['W2'], 'L1_attn_ln_scale': _L1_attn_in['ln_scale'], 'L1_attn_ln_bias': _L1_attn_in['ln_bias'], 'L1_attn_gn_scale': _L1_attn_in['gn_scale'], 'L1_attn_gn_bias': _L1_attn_in['gn_bias'], 'L1_ffn_gate_w': _L1_ffn_in['gate_w'], 'L1_ffn_w_up': _L1_ffn_in['w_up'], 'L1_ffn_w_down': _L1_ffn_in['w_down'], 'L1_ffn_sg_gate': _L1_ffn_in['sg_gate'], 'L1_ffn_sg_up': _L1_ffn_in['sg_up'], 'L1_ffn_sg_down': _L1_ffn_in['sg_down']}
    _x0 = _d['L0_attn_x']
    _d['L0_attn_x'] = jax.random.normal(jax.random.fold_in(jax.random.key(seed), 1), (32, 256, 128), dtype=_x0.dtype)
    del _x0
    return _d

def reference(L0_attn_x, L0_attn_Wq, L0_attn_Wk, L0_attn_Wv, L0_attn_Wo, L0_ffn_gate_w, L0_ffn_expert_bias, L0_ffn_w1, L0_ffn_w2, L1_attn_Wq, L1_attn_Wk, L1_attn_Wv, L1_attn_Wg, L1_attn_Wo, L1_attn_W1, L1_attn_W2, L1_attn_ln_scale, L1_attn_ln_bias, L1_attn_gn_scale, L1_attn_gn_bias, L1_ffn_gate_w, L1_ffn_w_up, L1_ffn_w_down, L1_ffn_sg_gate, L1_ffn_sg_up, L1_ffn_sg_down):

    def _L0_attn_ref(x, Wq, Wk, Wv, Wo):
        import math
        import jax, jax.numpy as jnp
        import numpy as np

        def get_alibi_slopes(n_heads: int) -> jnp.ndarray:

            def _pow2_slopes(n):
                i = jnp.arange(1, n + 1, dtype=jnp.float32)
                return jnp.power(2.0, -8.0 * i / n)
            if n_heads & n_heads - 1 == 0:
                return _pow2_slopes(n_heads)
            nearest = 2 ** math.ceil(math.log2(n_heads))
            full = _pow2_slopes(nearest)
            half = nearest // 2
            half_slopes = _pow2_slopes(half)
            extra = full[jnp.arange(half) * 2 + 1]
            return jnp.concatenate([half_slopes, extra])[:n_heads]

        def build_alibi_bias(n_heads: int, T: int, causal: bool=True) -> jnp.ndarray:
            slopes = get_alibi_slopes(n_heads)
            idx = jnp.arange(T)
            rel = jnp.abs(idx[:, None] - idx[None, :]).astype(jnp.float32)
            bias = -slopes[:, None, None] * rel[None]
            if causal:
                future = idx[None, :] > idx[:, None]
                bias = jnp.where(future[None], -jnp.inf, bias)
            return bias
        B, T, C = x.shape
        H = 16
        D = C // H
        scale = D ** (-0.5)

        def proj_split(W):
            t = jnp.einsum('btc,dc->btd', x, W)
            return t.reshape(B, T, H, D).transpose(0, 2, 1, 3)
        q, k, v = (proj_split(Wq), proj_split(Wk), proj_split(Wv))
        scores = jnp.einsum('bhtd,bhsd->bhts', q, k) * scale
        bias = build_alibi_bias(H, T, causal=True)
        scores = scores + bias[None]
        attn = jax.nn.softmax(scores, axis=-1)
        out = jnp.einsum('bhts,bhsd->bhtd', attn, v)
        out = out.transpose(0, 2, 1, 3).reshape(B, T, C)
        return jnp.einsum('btc,dc->btd', out, Wo)

    def _L0_ffn_ref(x, gate_w, expert_bias, w1, w2):
        import jax, jax.numpy as jnp
        import numpy as np
        B, S, D = (2, 256, 128)
        DFF = 256
        E_FFN = 8
        E_ZERO = 4
        E_TOT = E_FFN + E_ZERO
        TOP_K = 2
        logits = jnp.einsum('btd,ed->bte', x, gate_w) + expert_bias
        topk_logits, topk_idx = jax.lax.top_k(logits, TOP_K)
        topk_w = jax.nn.softmax(topk_logits, axis=-1)
        onehot = jax.nn.one_hot(topk_idx, E_TOT, dtype=x.dtype)
        w = jnp.einsum('btk,btke->bte', topk_w, onehot)
        w_ffn = w[..., :E_FFN]
        w_zero = jnp.sum(w[..., E_FFN:], axis=-1)
        h = jax.nn.silu(jnp.einsum('btd,efd->btef', x, w1))
        y = jnp.einsum('btef,edf->bted', h, w2)
        out = jnp.einsum('bte,bted->btd', w_ffn, y) + w_zero[..., None] * x
        return out

    def _L1_attn_ref(X, Wq, Wk, Wv, Wg, Wo, W1, W2, ln_scale, ln_bias, gn_scale, gn_bias):
        import jax, jax.numpy as jnp
        import numpy as np
        L, D, F, H = (4, 128, 256, 8)
        DH = D // H
        EPS = 1e-05

        def _layer_norm(x, scale, bias):
            mu = x.mean(-1, keepdims=True)
            var = x.var(-1, keepdims=True)
            return (x - mu) * jax.lax.rsqrt(var + EPS) * scale + bias

        def _rotate(x, cos, sin):
            x1, x2 = (x[..., 0::2], x[..., 1::2])
            r1 = x1 * cos - x2 * sin
            r2 = x1 * sin + x2 * cos
            return jnp.stack([r1, r2], axis=-1).reshape(x.shape)

        def _decay_matrix(S):
            gammas = 1.0 - jnp.exp(jnp.linspace(np.log(1 / 32), np.log(1 / 64), H)).astype(jnp.float32)
            n = jnp.arange(S)
            diff = (n[:, None] - n[None, :]).astype(jnp.float32)
            pw = jnp.exp(jnp.clip(diff, 0.0)[None] * jnp.log(gammas)[:, None, None])
            return jnp.where(diff[None] >= 0, pw, 0.0)

        def _retention(x, Wq, Wk, Wv, Wg, Wo, gn_s, gn_b, Dm, cos, sin):
            B, S, _ = x.shape
            Q = (x @ Wq).reshape(B, S, H, DH)
            K = (x @ Wk).reshape(B, S, H, DH)
            V = (x @ Wv).reshape(B, S, H, DH)
            Q = _rotate(Q, cos, sin)
            K = _rotate(K, cos, -sin)
            att = jnp.einsum('bnhd,bmhd->bhnm', Q, K) * Dm
            Y = jnp.einsum('bhnm,bmhd->bnhd', att, V)
            mu = Y.mean(-1, keepdims=True)
            var = Y.var(-1, keepdims=True)
            Y = (Y - mu) * jax.lax.rsqrt(var + EPS)
            Y = Y.reshape(B, S, D) * gn_s + gn_b
            G = jax.nn.swish(x @ Wg)
            return G * Y @ Wo
        B, S, _ = X.shape
        pos = jnp.arange(S, dtype=jnp.float32)
        inv_freq = 1.0 / 10000.0 ** (jnp.arange(0, DH, 2, dtype=jnp.float32) / DH)
        ang = pos[:, None] * inv_freq[None, :]
        cos = jnp.cos(ang)[None, :, None, :]
        sin = jnp.sin(ang)[None, :, None, :]
        Dm = _decay_matrix(S)
        for i in range(L):
            Yr = _retention(_layer_norm(X, ln_scale, ln_bias), Wq[i], Wk[i], Wv[i], Wg[i], Wo[i], gn_scale[i], gn_bias[i], Dm, cos, sin) + X
            X = jax.nn.gelu(_layer_norm(Yr, ln_scale, ln_bias) @ W1[i]) @ W2[i] + Yr
        return X

    def _L1_ffn_ref(x, gate_w, w_up, w_down, sg_gate, sg_up, sg_down):
        import jax, jax.numpy as jnp
        import numpy as np
        B, T, D = (4, 512, 128)
        E = 8
        TOP_K = 2
        FFN = 384
        HALF = FFN // 2

        def _kaiming_uniform(key, shape, fan_in):
            bound = 1.0 / np.sqrt(fan_in)
            return jax.random.uniform(key, shape, jnp.float32, -bound, bound)
        b, t, d = x.shape
        xf = x.reshape(b * t, d)
        N = xf.shape[0]
        logits = xf @ gate_w.T
        topk_logits, topk_idx = jax.lax.top_k(logits, TOP_K)
        topk_w = jax.nn.softmax(topk_logits.astype(jnp.float32), axis=-1).astype(x.dtype)
        comb = jnp.zeros((N, E), x.dtype).at[jnp.arange(N)[:, None], topk_idx].add(topk_w)
        wg = w_up[:, :HALF, :]
        wu = w_up[:, HALF:, :]
        out = jnp.zeros_like(xf)
        for e in range(E):
            g = xf @ wg[e].T
            u = xf @ wu[e].T
            y = jax.nn.silu(g) * u @ w_down[e].T
            out = out + comb[:, e:e + 1] * y
        shared = jax.nn.silu(xf @ sg_gate.T) * (xf @ sg_up.T) @ sg_down.T
        return (shared + out).reshape(b, t, d)
    x = L0_attn_x
    xn = _layernorm(x, axis=-1)
    x = x + _L0_attn_ref(xn, L0_attn_Wq, L0_attn_Wk, L0_attn_Wv, L0_attn_Wo) + _L0_ffn_ref(xn, L0_ffn_gate_w, L0_ffn_expert_bias, L0_ffn_w1, L0_ffn_w2)
    xn = _layernorm(x, axis=-1)
    x = x + _L1_attn_ref(xn, L1_attn_Wq, L1_attn_Wk, L1_attn_Wv, L1_attn_Wg, L1_attn_Wo, L1_attn_W1, L1_attn_W2, L1_attn_ln_scale, L1_attn_ln_bias, L1_attn_gn_scale, L1_attn_gn_bias) + _L1_ffn_ref(xn, L1_ffn_gate_w, L1_ffn_w_up, L1_ffn_w_down, L1_ffn_sg_gate, L1_ffn_sg_up, L1_ffn_sg_down)
    return x

_drawn_inputs = setup_inputs


def setup_inputs(seed=0):
    import zlib

    import numpy as np

    out = dict(_drawn_inputs(seed))
    spreads = {'L0_ffn_expert_bias': (0.0, 0.1),
     'L1_attn_ln_scale': (1.0, 0.2),
     'L1_attn_ln_bias': (0.0, 0.1),
     'L1_attn_gn_scale': (1.0, 0.2),
     'L1_attn_gn_bias': (0.0, 0.1)}
    factors = {'L0_attn_Wq': 8.0, 'L0_attn_Wk': 8.0}
    for name, (base, spread) in spreads.items():
        noise = np.random.default_rng([zlib.crc32(name.encode()), seed]).standard_normal(out[name].shape)
        drawn = base * np.exp(spread * noise) if base else spread * noise
        out[name] = jnp.asarray(drawn.astype(out[name].dtype))
    for name, factor in factors.items():
        out[name] = (out[name] * factor).astype(out[name].dtype)
    return out
```

```python
from contextlib import ExitStack

import numpy as np

import concourse.bass as bass
from concourse import mybir

P = 128
F32 = mybir.dt.float32
BF16 = mybir.dt.bfloat16
I32 = mybir.dt.int32
U32 = mybir.dt.uint32
ALU = mybir.AluOpType
ACT = mybir.ActivationFunctionType
AX = mybir.AxisListType

T = 256
NB = 2
TOK = NB * T
NT = TOK // P
D = 128
H0, DH0 = 16, 8
H1, DH1, L1 = 8, 16, 4
HG = 8
RM, RS = 8, 9
E0, EALL0 = 8, 12
E1 = 8
BLK = 384
EPS = 1e-5
BIG = -1e30


class Sig:

    def __init__(self, sem, per_pass):
        self.sem, self.per_pass = sem, per_pass

    def at(self, it, n):
        return it * self.per_pass + n


def shape_constants():
    def bf16_bits(t):
        return (t.view(np.uint32) >> 16).astype(np.uint16)

    f = np.float32
    p = np.arange(P)
    c = {}
    slopes = np.power(f(2.0), (f(-8.0) * np.arange(1, H0 + 1, dtype=f) / f(H0))).astype(f)
    bias_q = np.zeros((P, 2), f)
    pos_k = np.zeros((P, TOK), f)
    for g in range(2):
        for h in range(HG):
            bias_q[h * 16 + RS, g] = slopes[g * HG + h]
    s = np.tile(np.arange(T), NB)
    pos_k[RM::16] = 1.0
    pos_k[RS::16] = s - 128.0
    c["bias_q"], c["pos_k"] = bias_q, pos_k
    c["head_mask"] = (p[:, None] // 16 == np.arange(8)[None]).astype(f)
    c["ident"] = np.eye(P, dtype=f)
    c["ident_bf"] = bf16_bits(np.eye(P, dtype=f))
    later = np.where(p[None] > p[:, None], f(BIG), f(0))
    zero = np.zeros((P, P), f)
    c["mask_q0"] = bf16_bits(np.concatenate([later] * 4, 1))
    c["mask_q1"] = bf16_bits(np.concatenate([zero, later] * 2, 1))
    c["mask_k"] = bf16_bits(np.concatenate([later.T, zero, later.T], 1))
    sel = np.zeros((P, P), f)
    for r in range(4):
        sel[32 * r + 8, 32 * r:32 * r + 32] = 1.0
    c["sel_sum"] = sel
    c["mean_sq"] = ((p[:, None] // 32 == np.arange(4)[None]) & (p[:, None] % 32 < DH1)).astype(f) / f(DH1)
    c["centre"] = (np.eye(P) - (p[:, None] // DH1 == p[None] // DH1) / DH1).astype(f)
    keep = (p[None] >= p[:, None]).astype(f)
    c["causal"] = np.concatenate([keep, zero + 1, keep], 1).astype(f)
    c["iota"] = np.tile(np.arange(16, dtype=f)[None, None], (P, NT, 1)).reshape(P, NT * 16)
    gammas = (f(1.0) - np.exp(np.linspace(np.log(1 / 32), np.log(1 / 64), H1)).astype(f)).astype(f)
    log_g = np.log(gammas).astype(f).astype(np.float64)[p // DH1][:, None]
    inv_freq = (f(1.0) / np.power(f(10000.0), np.arange(0, DH1, 2, dtype=f) / f(DH1))).astype(f)
    ang = (np.arange(T, dtype=f)[None] * inv_freq[(p % DH1) // 2][:, None]).astype(f).astype(np.float64)
    sign = np.where(p % 2 == 0, -1.0, 1.0)[:, None]
    n = np.arange(T)[None] - 128.0
    dq, dk = np.exp(n * log_g), np.exp(-n * log_g)
    rope = [np.cos(ang) * dq, np.sin(ang) * sign * dq, np.cos(ang) * dk, -np.sin(ang) * sign * dk]
    c["rope"] = np.concatenate([np.tile(t, (1, NB)) for t in rope], 1).astype(f)
    return c


def program(nc, x, out, w):
    passes = x.shape[0] // TOK
    with ExitStack() as ctx:
        def sb(name, shape, dt=F32):
            return ctx.enter_context(nc.sbuf_tensor(name, shape, dt))

        sigs = {}

        def sig(name, per_pass):
            sigs[name] = Sig(ctx.enter_context(nc.semaphore(name)), per_pass)
            return sigs[name]

        W = {n: sb("s_" + n, list(a.shape), a.dtype) for n, a in w.items()}
        wv_c = sb("wv_c", [P, L1 * P])
        ident_bf = W["ident_bf"][:, :].bitcast(BF16)
        wo1h = W["wo1"]

        x_in = sb("x_in", [P, NT, D])
        xn = sb("xn", [P, NT, D])
        xnT = sb("xnT", [P, TOK])
        acc = sb("acc", [P, NT, D])
        settled = sb("settled", [P, 1])
        st = sb("st", [P, NT, 6])
        mv = sb("mv", [P, NT, 2])
        nv = sb("nv", [P, 4, 32])
        lg = sb("lg", [P, NT, 16])
        m8 = sb("m8", [P, NT, 8])
        i8 = sb("i8", [P, NT, 8], U32)
        i2 = sb("i2", [P, NT, 2])
        gd = sb("gd", [P, NT])
        gth = sb("gth", [P, NT])
        gw = sb("gw", [P, 2, NT])
        ge = sb("ge", [P, 2, NT, 16])
        comb = sb("comb", [P, NT, 16])
        wz = sb("wz", [P, NT])
        Qg = sb("Qg", [P, 2, TOK])
        Kg = sb("Kg", [P, 2, TOK])
        Km = sb("Km", [P, H0, TOK])
        Vx = sb("Vx", [P, NT, H0, 32])
        mpad = sb("mpad", [P, 2, 2, HG, 16])
        NPR = 6
        Pr = sb("Pr", [P, NPR, BLK])
        Osb = sb("Osb", [P, 4, TOK])
        On = sb("On", [P, 4, TOK])
        rc = sb("rc", [P, TOK])
        th = sb("th", [P, 2, TOK])
        fs = sb("fs", [P, 1, TOK])
        hf = sb("hf", [P, 4, TOK])
        x1 = sb("x1", [P, NT, D])
        X = sb("X", [P, NT, D])
        Yr = sb("Yr", [P, NT, D])
        xh = sb("xh", [P, NT, D])
        hT = sb("hT", [P, TOK])
        qr = On
        Qh, Kh = Km[:, H1], Km[:, H1 + 1]
        Gs, gt2, sq, Hh = (Km[:, H1 + j:H1 + j + 2] for j in (2, 4, 6, 6))
        Z = Osb[:, 2:4]
        Vr = sb("Vr", [P, NT, H1, 32])
        rsx = Kg[:].rearrange("p g (k r c) -> p (g k) r c", k=4, r=4).rearrange("p (k q) r c -> p k q r c", k=NT)
        x_out = sb("x_out", [P, NT, D])

        bank = [ctx.enter_context(nc.psum_tensor(f"bank{i}", [P, 512], F32)) for i in range(8)]

        weights_in = ctx.enter_context(nc.semaphore("weights_in"))
        set_up = ctx.enter_context(nc.semaphore("set_up"))
        fold_ps = ctx.enter_context(nc.semaphore("fold_ps"))
        x_loaded = sig("x_loaded", 16)
        x_used = sig("x_used", 1)
        stored = sig("stored", 16)
        out_ready = sig("out_ready", 1)
        out_free = sig("out_free", 1)
        dve_step = sig("dve_step", 250)
        xn_ready = sig("xn_ready", 2)
        xnT_ps = sig("xnT_ps", 2)
        xnT_ready = sig("xnT_ready", 2)
        logit_ps = sig("logit_ps", 2)
        gap_ready = sig("gap_ready", 2)
        gate_tanh = sig("gate_tanh", 2)
        logits_read = sig("logits_read", 2)
        qk_ps = sig("qk_ps", 4)
        v_ps = sig("v_ps", 1)
        q_ready = sig("q_ready", 2)
        k_ready = sig("k_ready", H0)
        v_ready = sig("v_ready", 1)
        NP1 = 12
        rows_ps = sig("rows_ps", NB * NP1)
        rows_max = sig("rows_max", NB * NP1)
        mpadT_ps = sig("mpadT_ps", NB)
        q_shifted = sig("q_shifted", NB)
        cols_ps = sig("cols_ps", NB * H0)
        exp_ready = sig("exp_ready", NB * H0)
        pv_ps = sig("pv_ps", NB * H0)
        pv_copied = sig("pv_copied", NB * 2)
        sums_ps = sig("sums_ps", 4)
        o_ready = sig("o_ready", 4)
        y0_ps = sig("y0_ps", 1)
        up_ps = sig("up_ps", 2 * E0)
        up_tanh = sig("up_tanh", 2 * E0)
        hid_ready = sig("hid_ready", E0)
        down_ps = sig("down_ps", E0)
        down_added = sig("down_added", E0)
        C1 = 3 * (E1 // 2) + 2
        up1_ps = sig("up1_ps", C1)
        up1_tanh = sig("up1_tanh", C1)
        hid1_ready = sig("hid1_ready", C1)
        down1_ps = sig("down1_ps", E1 + 1)
        down1_added = sig("down1_added", E1 + 1)
        ln_ready = sig("ln_ready", 2 * L1)
        lnT_ps = sig("lnT_ps", 2 * L1)
        lnT_ready = sig("lnT_ready", 2 * L1)
        qk1_ps = sig("qk1_ps", 4 * L1)
        v1_ps = sig("v1_ps", L1)
        v1_ready = sig("v1_ready", L1)
        qk1_rot = sig("qk1_rot", 4 * L1)
        q1_ready = sig("q1_ready", L1)
        k1_ready = sig("k1_ready", L1 * H1)
        g_ps = sig("g_ps", 2 * L1)
        g_tanh = sig("g_tanh", 2 * L1)
        g_ready = sig("g_ready", 2 * L1)
        att_ps = sig("att_ps", NB * H1 * L1)
        att_ready = sig("att_ready", NB * H1 * L1)
        ret_ps = sig("ret_ps", NB * H1 * L1)
        ret_copied = sig("ret_copied", 2 * L1)
        var_ps = sig("var_ps", L1)
        rstd_ready = sig("rstd_ready", L1)
        rstdT_ps = sig("rstdT_ps", 2 * L1)
        z_ready = sig("z_ready", 2 * L1)
        wo_ps = sig("wo_ps", L1)
        ffh_ps = sig("ffh_ps", 2 * L1)
        gelu_ready = sig("gelu_ready", 2 * L1)
        w2_ps = sig("w2_ps", L1)

        pieces = []
        for pair in range(E1 // 2):
            for j in range(3):
                pieces.append(("up", 3 * pair + j, 6 * pair + 2 * j))
            pieces += [("down", 2 * pair, 3 * pair), ("down", 2 * pair + 1, 3 * pair + 1)]
        base = 3 * (E1 // 2)
        pieces += [("up", base, 6 * (E1 // 2)), ("up", base + 1, 6 * (E1 // 2) + 2), ("down", E1, base)]
        SLOTS = 6

        def down_blocks(e):
            pair, odd = (e // 2, e % 2)
            a = 3 * pair + odd
            b = 3 * pair + 2 if e < E1 else base + 1
            return [(a, 2 * e), (b, 2 * e + 1)]

        block = ctx.enter_context(nc.Block())
        x_v = x.rearrange("(n k p) c -> n p k c", p=P, k=NT)
        o_v = out.rearrange("(n k p) c -> n p k c", p=P, k=NT)

        @block.sync
        def _(sp):
            for n in w:
                sp.dma_start(W[n][:, :], w[n]).then_inc(weights_in, 16)
            def load(p):
                sp.dma_start(x_in[:], x[bass.ds(p * TOK, TOK), :].rearrange("(k p) c -> p k c", p=P)).then_inc(x_loaded.sem, 16)

            def store(p):
                sp.wait_ge(out_ready.sem, out_ready.at(p, 1))
                sp.dma_start(out[bass.ds(p * TOK, TOK), :].rearrange("(k p) c -> p k c", p=P), x_out[:]).then_inc(stored.sem, 16)
                sp.wait_ge(stored.sem, stored.at(p, 16))
                sp.sem_inc(out_free.sem, 1)

            sp.sem_inc(out_free.sem, 1)
            load(0)
            with sp.Fori(0, passes - 1) as it:
                sp.wait_ge(x_used.sem, x_used.at(it, 1))
                load(it + 1)
                store(it)
            store(passes - 1)

        @block.tensor
        def _(pe):
            mm = nc.tensor.matmul
            pe.wait_ge(weights_in, 16 * len(w))
            for l in range(L1):
                mm(bank[l][:, 0:P], W["wvT1"][:, l * P:(l + 1) * P], W["centre"][:, :], start=True, stop=True).then_inc(fold_ps, 1)
            pe.wait_ge(set_up, 3)

            def four_transposes(dst, src):
                for k in range(NT):
                    last = nc.tensor.transpose(dst[:, k * P:(k + 1) * P], src[:, k, :], W["ident"][:, :])
                return last

            def by_token(dst, lhs, rhs_blocks):
                for k in range(NT):
                    n = len(rhs_blocks)
                    for j in range(n):
                        last = mm(dst[:, k * P:(k + 1) * P], lhs[j][:, k * P:(k + 1) * P], rhs_blocks[j],
                                  start=(j == 0), stop=(j == n - 1))
                return last

            with pe.Fori(0, passes) as it:
                def up(e):
                    if e:
                        pe.wait_ge(hid_ready.sem, hid_ready.at(it, e))
                    for m in range(2):
                        c = (2 * e + m) * P
                        mm(bank[4 + m][:, :], W["w1"][:, c:c + P], xnT[:, :], start=True, stop=True).then_inc(up_ps.sem, 1)

                def down(e):
                    pe.wait_ge(hid_ready.sem, hid_ready.at(it, e + 1))
                    if e:
                        pe.wait_ge(down_added.sem, down_added.at(it, e))
                    by_token(bank[6], [hf[:, 2 * (e % 2) + m] for m in range(2)],
                             [W["w2"][:, (2 * e + m) * P:(2 * e + m + 1) * P] for m in range(2)]).then_inc(down_ps.sem, 1)

                pe.wait_ge(xn_ready.sem, xn_ready.at(it, 1))
                four_transposes(bank[7], xn).then_inc(xnT_ps.sem, 1)
                pe.wait_ge(xnT_ready.sem, xnT_ready.at(it, 1))
                for k in range(NT):
                    last = mm(bank[7][:, k * 16:k * 16 + EALL0], xnT[:, k * P:(k + 1) * P], W["gate0"][:, :], start=True, stop=True)
                last.then_inc(logit_ps.sem, 1)
                for j in range(2):
                    mm(bank[j][:, :], W["wq"][:, j * P:(j + 1) * P], xnT[:, :], start=True, stop=True).then_inc(qk_ps.sem, 1)
                for j in range(2):
                    mm(bank[2 + j][:, :], W["wk"][:, j * P:(j + 1) * P], xnT[:, :], start=True, stop=True).then_inc(qk_ps.sem, 1)
                by_token(bank[4], [xnT], [W["wv"][:, :]]).then_inc(v_ps.sem, 1)
                pe.wait_ge(q_ready.sem, q_ready.at(it, 2))
                pe.wait_ge(v_ready.sem, v_ready.at(it, 1))
                up(0)
                for b in range(NB):
                    for i in range(NP1):
                        n = b * NP1 + i
                        t_tile = 0 if i < 4 else 1
                        heads = range(4 * i, 4 * i + 4) if t_tile == 0 else range(2 * (i - 4), 2 * (i - 4) + 2)
                        width = P * (1 + t_tile)
                        if n < H0 // 2 + 4:
                            pe.wait_ge(k_ready.sem, k_ready.at(it, min(H0, max(heads) + 1) if n < 4 else H0))
                        if n >= 3:
                            pe.wait_ge(rows_max.sem, rows_max.at(it, n - 2))
                        dst = bank[n % 3]
                        mm(dst[:, :], ident_bf, W[f"mask_q{t_tile}"][:, :].bitcast(BF16), start=True, stop=False)
                        q0 = b * T + t_tile * P
                        for j, h in enumerate(heads):
                            last = mm(dst[:, j * width:(j + 1) * width], Qg[:, h // HG, q0:q0 + P],
                                      Km[:, h, b * T:b * T + width], start=False, stop=(j == len(heads) - 1))
                        last.then_inc(rows_ps.sem, 1)
                        if n % 3 == 2:
                            e = n // 3
                            down(e)
                            if e + 1 < E0:
                                up(e + 1)
                    pe.wait_ge(rows_max.sem, rows_max.at(it, (b + 1) * NP1))
                    if b == 0:
                        pe.wait_ge(logits_read.sem, logits_read.at(it, 1))
                    else:
                        pe.wait_ge(q_shifted.sem, q_shifted.at(it, b))
                    for g in range(2):
                        for k in range(2):
                            last = nc.tensor.transpose(bank[7][:, (2 * g + k) * P:(2 * g + k + 1) * P],
                                                       mpad[:, k, g].rearrange("p h r -> p (h r)"), W["ident"][:, :])
                    last.then_inc(mpadT_ps.sem, 1)
                pe.wait_ge(q_shifted.sem, q_shifted.at(it, NB))
                LAG = 2

                def weigh(n):
                    b, h = n // H0, n % H0
                    q, r = h // 4, h % 4
                    pe.wait_ge(exp_ready.sem, exp_ready.at(it, n + 1))
                    if h % 8 == 0 and b:
                        pe.wait_ge(pv_copied.sem, pv_copied.at(it, 2 * b - 1 + h // 8))
                    dst = bank[3 if q < 2 else 7]
                    c = (q % 2) * T
                    p = Pr[:, n % NPR]
                    mm(dst[32 * r:32 * r + 32, c:c + T], Vx[:, 2 * b, h, :], p[:, 0:T], start=True, stop=False, skip_group_check=True)
                    mm(dst[32 * r:32 * r + 32, c + P:c + T], Vx[:, 2 * b + 1, h, :], p[:, T:BLK], start=False, stop=True,
                       skip_group_check=True).then_inc(pv_ps.sem, 1)

                for n in range(NB * H0):
                    b, h = n // H0, n % H0
                    dst = bank[n % 3]
                    if n < 3:
                        pe.wait_ge(rows_max.sem, rows_max.at(it, NB * NP1))
                    else:
                        pe.wait_ge(exp_ready.sem, exp_ready.at(it, n - 2))
                    mm(dst[:, 0:BLK], ident_bf, W["mask_k"][:, :].bitcast(BF16), start=True, stop=False)
                    mm(dst[:, 0:T], Km[:, h, b * T:b * T + P], Qg[:, h // HG, b * T:(b + 1) * T], start=False, stop=False)
                    mm(dst[:, T:BLK], Km[:, h, b * T + P:(b + 1) * T], Qg[:, h // HG, b * T + P:(b + 1) * T], start=False, stop=True).then_inc(cols_ps.sem, 1)
                    if n >= LAG:
                        weigh(n - LAG)
                for n in range(NB * H0 - LAG, NB * H0):
                    weigh(n)
                pe.wait_ge(pv_copied.sem, pv_copied.at(it, 2 * NB))
                pe.wait_ge(exp_ready.sem, exp_ready.at(it, NB * H0))
                for q in range(4):
                    if q == 3:
                        pe.wait_ge(o_ready.sem, o_ready.at(it, 1))
                    mm(bank[q % 3][:, :], W["sel_sum"][:, :], Osb[:, q], start=True, stop=True).then_inc(sums_ps.sem, 1)
                pe.wait_ge(o_ready.sem, o_ready.at(it, 4))
                by_token(bank[7], [On[:, q] for q in range(4)], [W["wo"][:, q * P:(q + 1) * P] for q in range(4)]).then_inc(y0_ps.sem, 1)

                pe.wait_ge(xn_ready.sem, xn_ready.at(it, 2))
                four_transposes(bank[7], xn).then_inc(xnT_ps.sem, 1)
                pe.wait_ge(xnT_ready.sem, xnT_ready.at(it, 2))
                for k in range(NT):
                    last = mm(bank[7][:, k * 16:k * 16 + E1], xnT[:, k * P:(k + 1) * P], W["gate1"][:, :], start=True, stop=True)
                last.then_inc(logit_ps.sem, 1)

                def piece(i):
                    if i >= len(pieces):
                        return
                    kind, a, c = pieces[i]
                    if kind == "up":
                        if a:
                            pe.wait_ge(hid1_ready.sem, hid1_ready.at(it, a))
                        mm(bank[4][:, :], W["wup"][:, c * P:(c + 1) * P], xnT[:, :], start=True, stop=True)
                        mm(bank[5][:, :], W["wup"][:, (c + 1) * P:(c + 2) * P], xnT[:, :], start=True, stop=True).then_inc(up1_ps.sem, 1)
                    else:
                        blocks = down_blocks(a)
                        pe.wait_ge(hid1_ready.sem, hid1_ready.at(it, blocks[1][0] + 1))
                        if a:
                            pe.wait_ge(down1_added.sem, down1_added.at(it, a))
                        by_token(bank[6], [hf[:, j[0] % 4] for j in blocks],
                                 [W["wdn"][:, j[1] * P:(j[1] + 1) * P] for j in blocks]).then_inc(down1_ps.sem, 1)

                for l in range(L1):
                    pe.wait_ge(ln_ready.sem, ln_ready.at(it, 2 * l + 1))
                    if l == 0:
                        pe.wait_ge(logits_read.sem, logits_read.at(it, 2))
                    four_transposes(bank[7], xh).then_inc(lnT_ps.sem, 1)
                    piece(SLOTS * l)
                    pe.wait_ge(lnT_ready.sem, lnT_ready.at(it, 2 * l + 1))
                    for j, name in enumerate(("wq1", "wqs1", "wk1", "wks1")):
                        mm(bank[j][:, :], W[name][:, l * P:(l + 1) * P], hT[:, :], start=True, stop=True).then_inc(qk1_ps.sem, 1)
                    by_token(bank[7], [hT], [wv_c[:, l * P:(l + 1) * P]]).then_inc(v1_ps.sem, 1)
                    for q in range(2):
                        pe.wait_ge(qk1_rot.sem, qk1_rot.at(it, 4 * l + q + 1))
                        mm(bank[q][:, :], W["wg1"][:, (2 * l + q) * P:(2 * l + q + 1) * P], hT[:, :], start=True, stop=True).then_inc(g_ps.sem, 1)
                    piece(SLOTS * l + 1)
                    pe.wait_ge(q1_ready.sem, q1_ready.at(it, l + 1))
                    pe.wait_ge(v1_ready.sem, v1_ready.at(it, l + 1))
                    ring = [2, 0, 1]

                    def retain(n):
                        b, h = n // H1, n % H1
                        m = l * NB * H1 + n
                        q, r = h // 4, h % 4
                        pe.wait_ge(att_ready.sem, att_ready.at(it, m + 1))
                        dst = bank[7 if b == 0 else 3]
                        c = q * T
                        a = Pr[:, n % NPR]
                        mm(dst[32 * r:32 * r + 32, c:c + T], Vr[:, 2 * b, h, :], a[:, 0:T], start=True, stop=False, skip_group_check=True)
                        mm(dst[32 * r:32 * r + 32, c + P:c + T], Vr[:, 2 * b + 1, h, :], a[:, T:BLK], start=False, stop=True,
                           skip_group_check=True).then_inc(ret_ps.sem, 1)

                    for n in range(NB * H1):
                        b, h = n // H1, n % H1
                        if n < H1:
                            pe.wait_ge(k1_ready.sem, k1_ready.at(it, l * H1 + n + 1))
                        if n == 1:
                            pe.wait_ge(g_ready.sem, g_ready.at(it, 2 * l + 2))
                        if n >= 3:
                            pe.wait_ge(att_ready.sem, att_ready.at(it, l * NB * H1 + n - 2))
                        dst = bank[ring[n % 3]]
                        mm(dst[:, 0:T], Km[:, h, b * T:b * T + P], Qh[:, b * T:(b + 1) * T], start=True, stop=True)
                        mm(dst[:, T:BLK], Km[:, h, b * T + P:(b + 1) * T], Qh[:, b * T + P:(b + 1) * T], start=True, stop=True).then_inc(att_ps.sem, 1)
                        if n >= 2:
                            retain(n - 2)
                        if n == 7:
                            piece(SLOTS * l + 2)
                    retain(NB * H1 - 2)
                    retain(NB * H1 - 1)
                    pe.wait_ge(ret_copied.sem, ret_copied.at(it, 2 * l + 2))
                    for k in range(NT):
                        for q in range(2):
                            c = (2 * k + q) * 4
                            last = mm(bank[0][:, c:c + 4], sq[:, q, k * P:(k + 1) * P], W["mean_sq"][:, :], start=True, stop=True)
                    last.then_inc(var_ps.sem, 1)
                    piece(SLOTS * l + 3)
                    pe.wait_ge(rstd_ready.sem, rstd_ready.at(it, l + 1))
                    for q in range(2):
                        for k in range(NT):
                            last = nc.tensor.transpose(bank[1 + q][:, k * P:(k + 1) * P],
                                                       rsx[:, k, q].rearrange("p r c -> p (r c)"), W["ident"][:, :])
                        last.then_inc(rstdT_ps.sem, 1)
                    pe.wait_ge(z_ready.sem, z_ready.at(it, 2 * l + 2))
                    by_token(bank[3], [Z[:, q] for q in range(2)],
                             [wo1h[:, (2 * l + q) * P:(2 * l + q + 1) * P] for q in range(2)]).then_inc(wo_ps.sem, 1)
                    piece(SLOTS * l + 4)
                    pe.wait_ge(ln_ready.sem, ln_ready.at(it, 2 * l + 2))
                    four_transposes(bank[7], xh).then_inc(lnT_ps.sem, 1)
                    pe.wait_ge(lnT_ready.sem, lnT_ready.at(it, 2 * l + 2))
                    for j in range(2):
                        mm(bank[j][:, :], W["w11"][:, (2 * l + j) * P:(2 * l + j + 1) * P], hT[:, :], start=True, stop=True).then_inc(ffh_ps.sem, 1)
                    piece(SLOTS * l + 5)
                    pe.wait_ge(gelu_ready.sem, gelu_ready.at(it, 2 * l + 2))
                    by_token(bank[3], [Hh[:, j] for j in range(2)],
                             [W["w21"][:, (2 * l + j) * P:(2 * l + j + 1) * P] for j in range(2)]).then_inc(w2_ps.sem, 1)

        @block.scalar
        def _(act):
            A = nc.scalar.activation
            act.wait_ge(weights_in, 16 * len(w))
            act.wait_ge(fold_ps, L1)
            for l in range(L1):
                last = A(wv_c[:, l * P:(l + 1) * P], bank[l][:, 0:P], ACT.Copy)
            last.then_inc(set_up, 1)
            A(wo1h[:, :], W["wo1"][:, :], ACT.Copy, scale=0.5).then_inc(set_up, 1)
            with act.Fori(0, passes) as it:
                def tanh0(e):
                    for m in range(2):
                        act.wait_ge(up_ps.sem, up_ps.at(it, 2 * e + m + 1))
                        A(th[:, m], bank[4 + m][:, :], ACT.Tanh, scale=0.5).then_inc(up_tanh.sem, 1)

                act.wait_ge(xnT_ps.sem, xnT_ps.at(it, 1))
                A(xnT[:, :], bank[7][:, :], ACT.Copy).then_inc(xnT_ready.sem, 1)
                for j in range(2):
                    act.wait_ge(qk_ps.sem, qk_ps.at(it, j + 1))
                    A(Qg[:, j], bank[j][:, :], ACT.Identity, bias=W["bias_q"][:, j:j + 1], scale=float(DH0) ** -0.5).then_inc(q_ready.sem, 1)
                act.wait_ge(v_ps.sem, v_ps.at(it, 1))
                A(Vx[:, :, :, 0:DH0], bank[4][:, :].rearrange("p (k h d) -> p k h d", k=NT, h=H0), ACT.Copy).then_inc(v_ready.sem, 1)
                act.wait_ge(gap_ready.sem, gap_ready.at(it, 1))
                A(gth[:, :], gd[:, :], ACT.Tanh, scale=0.5).then_inc(gate_tanh.sem, 1)
                for e in range(E0):
                    tanh0(e)

                def copy_o(b, half):
                    act.wait_ge(pv_ps.sem, pv_ps.at(it, H0 * b + 8 * half + 8))
                    src = bank[3 if half == 0 else 7]
                    A(Osb[:, 2 * half:2 * half + 2, b * T:(b + 1) * T], src[:, :].rearrange("p (q t) -> p q t", q=2),
                      ACT.Copy).then_inc(pv_copied.sem, 1)

                for n in range(NB * H0):
                    act.wait_ge(cols_ps.sem, cols_ps.at(it, n + 1))
                    if n >= NPR:
                        act.wait_ge(pv_ps.sem, pv_ps.at(it, n - NPR + 1))
                    A(Pr[:, n % NPR], bank[n % 3][:, 0:BLK], ACT.Exp).then_inc(exp_ready.sem, 1)
                    b, h = n // H0, n % H0
                    if h == 10:
                        copy_o(b, 0)
                    if h == 2 and b:
                        copy_o(b - 1, 1)
                copy_o(NB - 1, 1)

                act.wait_ge(xnT_ps.sem, xnT_ps.at(it, 2))
                A(xnT[:, :], bank[7][:, :], ACT.Copy).then_inc(xnT_ready.sem, 1)
                act.wait_ge(gap_ready.sem, gap_ready.at(it, 2))
                A(gth[:, :], gd[:, :], ACT.Tanh, scale=0.5).then_inc(gate_tanh.sem, 1)

                def piece(i):
                    if i < len(pieces) and pieces[i][0] == "up":
                        a = pieces[i][1]
                        act.wait_ge(up1_ps.sem, up1_ps.at(it, a + 1))
                        A(th[:, a % 2], bank[4][:, :], ACT.Tanh, scale=0.5).then_inc(up1_tanh.sem, 1)

                def turned(n):
                    act.wait_ge(lnT_ps.sem, lnT_ps.at(it, n))
                    A(hT[:, :], bank[7][:, :], ACT.Identity, bias=W["ln_b"][:, 0:1], scale=W["ln_s"][:, 0:1]).then_inc(lnT_ready.sem, 1)

                for l in range(L1):
                    turned(2 * l + 1)
                    piece(SLOTS * l)
                    act.wait_ge(v1_ps.sem, v1_ps.at(it, l + 1))
                    A(Vr[:, :, :, 0:DH1], bank[7][:, :].rearrange("p (k h d) -> p k h d", k=NT, h=H1), ACT.Copy).then_inc(v1_ready.sem, 1)
                    for q in range(2):
                        act.wait_ge(g_ps.sem, g_ps.at(it, 2 * l + q + 1))
                        A(gt2[:, q], bank[q][:, :], ACT.Tanh, scale=0.5).then_inc(g_tanh.sem, 1)
                    piece(SLOTS * l + 1)
                    piece(SLOTS * l + 2)
                    for b in range(NB):
                        act.wait_ge(ret_ps.sem, ret_ps.at(it, l * NB * H1 + (b + 1) * H1))
                        src = bank[7 if b == 0 else 3][:, :].rearrange("p (q t) -> p q t", q=2)
                        A(Osb[:, 0:2, b * T:(b + 1) * T], src, ACT.Copy)
                        A(sq[:, :, b * T:(b + 1) * T], src, ACT.Square).then_inc(ret_copied.sem, 1)
                    piece(SLOTS * l + 3)
                    piece(SLOTS * l + 4)
                    turned(2 * l + 2)
                    for j in range(2):
                        act.wait_ge(ffh_ps.sem, ffh_ps.at(it, 2 * l + j + 1))
                        A(Hh[:, j], bank[j][:, :], ACT.Gelu_apprx_tanh).then_inc(gelu_ready.sem, 1)
                    piece(SLOTS * l + 5)

        @block.gpsimd
        def _(pool):
            nc.gpsimd.memset(Vx[:], 0.0).then_inc(set_up, 1)
            nc.gpsimd.memset(Vr[:], 0.0)
            nc.gpsimd.memset(mpad[:], 0.0)
            pool.wait_ge(set_up, 3)
            nc.gpsimd.memset(Vx[:, :, :, DH0:DH0 + 1], 1.0).then_inc(set_up, 1)
            with pool.Fori(0, passes) as it:
                for l in range(L1):
                    pool.wait_ge(qk1_rot.sem, qk1_rot.at(it, 4 * l + 2))
                    nc.gpsimd.tensor_tensor(Qh[:, :], qr[:, 0], qr[:, 1], ALU.add).then_inc(q1_ready.sem, 1)

        @block.vector
        def _(dve):
            V = nc.vector
            dve.wait_ge(weights_in, 16 * len(w))
            dve.wait_ge(set_up, 4)
            with dve.Fori(0, passes) as it:
                steps = [0]

                def link(ins):
                    steps[0] += 1
                    ins.then_inc(dve_step.sem, 1)
                    dve.wait_ge(dve_step.sem, dve_step.at(it, steps[0]))

                def settle():
                    V.memset(settled[:, :], 0.0)

                def rsqrt(n):
                    v, half, y, t = (nv[:, j, 0:n] for j in range(4))
                    V.tensor_scalar(half, v, -0.5, None, ALU.mult)
                    link(V.tensor_scalar(t.bitcast(I32), v.bitcast(I32), 1, None, ALU.logical_shift_right))
                    link(V.tensor_scalar(y.bitcast(I32), t.bitcast(I32), -1.0, float(0x5F3759DF), ALU.mult, ALU.add))
                    for _ in range(3):
                        link(V.tensor_tensor(t, y, y, ALU.mult))
                        link(V.tensor_tensor(t, t, half, ALU.mult))
                        link(V.scalar_tensor_tensor(y, t, 1.5, y, ALU.add, ALU.mult))

                def layer_norm(src, dst):
                    for k in range(NT):
                        last = V.bn_stats(st[:, k], src[:, k])
                    link(last)
                    settle()
                    for k in range(NT):
                        last = V.bn_aggr(mv[:, k], st[:, k])
                    link(last)
                    link(V.tensor_scalar(nv[:, 0, 0:NT], mv[:, :, 1], EPS, None, ALU.add))
                    rsqrt(NT)
                    for k in range(NT):
                        last = V.tensor_scalar(dst[:, k], src[:, k], mv[:, k, 0:1], nv[:, 2, k:k + 1], ALU.subtract, ALU.mult)
                    return last

                def gate(block_no, n, bias):
                    dve.wait_ge(logit_ps.sem, logit_ps.at(it, block_no))
                    src = bank[7][:, 0:NT * 16].rearrange("p (k e) -> p k e", k=NT)[:, :, 0:n]
                    if bias is not None:
                        ins = V.tensor_tensor(lg[:, :, 0:n], src, bias, ALU.add)
                    else:
                        ins = V.tensor_copy(lg[:, :, 0:n], src)
                    ins.then_inc(logits_read.sem, 1)
                    dve.wait_ge(logits_read.sem, logits_read.at(it, block_no))
                    settle()
                    for k in range(NT):
                        last = V.max(m8[:, k], lg[:, k, 0:n])
                    link(last)
                    settle()
                    for k in range(NT):
                        V.max_index(i8[:, k], m8[:, k], lg[:, k, 0:n])
                    V.tensor_tensor(gd[:, :], m8[:, :, 0], m8[:, :, 1], ALU.subtract).then_inc(gap_ready.sem, 1)
                    dve.wait_ge(gap_ready.sem, gap_ready.at(it, block_no))
                    link(V.tensor_copy(i2[:, :, :], i8[:, :, 0:2]))
                    iota = W["iota"][:, :].rearrange("p (k e) -> p k e", k=NT)[:, :, 0:n]
                    for j in range(2):
                        last = V.tensor_tensor(ge[:, j, :, 0:n], iota, i2[:, :, j:j + 1].to_broadcast([P, NT, n]), ALU.is_equal)
                    link(last)
                    dve.wait_ge(gate_tanh.sem, gate_tanh.at(it, block_no))
                    V.tensor_scalar(gw[:, 0], gth[:, :], 0.25, 0.25, ALU.mult, ALU.add)
                    link(V.tensor_scalar(gw[:, 1], gth[:, :], -0.25, 0.25, ALU.mult, ALU.add))
                    for j in range(2):
                        last = V.tensor_tensor(ge[:, j, :, 0:n], ge[:, j, :, 0:n], gw[:, j].unsqueeze(2).to_broadcast([P, NT, n]), ALU.mult)
                    link(last)
                    link(V.tensor_tensor(comb[:, :, 0:n], ge[:, 0, :, 0:n], ge[:, 1, :, 0:n], ALU.add))

                def silu0(e):
                    for m in range(2):
                        dve.wait_ge(up_tanh.sem, up_tanh.at(it, 2 * e + m + 1))
                        last = V.scalar_tensor_tensor(hf[:, 2 * (e % 2) + m], th[:, m], 1.0, bank[4 + m][:, :], ALU.add, ALU.mult)
                    last.then_inc(hid_ready.sem, 1)

                def add0(e):
                    dve.wait_ge(down_ps.sem, down_ps.at(it, e + 1))
                    if e:
                        dve.wait_ge(down_added.sem, down_added.at(it, e))
                    for k in range(NT):
                        last = V.scalar_tensor_tensor(acc[:, k], bank[6][:, k * P:(k + 1) * P], comb[:, k, e:e + 1], acc[:, k], ALU.mult, ALU.add)
                    last.then_inc(down_added.sem, 1)

                dve.wait_ge(x_loaded.sem, x_loaded.at(it, 16))
                layer_norm(x_in, xn).then_inc(xn_ready.sem, 1)
                for g in range(2):
                    dve.wait_ge(qk_ps.sem, qk_ps.at(it, 3 + g))
                    last = V.tensor_tensor(Kg[:, g], bank[2 + g][:, :], W["pos_k"][:, :], ALU.add)
                link(last)
                for h in range(H0):
                    V.tensor_scalar(Km[:, h], Kg[:, h // HG], W["head_mask"][:, h % HG:h % HG + 1], None, ALU.mult).then_inc(k_ready.sem, 1)
                gate(1, EALL0, W["bias0"][:, :].rearrange("p (k e) -> p k e", k=NT))
                link(V.tensor_reduce(wz[:, :], comb[:, :, E0:EALL0], AX.X, ALU.add))
                link(V.tensor_scalar(wz[:, :], wz[:, :], 2.0, None, ALU.mult))
                for k in range(NT):
                    last = V.scalar_tensor_tensor(acc[:, k], xn[:, k], wz[:, k:k + 1], x_in[:, k], ALU.mult, ALU.add)
                last.then_inc(x_used.sem, 1)
                dve.wait_ge(x_used.sem, x_used.at(it, 1))
                silu0(0)
                for b in range(NB):
                    for i in range(NP1):
                        n = b * NP1 + i
                        dve.wait_ge(rows_ps.sem, rows_ps.at(it, n + 1))
                        if i == 0 and b:
                            dve.wait_ge(mpadT_ps.sem, mpadT_ps.at(it, b))
                        if i < 4:
                            g, h, cnt, k = i // 2, (i % 2) * 4, 4, 0
                        else:
                            g, h, cnt, k = (i - 4) // 4, ((i - 4) % 4) * 2, 2, 1
                        V.tensor_reduce(mpad[:, k, g, h:h + cnt, RM:RM + 1], bank[n % 3][:, :].rearrange("p (h s) -> p h s", h=cnt),
                                        AX.X, ALU.max).then_inc(rows_max.sem, 1)
                        if n % 3 == 2:
                            e = n // 3
                            add0(e)
                            if e + 1 < E0:
                                silu0(e + 1)
                    dve.wait_ge(mpadT_ps.sem, mpadT_ps.at(it, b + 1))
                    for g in range(2):
                        last = V.tensor_tensor(Qg[:, g, b * T:(b + 1) * T], Qg[:, g, b * T:(b + 1) * T], bank[7][:, g * T:(g + 1) * T], ALU.subtract)
                    last.then_inc(q_shifted.sem, 1)
                for q in range(4):
                    dve.wait_ge(sums_ps.sem, sums_ps.at(it, q + 1))
                    link(V.reciprocal(rc[:, :], bank[q % 3][:, :]))
                    V.tensor_tensor(On[:, q], Osb[:, q], rc[:, :], ALU.mult).then_inc(o_ready.sem, 1)
                    dve.wait_ge(o_ready.sem, o_ready.at(it, q + 1))
                dve.wait_ge(y0_ps.sem, y0_ps.at(it, 1))
                x1f, accf = x1[:].rearrange("p k c -> p (k c)"), acc[:].rearrange("p k c -> p (k c)")
                link(V.tensor_tensor(x1f, accf, bank[7][:, :], ALU.add))

                layer_norm(x1, xn).then_inc(xn_ready.sem, 1)
                dve.wait_ge(xn_ready.sem, xn_ready.at(it, 2))
                layer_norm(xn, xh).then_inc(ln_ready.sem, 1)
                gate(2, E1, None)

                def piece(i):
                    if i >= len(pieces):
                        return
                    kind, a, _ = pieces[i]
                    if kind == "up":
                        dve.wait_ge(up1_tanh.sem, up1_tanh.at(it, a + 1))
                        link(V.scalar_tensor_tensor(fs[:, 0], th[:, a % 2], 1.0, bank[4][:, :], ALU.add, ALU.mult))
                        V.tensor_tensor(hf[:, a % 4], fs[:, 0], bank[5][:, :], ALU.mult).then_inc(hid1_ready.sem, 1)
                        dve.wait_ge(hid1_ready.sem, hid1_ready.at(it, a + 1))
                    else:
                        dve.wait_ge(down1_ps.sem, down1_ps.at(it, a + 1))
                        if a:
                            dve.wait_ge(down1_added.sem, down1_added.at(it, a))
                        for k in range(NT):
                            s = comb[:, k, a:a + 1] if a < E1 else 0.5
                            last = V.scalar_tensor_tensor(x1[:, k], bank[6][:, k * P:(k + 1) * P], s, x1[:, k], ALU.mult, ALU.add)
                        last.then_inc(down1_added.sem, 1)

                flat = lambda t: t[:].rearrange("p k c -> p (k c)")
                for l in range(L1):
                    piece(SLOTS * l)
                    for j in range(4):
                        dve.wait_ge(qk1_ps.sem, qk1_ps.at(it, 4 * l + j + 1))
                        V.tensor_tensor(qr[:, j], bank[j][:, :], W["rope"][:, j * TOK:(j + 1) * TOK], ALU.mult).then_inc(qk1_rot.sem, 1)
                    dve.wait_ge(qk1_rot.sem, qk1_rot.at(it, 4 * l + 4))
                    link(V.tensor_tensor(Kh[:, :], qr[:, 2], qr[:, 3], ALU.add))
                    for h in range(H1):
                        V.tensor_scalar(Km[:, h], Kh[:, :], W["head_mask"][:, h:h + 1], None, ALU.mult).then_inc(k1_ready.sem, 1)
                    for q in range(2):
                        dve.wait_ge(g_tanh.sem, g_tanh.at(it, 2 * l + q + 1))
                        V.scalar_tensor_tensor(Gs[:, q], gt2[:, q], 1.0, bank[q][:, :], ALU.add, ALU.mult).then_inc(g_ready.sem, 1)
                    piece(SLOTS * l + 1)
                    ring = [2, 0, 1]
                    for n in range(NB * H1):
                        dve.wait_ge(att_ps.sem, att_ps.at(it, l * NB * H1 + n + 1))
                        if n >= NPR:
                            dve.wait_ge(ret_ps.sem, ret_ps.at(it, l * NB * H1 + n - NPR + 1))
                        V.tensor_tensor(Pr[:, n % NPR], bank[ring[n % 3]][:, 0:BLK], W["causal"][:, :], ALU.mult).then_inc(att_ready.sem, 1)
                        if n == 8:
                            piece(SLOTS * l + 2)
                    dve.wait_ge(var_ps.sem, var_ps.at(it, l + 1))
                    link(V.tensor_scalar(nv[:, 0, :], bank[0][:, 0:32], EPS, None, ALU.add))
                    rsqrt(32)
                    V.tensor_copy(rsx[:].rearrange("p k q r c -> p (k q r) c"), nv[:, 2, :].unsqueeze(2).to_broadcast([P, 32, 32])).then_inc(rstd_ready.sem, 1)
                    piece(SLOTS * l + 3)
                    for q in range(2):
                        dve.wait_ge(rstdT_ps.sem, rstdT_ps.at(it, 2 * l + q + 1))
                        link(V.tensor_tensor(Z[:, q], Osb[:, q], bank[1 + q][:, :], ALU.mult))
                        g = 2 * l + q
                        link(V.tensor_scalar(Z[:, q], Z[:, q], W["gn_s"][:, g:g + 1], W["gn_b"][:, g:g + 1], ALU.mult, ALU.add))
                        V.tensor_tensor(Z[:, q], Z[:, q], Gs[:, q], ALU.mult).then_inc(z_ready.sem, 1)
                    dve.wait_ge(wo_ps.sem, wo_ps.at(it, l + 1))
                    link(V.tensor_tensor(flat(Yr), flat(xn if l == 0 else X), bank[3][:, :], ALU.add))
                    layer_norm(Yr, xh).then_inc(ln_ready.sem, 1)
                    piece(SLOTS * l + 4)
                    piece(SLOTS * l + 5)
                    dve.wait_ge(w2_ps.sem, w2_ps.at(it, l + 1))
                    link(V.tensor_tensor(flat(X), flat(Yr), bank[3][:, :], ALU.add))
                    if l + 1 < L1:
                        layer_norm(X, xh).then_inc(ln_ready.sem, 1)
                dve.wait_ge(out_free.sem, out_free.at(it, 1))
                dve.wait_ge(down1_added.sem, down1_added.at(it, E1 + 1))
                V.tensor_tensor(flat(x_out), flat(x1), flat(X), ALU.add).then_inc(out_ready.sem, 1)
                assert steps[0] == dve_step.per_pass, steps[0]


def laid_out(a):
    f = np.float32

    def z(*s):
        return np.zeros(s, f)

    w = {}
    wq, wk = z(P, 2, 8, 16), z(P, 2, 8, 16)
    wq[..., 0:8] = a["L0_attn_Wq"].T.reshape(P, 2, 8, 8)
    wk[..., 0:8] = a["L0_attn_Wk"].T.reshape(P, 2, 8, 8)
    w["wq"], w["wk"] = wq, wk
    w["wv"] = a["L0_attn_Wv"].T
    wo = z(4, 32, 4, P)
    wo[:, 0:8] = a["L0_attn_Wo"].T.reshape(4, 4, 8, P).transpose(1, 2, 0, 3)
    w["wo"] = wo
    w["gate0"] = a["L0_ffn_gate_w"].T
    w["bias0"] = np.broadcast_to(a["L0_ffn_expert_bias"][None, None], (P, NT, EALL0))
    w["w1"] = a["L0_ffn_w1"].transpose(2, 0, 1)
    w["w2"] = a["L0_ffn_w2"].reshape(E0, P, 2, P).transpose(3, 0, 2, 1)
    swap = np.arange(P) ^ 1
    for n in ("q", "k"):
        m = a[f"L1_attn_W{n}"].transpose(1, 0, 2)
        w[f"w{n}1"] = m
        w[f"w{n}s1"] = m[:, :, swap]
    w["wvT1"] = a["L1_attn_Wv"].transpose(2, 0, 1)
    wg = z(P, L1, 2, 4, 32)
    wg[..., 0:16] = a["L1_attn_Wg"].transpose(1, 0, 2).reshape(P, L1, 2, 4, 16)
    w["wg1"] = wg
    wo = z(4, 32, L1, 2, P)
    wo[:, 0:16] = a["L1_attn_Wo"].reshape(L1, 2, 4, 16, P).transpose(2, 3, 0, 1, 4)
    w["wo1"] = wo
    w["w11"] = a["L1_attn_W1"].transpose(1, 0, 2)
    w["w21"] = a["L1_attn_W2"].reshape(L1, 2, P, P).transpose(2, 0, 1, 3)
    w["ln_s"] = a["L1_attn_ln_scale"][:, None]
    w["ln_b"] = a["L1_attn_ln_bias"][:, None]
    for n, s in (("gn_s", "scale"), ("gn_b", "bias")):
        g = z(4, 32, L1, 2)
        g[:, 0:16] = a[f"L1_attn_gn_{s}"].reshape(L1, 2, 4, 16).transpose(2, 3, 0, 1)
        w[n] = g
    w["gate1"] = a["L1_ffn_gate_w"].T
    up, half = a["L1_ffn_w_up"], 192
    blocks = []
    for p in range(E1 // 2):
        for e in (2 * p, 2 * p + 1):
            blocks += [up[e, 0:P], up[e, half:half + P]]
        for o in (0, half):
            blocks.append(np.concatenate([up[2 * p, o + P:o + half], up[2 * p + 1, o + P:o + half]]))
    sg, su = a["L1_ffn_sg_gate"], a["L1_ffn_sg_up"]
    blocks += [sg[0:P], su[0:P]]
    blocks += [np.concatenate([s[P:half], z(64, P)]) for s in (sg, su)]
    w["wup"] = np.stack(blocks).transpose(2, 0, 1)
    dn = z(P, E1 + 1, 2, P)
    for e in range(E1 + 1):
        m = (a["L1_ffn_w_down"][e] if e < E1 else a["L1_ffn_sg_down"]).T
        o = 64 * (e % 2) if e < E1 else 0
        dn[:, e, 0] = m[0:P]
        dn[o:o + 64, e, 1] = m[P:half]
    w["wdn"] = dn
    return {n: np.ascontiguousarray(v.reshape(P, -1)) for n, v in w.items()}


def kernel(**inputs):
    import concourse.bacc as bacc
    from concourse.bass_utils import run_bass_kernel_spmd

    a = {n: np.asarray(v) for n, v in inputs.items()}
    shape = a["L0_attn_x"].shape
    arrays = laid_out(a)
    arrays.update(shape_constants())
    nc = bacc.Bacc("TRN2", target_bir_lowering=False, num_devices=1)
    w = {n: nc.dram_tensor("w_" + n, v.shape, mybir.dt.from_np(v.dtype), kind="ExternalInput").ap() for n, v in arrays.items()}
    x = np.ascontiguousarray(a["L0_attn_x"].reshape(-1, D))
    x_dram = nc.dram_tensor("x", x.shape, F32, kind="ExternalInput").ap()
    out = nc.dram_tensor("out", x.shape, F32, kind="ExternalOutput").ap()
    program(nc, x_dram, out, w)
    feed = {"w_" + n: v for n, v in arrays.items()}
    feed["x"] = x
    r = run_bass_kernel_spmd(nc, [feed], core_ids=[0])
    return r.results[0]["out"].reshape(shape)
```

```python
from contextlib import ExitStack

import numpy as np

import concourse.bass as bass
from concourse import mybir

P = 128
F32 = mybir.dt.float32
BF16 = mybir.dt.bfloat16
I32 = mybir.dt.int32
U32 = mybir.dt.uint32
ALU = mybir.AluOpType
ACT = mybir.ActivationFunctionType
AX = mybir.AxisListType

T = 256
NB = 2
TOK = NB * T
NT = TOK // P
D = 128
H0, DH0 = 16, 8
H1, DH1, L1 = 8, 16, 4
HG = 8
RM, RS = 8, 9
E0, EALL0 = 8, 12
E1 = 8
BLK = 384
EPS = 1e-5
BIG = -1e30
EARLY = 6
HEAD_LAYER = 1
HEAD_STEPS = 9
BODY_STEPS = 59


class Sig:

    def __init__(self, sem, per_pass):
        self.sem, self.per_pass = sem, per_pass

    def at(self, it, n):
        return it * self.per_pass + n


def shape_constants():
    def bf16_bits(t):
        return (t.view(np.uint32) >> 16).astype(np.uint16)

    f = np.float32
    p = np.arange(P)
    c = {}
    slopes = np.power(f(2.0), (f(-8.0) * np.arange(1, H0 + 1, dtype=f) / f(H0))).astype(f)
    bias_q = np.zeros((P, 2), f)
    pos_k = np.zeros((P, TOK), f)
    for g in range(2):
        for h in range(HG):
            bias_q[h * 16 + RS, g] = slopes[g * HG + h]
    s = np.tile(np.arange(T), NB)
    pos_k[RM::16] = 1.0
    pos_k[RS::16] = s - 128.0
    c["bias_q"], c["pos_k"] = bias_q, pos_k
    c["head_mask"] = (p[:, None] // 16 == np.arange(8)[None]).astype(f)
    c["ident"] = np.eye(P, dtype=f)
    c["ident_bf"] = bf16_bits(np.eye(P, dtype=f))
    later = np.where(p[None] > p[:, None], f(BIG), f(0))
    zero = np.zeros((P, P), f)
    c["mask_q0"] = bf16_bits(np.concatenate([later] * 4, 1))
    c["mask_q1"] = bf16_bits(np.concatenate([zero, later] * 2, 1))
    c["mask_k"] = bf16_bits(np.concatenate([later.T, zero, later.T], 1))
    c["sum_rows"] = (p[:, None] == 32 * (np.arange(32)[None] % 4) + DH0).astype(f)
    c["spread"] = np.concatenate([(p[:, None] == 32 * q + p[None] // 32) for q in range(4)], 1).astype(f)
    c["minus_half"] = np.full((P, 16), -0.5, f)
    c["eps"] = np.full((P, 2), EPS, f)
    c["mean_sq"] = ((p[:, None] // 32 == np.arange(4)[None]) & (p[:, None] % 32 < DH1)).astype(f) / f(DH1)
    c["centre"] = (np.eye(P) - (p[:, None] // DH1 == p[None] // DH1) / DH1).astype(f)
    keep = (p[None] >= p[:, None]).astype(f)
    c["causal"] = np.concatenate([keep, zero + 1, keep], 1).astype(f)
    c["iota"] = np.tile(np.arange(16, dtype=f)[None, None], (P, NT, 1)).reshape(P, NT * 16)
    gammas = (f(1.0) - np.exp(np.linspace(np.log(1 / 32), np.log(1 / 64), H1)).astype(f)).astype(f)
    log_g = np.log(gammas).astype(f).astype(np.float64)[p // DH1][:, None]
    inv_freq = (f(1.0) / np.power(f(10000.0), np.arange(0, DH1, 2, dtype=f) / f(DH1))).astype(f)
    ang = (np.arange(T, dtype=f)[None] * inv_freq[(p % DH1) // 2][:, None]).astype(f).astype(np.float64)
    sign = np.where(p % 2 == 0, -1.0, 1.0)[:, None]
    n = np.arange(T)[None] - 128.0
    dq, dk = np.exp(n * log_g), np.exp(-n * log_g)
    rope = [np.cos(ang) * dq, np.sin(ang) * sign * dq, np.cos(ang) * dk, -np.sin(ang) * sign * dk]
    c["rope"] = np.concatenate(rope, 1).astype(f)
    return c


def program(nc, x, out, w):
    passes = x.shape[0] // TOK
    with ExitStack() as ctx:
        def sb(name, shape, dt=F32):
            return ctx.enter_context(nc.sbuf_tensor(name, shape, dt))

        sigs = {}

        def sig(name, per_pass):
            sigs[name] = Sig(ctx.enter_context(nc.semaphore(name)), per_pass)
            return sigs[name]

        W = {n: sb("s_" + n, list(a.shape), a.dtype) for n, a in w.items()}
        wv_c = sb("wv_c", [P, L1 * P])
        ident_bf = W["ident_bf"][:, :].bitcast(BF16)

        x_in = sb("x_in", [P, NT, D])
        xn0 = sb("xn0", [P, NT, D])
        xnT0 = sb("xnT0", [P, TOK])
        xn = sb("xn", [P, NT, D])
        xnT = sb("xnT", [P, TOK])
        acc = sb("acc", [P, NT, D])
        settled = sb("settled", [P, 1])
        st0, st = sb("st0", [P, NT, 6]), sb("st", [P, NT, 6])
        mv0, mv = sb("mv0", [P, NT, 2]), sb("mv", [P, NT, 2])
        ln_v0, ln_v = sb("ln_v0", [P, NT, 1]), sb("ln_v", [P, NT, 1])
        ln_r0, ln_r = sb("ln_r0", [P, NT, 1]), sb("ln_r", [P, NT, 1])
        lg = sb("lg", [P, NT, 16])
        m8 = sb("m8", [P, NT, 8])
        i8 = sb("i8", [P, NT, 8], U32)
        i2 = sb("i2", [P, NT, 2])
        gd = sb("gd", [P, NT])
        gth = sb("gth", [P, NT])
        gw = sb("gw", [P, 2, NT])
        ge = sb("ge", [P, 2, NT, 16])
        comb0 = sb("comb0", [P, NT, 16])
        comb = sb("comb", [P, NT, 16])
        wz = sb("wz", [P, NT])
        Qg = sb("Qg", [P, 2, TOK])
        Kg = sb("Kg", [P, 2, TOK])
        Km = sb("Km", [P, H0, TOK])
        Vx = sb("Vx", [P, NT, H0, 32])
        mpad = sb("mpad", [P, 2, 2, HG, 16])
        NPR = 8
        Pr = sb("Pr", [P, NPR, BLK])
        Osb = sb("Osb", [P, 4, TOK])
        On = sb("On", [P, 4, TOK])
        rc = sb("rc", [P, T])
        th = sb("th", [P, 2, TOK])
        hf = sb("hf", [P, 4, TOK])
        x1 = sb("x1", [P, NT, D])
        X = sb("X", [P, NT, D])
        Yr = sb("Yr", [P, NT, D])
        xh = sb("xh", [P, NT, D])
        hT = sb("hT", [P, TOK])
        qr = On[:, :, :].rearrange("p (b j) t -> p b j t", b=NB)
        Qh, Kh = Km[:, H1], Km[:, H1 + 1]
        Gs, sq, Hh = (Km[:, H1 + j:H1 + j + 2] for j in (2, 4, 6))
        Z = Osb[:, 2:4]
        Vr = sb("Vr", [P, NT, H1, 32])
        rsx = Kg[:, :, :].rearrange("p b (n c) -> p b n c", c=32)
        rv = sb("rv", [P, NB, 16])
        rr = sb("rr", [P, NB, 16])

        bank = [ctx.enter_context(nc.psum_tensor(f"bank{i}", [P, 512], F32)) for i in range(8)]

        weights_in = ctx.enter_context(nc.semaphore("weights_in"))
        set_up = ctx.enter_context(nc.semaphore("set_up"))
        fold_ps = ctx.enter_context(nc.semaphore("fold_ps"))
        x_loaded = sig("x_loaded", 16)
        x_used = sig("x_used", 1)
        stored = sig("stored", 16)
        out_ready = sig("out_ready", 1)
        out_free = sig("out_free", 1)
        head_step = sig("head_step", HEAD_STEPS)
        body_step = sig("body_step", BODY_STEPS)
        stats0 = sig("stats0", NB)
        eps0 = sig("eps0", NB)
        root0 = sig("root0", NB)
        xn0_ready = sig("xn0_ready", 1)
        xnT0_ps = sig("xnT0_ps", 1)
        xnT0_ready = sig("xnT0_ready", 1)
        logits0_ps = sig("logits0_ps", 1)
        logits0_read = sig("logits0_read", 1)
        gap0_ready = sig("gap0_ready", 1)
        tanh0_ready = sig("tanh0_ready", 1)
        NLN = NB * (1 + 2 * L1)
        ln_stats = sig("ln_stats", NLN)
        ln_eps = sig("ln_eps", NLN)
        ln_root = sig("ln_root", NLN)
        xn_ready = sig("xn_ready", NB)
        xnT_ps = sig("xnT_ps", NB)
        xnT_ready = sig("xnT_ready", NB)
        logits_ps = sig("logits_ps", 1)
        logits_read = sig("logits_read", 1)
        gap_ready = sig("gap_ready", 1)
        tanh_ready = sig("tanh_ready", 1)
        kk0_ps = sig("kk0_ps", 2)
        qq0_ps = sig("qq0_ps", 2)
        v_ps = sig("v_ps", 1)
        q_ready = sig("q_ready", 2)
        k_ready = sig("k_ready", H0)
        v_ready = sig("v_ready", 1)
        NP1 = 12
        rows_ps = sig("rows_ps", NB * NP1)
        rows_max = sig("rows_max", NB * NP1)
        mpadT_ps = sig("mpadT_ps", NB)
        q_shifted = sig("q_shifted", NB)
        cols_ps = sig("cols_ps", NB * H0)
        exp_ready = sig("exp_ready", NB * H0)
        NG = NB * H0 // 4
        pv_ps = sig("pv_ps", NG)
        pv_copied = sig("pv_copied", NG // 2)
        sums_ps = sig("sums_ps", NB)
        sums_inv = sig("sums_inv", NB)
        spread_ps = sig("spread_ps", 2 * NB)
        o_ready = sig("o_ready", 2 * NB)
        y0_ps = sig("y0_ps", NB)
        y0_added = sig("y0_added", 1)
        up_ps = sig("up_ps", 2 * E0)
        hid_ready = sig("hid_ready", 2 * E0)
        down_ps = sig("down_ps", NB * E0)
        down_added = sig("down_added", NB * E0)
        C1 = 3 * (E1 // 2) + 2
        gate1_ps = sig("gate1_ps", C1)
        up1_ps = sig("up1_ps", C1)
        silu1_ready = sig("silu1_ready", C1)
        hid1_ready = sig("hid1_ready", C1)
        down1_ps = sig("down1_ps", NB * (E1 + 1))
        down1_added = sig("down1_added", NB * (E1 + 1))
        LB = L1 * NB
        ln_ready = sig("ln_ready", 2 * LB)
        lnT_ps = sig("lnT_ps", 2 * LB)
        lnT_ready = sig("lnT_ready", 2 * LB)
        qq_ps = sig("qq_ps", LB)
        kk_ps = sig("kk_ps", LB)
        v1_ps = sig("v1_ps", LB)
        v1_ready = sig("v1_ready", LB)
        q1_rot = sig("q1_rot", LB)
        q1_ready = sig("q1_ready", LB)
        k1_sum = sig("k1_sum", LB)
        KD, KA = 5, 3
        k1_dve = sig("k1_dve", LB * KD)
        k1_act = sig("k1_act", LB * KA)
        g_ps = sig("g_ps", LB)
        g_ready = sig("g_ready", LB)
        g_scaled = sig("g_scaled", LB)
        att_ps = sig("att_ps", H1 * LB)
        att_ready = sig("att_ready", H1 * LB)
        ret_ps = sig("ret_ps", 2 * LB)
        ret_copied = sig("ret_copied", LB)
        var_ps = sig("var_ps", LB)
        var_read = sig("var_read", LB)
        var_root = sig("var_root", LB)
        roots_wide = sig("roots_wide", LB)
        rootsT_ps = sig("rootsT_ps", LB)
        z_weighed = sig("z_weighed", LB)
        z_ready = sig("z_ready", LB)
        wo_ps = sig("wo_ps", LB)
        ffh_ps = sig("ffh_ps", LB)
        gelu_ready = sig("gelu_ready", LB)
        w2_ps = sig("w2_ps", LB)

        pieces = []

        def couple(a, c):
            return [("gate", a, c), ("up", a, c + 1)]

        base = 3 * (E1 // 2)
        for pair in range(E1 // 2):
            if pair == 0:
                pieces += couple(0, 0) + couple(1, 2)
            pieces += couple(3 * pair + 2, 6 * pair + 4)
            for odd in range(2):
                hidden = couple(3 * pair + 3 + odd, 6 * pair + 6 + 2 * odd)
                pieces += [hidden[0], ("down", 2 * pair + odd, 0), hidden[1], ("down", 2 * pair + odd, 1)]
        pieces += [("down", E1, b) for b in range(NB)]
        head = [("turn0", 0, 0), ("logits0", 0, 0), ("up0", 0, 0), ("up0", 0, 1)]
        for e in range(1, EARLY):
            head += [("up0", e, 0), ("down0", e - 1, 0), ("up0", e, 1), ("down0", e - 1, 1)]
        head += [("down0", EARLY - 1, b) for b in range(NB)]
        pieces += head
        plan = [[0, 1, 1, 1, 1, 0, 2, 2, 1, 2, 1, 1, 2, 3]] + [[1, 1, 1, 1, 1, 0, 2, 2, 1, 2, 1, 1, 2, 3]] * (L1 - 1)
        starts = np.cumsum([0] + [n for layer in plan for n in layer]).tolist()

        def slot(l, s):
            i = sum(len(layer) for layer in plan[:l]) + s
            last = l == L1 - 1 and s == len(plan[l]) - 1
            return pieces[starts[i]:len(pieces) if last else starts[i + 1]]

        def down_blocks(e):
            pair, odd = (e // 2, e % 2)
            a = 3 * pair + odd
            b = 3 * pair + 2 if e < E1 else base + 1
            return [(a, 2 * e), (b, 2 * e + 1)]

        A_bank = [bank[0], bank[2]]
        B_bank = [bank[1], bank[3]]

        def half(b):
            return slice(b * T, (b + 1) * T)

        def tiles(b):
            return range(2 * b, 2 * b + 2)

        def pair_view(t):
            return t[:, 0:TOK].rearrange("p (q t) -> p q t", q=2)

        block = ctx.enter_context(nc.Block())

        @block.sync
        def _(sp):
            for n in w:
                sp.dma_start(W[n][:, :], w[n]).then_inc(weights_in, 16)

            def load(p):
                sp.dma_start(x_in[:], x[bass.ds(p * TOK, TOK), :].rearrange("(k p) c -> p k c", p=P)).then_inc(x_loaded.sem, 16)

            def store(p):
                sp.wait_ge(out_ready.sem, out_ready.at(p, 1))
                sp.dma_start(out[bass.ds(p * TOK, TOK), :].rearrange("(k p) c -> p k c", p=P), X[:]).then_inc(stored.sem, 16)
                sp.wait_ge(stored.sem, stored.at(p, 16))
                sp.sem_inc(out_free.sem, 1)

            sp.sem_inc(out_free.sem, 1)
            load(0)
            with sp.Fori(0, passes - 1) as it:
                sp.wait_ge(x_used.sem, x_used.at(it, 1))
                load(it + 1)
                store(it)
            store(passes - 1)

        @block.tensor
        def _(pe):
            mm = nc.tensor.matmul
            pe.wait_ge(weights_in, 16 * len(w))
            for l in range(L1):
                mm(bank[l][:, 0:P], W["wvT1"][:, l * P:(l + 1) * P], W["centre"][:, :], start=True, stop=True).then_inc(fold_ps, 1)
            pe.wait_ge(set_up, 3)

            def transposes(dst, col, src, tiles):
                for j, k in enumerate(tiles):
                    last = nc.tensor.transpose(dst[:, col + j * P:col + (j + 1) * P], src[:, k, :], W["ident"][:, :])
                return last

            def by_token(dst, lhs, rhs_blocks, tiles, col=0):
                for i, k in enumerate(tiles):
                    n = len(rhs_blocks)
                    for j in range(n):
                        last = mm(dst[:, col + i * P:col + (i + 1) * P], lhs[j][:, k * P:(k + 1) * P], rhs_blocks[j],
                                  start=(j == 0), stop=(j == n - 1))
                return last

            def four_heads(dst, col, values, probs):
                for r in range(4):
                    mm(dst[32 * r:32 * r + 32, col:col + T], values[r][0], probs[r][:, 0:T], start=True, stop=False, skip_group_check=True)
                for r in range(4):
                    last = mm(dst[32 * r:32 * r + 32, col + P:col + T], values[r][1], probs[r][:, T:BLK], start=False, stop=True,
                              skip_group_check=True)
                return last

            def up0(p, e, m):
                if e:
                    pe.wait_ge(hid_ready.sem, hid_ready.at(p, 2 * e + m - 1))
                c = (2 * e + m) * P
                mm(bank[4 + m][:, :], W["w1"][:, c:c + P], xnT0[:, :], start=True, stop=True).then_inc(up_ps.sem, 1)

            def down0(p, e, b):
                pe.wait_ge(hid_ready.sem, hid_ready.at(p, 2 * e + 2))
                if e or b:
                    pe.wait_ge(down_added.sem, down_added.at(p, NB * e + b))
                else:
                    pe.wait_ge(logits0_read.sem, logits0_read.at(p, 1))
                by_token(bank[6], [hf[:, 2 * (e % 2) + m] for m in range(2)],
                         [W["w2"][:, (2 * e + m) * P:(2 * e + m + 1) * P] for m in range(2)], tiles(b), b * T).then_inc(down_ps.sem, 1)

            def run(piece, p, nxt):
                kind, a, c = piece
                if kind == "gate":
                    if a:
                        pe.wait_ge(silu1_ready.sem, silu1_ready.at(p, a))
                    mm(bank[4][:, :], W["wup"][:, c * P:(c + 1) * P], xnT[:, :], start=True, stop=True).then_inc(gate1_ps.sem, 1)
                elif kind == "up":
                    if a:
                        pe.wait_ge(hid1_ready.sem, hid1_ready.at(p, a))
                    mm(bank[5][:, :], W["wup"][:, c * P:(c + 1) * P], xnT[:, :], start=True, stop=True).then_inc(up1_ps.sem, 1)
                elif kind == "down":
                    blocks = down_blocks(a)
                    pe.wait_ge(hid1_ready.sem, hid1_ready.at(p, blocks[1][0] + 1))
                    if a or c:
                        pe.wait_ge(down1_added.sem, down1_added.at(p, NB * a + c))
                    else:
                        pe.wait_ge(logits_read.sem, logits_read.at(p, 1))
                    by_token(bank[6], [hf[:, j[0] % 4] for j in blocks],
                             [W["wdn"][:, j[1] * P:(j[1] + 1) * P] for j in blocks], tiles(c), c * T).then_inc(down1_ps.sem, 1)
                elif nxt is None:
                    return
                elif kind == "turn0":
                    pe.wait_ge(xn0_ready.sem, xn0_ready.at(nxt, 1))
                    if p is not None:
                        pe.wait_ge(down1_added.sem, down1_added.at(p, NB * (E1 + 1)))
                    transposes(bank[6], 0, xn0, range(NT)).then_inc(xnT0_ps.sem, 1)
                elif kind == "logits0":
                    pe.wait_ge(xnT0_ready.sem, xnT0_ready.at(nxt, 1))
                    for k in range(NT):
                        last = mm(bank[6][:, k * 16:k * 16 + EALL0], xnT0[:, k * P:(k + 1) * P], W["gate0"][:, :], start=True, stop=True)
                    last.then_inc(logits0_ps.sem, 1)
                elif kind == "up0":
                    if a == 0 and p is not None:
                        pe.wait_ge(hid1_ready.sem, hid1_ready.at(p, C1))
                    up0(nxt, a, c)
                else:
                    down0(nxt, a, c)

            def project_k(p):
                for j in range(2):
                    mm(bank[2 * j][:, :], W["wk"][:, j * P:(j + 1) * P], xnT0[:, :], start=True, stop=True).then_inc(kk0_ps.sem, 1)

            def project_qv(p):
                for j in range(2):
                    mm(bank[1 + 2 * j][:, :], W["wq"][:, j * P:(j + 1) * P], xnT0[:, :], start=True, stop=True).then_inc(qq0_ps.sem, 1)
                by_token(bank[7], [xnT0], [W["wv"][:, :]], range(NT)).then_inc(v_ps.sem, 1)

            def first_block(it):
                pe.wait_ge(k_ready.sem, k_ready.at(it, 1))
                pe.wait_ge(q_ready.sem, q_ready.at(it, 2))
                for b in range(NB):
                    for i in range(NP1):
                        n = b * NP1 + i
                        t_tile = 0 if i < 4 else 1
                        heads = range(4 * i, 4 * i + 4) if t_tile == 0 else range(2 * (i - 4), 2 * (i - 4) + 2)
                        width = P * (1 + t_tile)
                        if n < 4:
                            pe.wait_ge(k_ready.sem, k_ready.at(it, max(heads) + 1))
                        if n >= 3:
                            pe.wait_ge(rows_max.sem, rows_max.at(it, n - 2))
                        dst = bank[n % 3]
                        mm(dst[:, :], ident_bf, W[f"mask_q{t_tile}"][:, :].bitcast(BF16), start=True, stop=False)
                        q0 = b * T + t_tile * P
                        for j, h in enumerate(heads):
                            last = mm(dst[:, j * width:(j + 1) * width], Qg[:, h // HG, q0:q0 + P],
                                      Km[:, h, b * T:b * T + width], start=False, stop=(j == len(heads) - 1))
                        last.then_inc(rows_ps.sem, 1)
                    up0(it, EARLY, b)
                    pe.wait_ge(rows_max.sem, rows_max.at(it, (b + 1) * NP1))
                    if b == 0:
                        pe.wait_ge(v_ready.sem, v_ready.at(it, 1))
                    else:
                        pe.wait_ge(q_shifted.sem, q_shifted.at(it, b))
                    for g in range(2):
                        for k in range(2):
                            last = nc.tensor.transpose(bank[7][:, (2 * g + k) * P:(2 * g + k + 1) * P],
                                                       mpad[:, k, g].rearrange("p h r -> p (h r)"), W["ident"][:, :])
                    last.then_inc(mpadT_ps.sem, 1)
                down0(it, EARLY, 0)
                pe.wait_ge(q_shifted.sem, q_shifted.at(it, NB))

                def weigh(G):
                    b, q = G // 4, G % 4
                    pe.wait_ge(exp_ready.sem, exp_ready.at(it, 4 * G + 4))
                    if b and q % 2 == 0:
                        pe.wait_ge(pv_copied.sem, pv_copied.at(it, 1 + q // 2))
                    heads = range(4 * q, 4 * q + 4)
                    four_heads(bank[3 if q < 2 else 7], (q % 2) * T,
                               [(Vx[:, 2 * b, h, :], Vx[:, 2 * b + 1, h, :]) for h in heads],
                               [Pr[:, h % NPR] for h in heads]).then_inc(pv_ps.sem, 1)

                def sum_rows(b, dst):
                    pe.wait_ge(pv_copied.sem, pv_copied.at(it, 2 * b + 2))
                    for q in range(4):
                        last = mm(dst[32 * q:32 * q + 32, 0:T], W["sum_rows"][:, :], Osb[:, q, half(b)], start=True, stop=True)
                    last.then_inc(sums_ps.sem, 1)

                def spread(b, banks):
                    pe.wait_ge(sums_inv.sem, sums_inv.at(it, b + 1))
                    for q in range(4):
                        last = mm(banks[q // 2][:, (q % 2) * T:(q % 2 + 1) * T], W["spread"][:, q * P:(q + 1) * P], rc[:, :], start=True, stop=True)
                        if q % 2:
                            last.then_inc(spread_ps.sem, 1)

                def project(b, dst):
                    pe.wait_ge(o_ready.sem, o_ready.at(it, 2 * b + 2))
                    by_token(dst, [On[:, q] for q in range(4)], [W["wo"][:, q * P:(q + 1) * P] for q in range(4)],
                             tiles(b)).then_inc(y0_ps.sem, 1)

                for G in range(NG):
                    for h in range(4 * (G % 4), 4 * (G % 4) + 4):
                        b = G // 4
                        n = b * H0 + h
                        dst = bank[n % 3]
                        if n >= 3:
                            pe.wait_ge(exp_ready.sem, exp_ready.at(it, n - 2))
                        mm(dst[:, 0:BLK], ident_bf, W["mask_k"][:, :].bitcast(BF16), start=True, stop=False)
                        mm(dst[:, 0:T], Km[:, h, b * T:b * T + P], Qg[:, h // HG, half(b)], start=False, stop=False)
                        mm(dst[:, T:BLK], Km[:, h, b * T + P:(b + 1) * T], Qg[:, h // HG, b * T + P:(b + 1) * T], start=False, stop=True).then_inc(cols_ps.sem, 1)
                    if G:
                        weigh(G - 1)
                    if G == 1:
                        down0(it, EARLY, 1)
                    if G == 5:
                        sum_rows(0, bank[4])
                    if G == 6:
                        pe.wait_ge(down_added.sem, down_added.at(it, NB * (E0 - 1)))
                        spread(0, [bank[5], bank[6]])
                    if G == 7:
                        project(0, bank[4])
                pe.wait_ge(y0_added.sem, y0_added.at(it, 1))
                up0(it, E0 - 1, 0)
                weigh(NG - 1)
                up0(it, E0 - 1, 1)
                sum_rows(1, bank[0])
                down0(it, E0 - 1, 0)
                spread(1, [bank[1], bank[2]])
                down0(it, E0 - 1, 1)
                project(1, bank[3])

            def second_block(it, nxt):
                def turn_input(b):
                    pe.wait_ge(xn_ready.sem, xn_ready.at(it, b + 1))
                    transposes(bank[7 - b], 0, xn, tiles(b)).then_inc(xnT_ps.sem, 1)

                def fill(l, s):
                    for piece in slot(l, s):
                        run(piece, it, nxt)

                turn_input(0)
                for l in range(L1):
                    def turn(which, b, dst):
                        n = (2 * l + which) * NB + b + 1
                        pe.wait_ge(ln_ready.sem, ln_ready.at(it, n))
                        transposes(dst, 0, xh, tiles(b)).then_inc(lnT_ps.sem, 1)

                    def project(b):
                        m = NB * l + b
                        pe.wait_ge(lnT_ready.sem, lnT_ready.at(it, 2 * NB * l + b + 1))
                        for j, name in enumerate(("wk1", "wks1")):
                            last = mm(B_bank[b][:, j * T:(j + 1) * T], W[name][:, l * P:(l + 1) * P], hT[:, half(b)], start=True, stop=True)
                        last.then_inc(kk_ps.sem, 1)
                        for j, name in enumerate(("wq1", "wqs1")):
                            last = mm(A_bank[b][:, j * T:(j + 1) * T], W[name][:, l * P:(l + 1) * P], hT[:, half(b)], start=True, stop=True)
                        last.then_inc(qq_ps.sem, 1)
                        if b:
                            pe.wait_ge(v1_ready.sem, v1_ready.at(it, m))
                        elif l == 0:
                            pe.wait_ge(xnT_ready.sem, xnT_ready.at(it, 1))
                        by_token(bank[7], [hT], [wv_c[:, l * P:(l + 1) * P]], tiles(b)).then_inc(v1_ps.sem, 1)

                    def gates(b):
                        m = NB * l + b
                        pe.wait_ge(q1_rot.sem, q1_rot.at(it, m + 1))
                        for q in range(2):
                            last = mm(A_bank[b][:, q * T:(q + 1) * T], W["wg1"][:, (2 * l + q) * P:(2 * l + q + 1) * P], hT[:, half(b)], start=True, stop=True)
                        last.then_inc(g_ps.sem, 1)

                    def scores(b, heads):
                        m = NB * l + b
                        for h in heads:
                            n = m * H1 + h
                            if h < KD:
                                pe.wait_ge(k1_dve.sem, k1_dve.at(it, m * KD + h + 1))
                            else:
                                pe.wait_ge(k1_act.sem, k1_act.at(it, m * KA + h - KD + 1))
                            if h >= 2 or (b and h == 1):
                                pe.wait_ge(att_ready.sem, att_ready.at(it, n - 1))
                            dst = B_bank[b] if h % 2 == 0 else bank[7]
                            mm(dst[:, 0:T], Km[:, h, b * T:b * T + P], Qh[:, half(b)], start=True, stop=True)
                            mm(dst[:, T:BLK], Km[:, h, b * T + P:(b + 1) * T], Qh[:, b * T + P:(b + 1) * T], start=True, stop=True).then_inc(att_ps.sem, 1)

                    def retain(b, q):
                        m = NB * l + b
                        pe.wait_ge(att_ready.sem, att_ready.at(it, m * H1 + 4 * q + 4))
                        heads = range(4 * q, 4 * q + 4)
                        four_heads(A_bank[b], q * T, [(Vr[:, 2 * b, h, :], Vr[:, 2 * b + 1, h, :]) for h in heads],
                                   [Pr[:, h] for h in heads]).then_inc(ret_ps.sem, 1)

                    def variances(b):
                        m = NB * l + b
                        pe.wait_ge(ret_copied.sem, ret_copied.at(it, m + 1))
                        for k in range(2):
                            for q in range(2):
                                c = (2 * k + q) * 4
                                last = mm(B_bank[b][:, c:c + 4], sq[:, q, (2 * b + k) * P:(2 * b + k + 1) * P], W["mean_sq"][:, :], start=True, stop=True)
                        last.then_inc(var_ps.sem, 1)

                    def spread_roots(b):
                        m = NB * l + b
                        pe.wait_ge(roots_wide.sem, roots_wide.at(it, m + 1))
                        for q in range(2):
                            for k in range(2):
                                last = nc.tensor.transpose(B_bank[b][:, (2 * q + k) * P:(2 * q + k + 1) * P],
                                                           rsx[:, b, (2 * k + q) * 4:(2 * k + q) * 4 + 4, :].rearrange("p r c -> p (r c)"),
                                                           W["ident"][:, :])
                        last.then_inc(rootsT_ps.sem, 1)

                    def out_project(b):
                        m = NB * l + b
                        pe.wait_ge(z_ready.sem, z_ready.at(it, m + 1))
                        by_token(A_bank[b], [Z[:, q] for q in range(2)],
                                 [W["wo1"][:, (2 * l + q) * P:(2 * l + q + 1) * P] for q in range(2)], tiles(b)).then_inc(wo_ps.sem, 1)

                    def hidden(b):
                        pe.wait_ge(lnT_ready.sem, lnT_ready.at(it, (2 * l + 1) * NB + b + 1))
                        for j in range(2):
                            last = mm(A_bank[b][:, j * T:(j + 1) * T], W["w11"][:, (2 * l + j) * P:(2 * l + j + 1) * P], hT[:, half(b)], start=True, stop=True)
                        last.then_inc(ffh_ps.sem, 1)

                    def last_product(b):
                        pe.wait_ge(gelu_ready.sem, gelu_ready.at(it, NB * l + b + 1))
                        by_token(B_bank[b], [Hh[:, j] for j in range(2)],
                                 [W["w21"][:, (2 * l + j) * P:(2 * l + j + 1) * P] for j in range(2)], tiles(b)).then_inc(w2_ps.sem, 1)

                    turn(0, 0, A_bank[0])
                    fill(l, 0)
                    project(0)
                    if l == 0:
                        turn_input(1)
                        pe.wait_ge(xnT_ready.sem, xnT_ready.at(it, 2))
                        for k in range(NT):
                            last = mm(bank[6][:, k * 16:k * 16 + E1], xnT[:, k * P:(k + 1) * P], W["gate1"][:, :], start=True, stop=True)
                        last.then_inc(logits_ps.sem, 1)
                    turn(0, 1, A_bank[1])
                    fill(l, 1)
                    project(1)
                    fill(l, 2)
                    gates(0)
                    gates(1)
                    pe.wait_ge(v1_ready.sem, v1_ready.at(it, NB * l + NB))
                    pe.wait_ge(q1_ready.sem, q1_ready.at(it, NB * l + 1))
                    fill(l, 3)
                    scores(0, range(0, 8))
                    pe.wait_ge(g_ready.sem, g_ready.at(it, NB * l + 1))
                    retain(0, 0)
                    fill(l, 4)
                    pe.wait_ge(q1_ready.sem, q1_ready.at(it, NB * l + 2))
                    scores(1, range(0, 4))
                    retain(0, 1)
                    scores(1, range(4, 6))
                    variances(0)
                    scores(1, range(6, 8))
                    pe.wait_ge(g_ready.sem, g_ready.at(it, NB * l + 2))
                    retain(1, 0)
                    fill(l, 5)
                    retain(1, 1)
                    fill(l, 6)
                    spread_roots(0)
                    variances(1)
                    fill(l, 7)
                    out_project(0)
                    fill(l, 8)
                    spread_roots(1)
                    fill(l, 9)
                    out_project(1)
                    turn(1, 0, B_bank[0])
                    fill(l, 10)
                    hidden(0)
                    turn(1, 1, B_bank[1])
                    fill(l, 11)
                    last_product(0)
                    hidden(1)
                    fill(l, 12)
                    last_product(1)
                    fill(l, 13)
                if nxt is not None:
                    project_k(nxt)
                    pe.wait_ge(out_ready.sem, out_ready.at(it, 1))
                    project_qv(nxt)

            for piece in head:
                run(piece, None, 0)
            project_k(0)
            project_qv(0)
            with pe.Fori(0, passes - 1) as it:
                first_block(it)
                second_block(it, it + 1)
            first_block(passes - 1)
            second_block(passes - 1, None)

        @block.scalar
        def _(act):
            A = nc.scalar.activation
            act.wait_ge(weights_in, 16 * len(w))
            act.wait_ge(fold_ps, L1)
            for l in range(L1):
                last = A(wv_c[:, l * P:(l + 1) * P], bank[l][:, 0:P], ACT.Copy)
            last.then_inc(set_up, 1)

            def silu0(p, e, m):
                act.wait_ge(up_ps.sem, up_ps.at(p, 2 * e + m + 1))
                A(hf[:, 2 * (e % 2) + m], bank[4 + m][:, :], ACT.Silu).then_inc(hid_ready.sem, 1)

            def run(piece, p, nxt):
                kind, a, c = piece
                if kind == "gate":
                    act.wait_ge(gate1_ps.sem, gate1_ps.at(p, a + 1))
                    if a >= 2:
                        act.wait_ge(hid1_ready.sem, hid1_ready.at(p, a - 1))
                    A(th[:, a % 2], bank[4][:, :], ACT.Silu).then_inc(silu1_ready.sem, 1)
                elif nxt is None:
                    return
                elif kind == "turn0":
                    act.wait_ge(xnT0_ps.sem, xnT0_ps.at(nxt, 1))
                    A(xnT0[:, :], bank[6][:, :], ACT.Copy).then_inc(xnT0_ready.sem, 1)
                elif kind == "up0":
                    silu0(nxt, a, c)
                    if a == 0 and c == 1:
                        act.wait_ge(gap0_ready.sem, gap0_ready.at(nxt, 1))
                        A(gth[:, :], gd[:, :], ACT.Tanh, scale=0.5).then_inc(tanh0_ready.sem, 1)

            def first_block(it):
                for j in range(2):
                    act.wait_ge(qq0_ps.sem, qq0_ps.at(it, j + 1))
                    A(Qg[:, j], bank[1 + 2 * j][:, :], ACT.Identity, bias=W["bias_q"][:, j:j + 1], scale=float(DH0) ** -0.5).then_inc(q_ready.sem, 1)
                act.wait_ge(v_ps.sem, v_ps.at(it, 1))
                A(Vx[:, :, :, 0:DH0], bank[7][:, :].rearrange("p (k h d) -> p k h d", k=NT, h=H0), ACT.Copy).then_inc(v_ready.sem, 1)
                for m in range(2):
                    silu0(it, EARLY, m)

                def copy_o(i):
                    act.wait_ge(pv_ps.sem, pv_ps.at(it, 2 * i + 2))
                    b, q = i // 2, 2 * (i % 2)
                    A(Osb[:, q:q + 2, half(b)], pair_view(bank[3 if q == 0 else 7]), ACT.Copy).then_inc(pv_copied.sem, 1)

                for G in range(NG):
                    for n in range(4 * G, 4 * G + 4):
                        act.wait_ge(cols_ps.sem, cols_ps.at(it, n + 1))
                        if n % 4 == 0 and n >= NPR:
                            act.wait_ge(pv_ps.sem, pv_ps.at(it, G - 1))
                        A(Pr[:, n % NPR], bank[n % 3][:, 0:BLK], ACT.Exp).then_inc(exp_ready.sem, 1)
                    if G in (2, 4, 6):
                        copy_o(G // 2 - 1)
                copy_o(3)
                for m in range(2):
                    silu0(it, E0 - 1, m)

            def second_block(it, nxt):
                def turned_input(b):
                    act.wait_ge(xnT_ps.sem, xnT_ps.at(it, b + 1))
                    A(xnT[:, half(b)], bank[7 - b][:, 0:T], ACT.Copy).then_inc(xnT_ready.sem, 1)

                def fill(l, s):
                    for piece in slot(l, s):
                        run(piece, it, nxt)

                turned_input(0)
                for l in range(L1):
                    def turned(which, b, src):
                        act.wait_ge(lnT_ps.sem, lnT_ps.at(it, (2 * l + which) * NB + b + 1))
                        A(hT[:, half(b)], src[:, 0:T], ACT.Identity, bias=W["ln_b"][:, 0:1], scale=W["ln_s"][:, 0:1]).then_inc(lnT_ready.sem, 1)

                    def values(b):
                        act.wait_ge(v1_ps.sem, v1_ps.at(it, NB * l + b + 1))
                        A(Vr[:, 2 * b:2 * b + 2, :, 0:DH1], bank[7][:, 0:T].rearrange("p (k h d) -> p k h d", k=2, h=H1), ACT.Copy).then_inc(v1_ready.sem, 1)

                    def mask_keys(b):
                        act.wait_ge(k1_sum.sem, k1_sum.at(it, NB * l + b + 1))
                        for h in range(KD, H1):
                            A(Km[:, h, half(b)], Kh[:, half(b)], ACT.Copy, scale=W["head_mask"][:, h:h + 1]).then_inc(k1_act.sem, 1)

                    def gates(b):
                        act.wait_ge(g_ps.sem, g_ps.at(it, NB * l + b + 1))
                        A(Gs[:, :, half(b)], pair_view(A_bank[b]), ACT.Silu).then_inc(g_ready.sem, 1)

                    def scale_gates(b):
                        m = NB * l + b
                        act.wait_ge(g_ready.sem, g_ready.at(it, m + 1))
                        act.wait_ge(q1_ready.sem, q1_ready.at(it, m + 1))
                        act.wait_ge(k1_sum.sem, k1_sum.at(it, m + 1))
                        for j, name in enumerate(("gn_s", "gn_b")):
                            for q in range(2):
                                c = 2 * l + q
                                last = A(qr[:, b, j, q * T:(q + 1) * T], Gs[:, q, half(b)], ACT.Copy, scale=W[name][:, c:c + 1])
                        last.then_inc(g_scaled.sem, 1)

                    def retained(b):
                        act.wait_ge(ret_ps.sem, ret_ps.at(it, 2 * (NB * l + b) + 2))
                        A(sq[:, :, half(b)], pair_view(A_bank[b]), ACT.Square)
                        A(Osb[:, 0:2, half(b)], pair_view(A_bank[b]), ACT.Copy).then_inc(ret_copied.sem, 1)

                    def gelu(b):
                        act.wait_ge(ffh_ps.sem, ffh_ps.at(it, NB * l + b + 1))
                        A(Hh[:, :, half(b)], pair_view(A_bank[b]), ACT.Gelu_apprx_tanh).then_inc(gelu_ready.sem, 1)

                    turned(0, 0, A_bank[0])
                    fill(l, 0)
                    values(0)
                    if l == 0:
                        turned_input(1)
                    turned(0, 1, A_bank[1])
                    fill(l, 1)
                    mask_keys(0)
                    values(1)
                    fill(l, 2)
                    gates(0)
                    mask_keys(1)
                    gates(1)
                    scale_gates(0)
                    scale_gates(1)
                    fill(l, 3)
                    if l == 0:
                        act.wait_ge(gap_ready.sem, gap_ready.at(it, 1))
                        A(gth[:, :], gd[:, :], ACT.Tanh, scale=0.5).then_inc(tanh_ready.sem, 1)
                    fill(l, 4)
                    retained(0)
                    fill(l, 5)
                    retained(1)
                    for s in range(6, 10):
                        fill(l, s)
                    turned(1, 0, B_bank[0])
                    fill(l, 10)
                    gelu(0)
                    turned(1, 1, B_bank[1])
                    gelu(1)
                    fill(l, 11)
                    fill(l, 12)
                    fill(l, 13)

            for piece in head:
                run(piece, None, 0)
            with act.Fori(0, passes - 1) as it:
                first_block(it)
                second_block(it, it + 1)
            first_block(passes - 1)
            second_block(passes - 1, None)

        @block.gpsimd
        def _(pool):
            G = nc.gpsimd
            G.memset(Vx[:], 0.0).then_inc(set_up, 1)
            G.memset(Vr[:], 0.0)
            G.memset(mpad[:], 0.0)
            pool.wait_ge(set_up, 2)
            G.memset(Vx[:, :, :, DH0:DH0 + 1], 1.0).then_inc(set_up, 1)
            pool.wait_ge(weights_in, 16 * len(w))

            def head_roots(p):
                for b in range(NB):
                    k = slice(2 * b, 2 * b + 2)
                    pool.wait_ge(stats0.sem, stats0.at(p, b + 1))
                    G.tensor_tensor(ln_v0[:, k, 0], mv0[:, k, 1], W["eps"][:, 0:2], ALU.add).then_inc(eps0.sem, 1)
                    pool.wait_ge(eps0.sem, eps0.at(p, b + 1))
                    G.tensor_tensor(ln_r0[:, k, 0], ln_v0[:, k, 0], W["minus_half"][:, 0:2], ALU.pow).then_inc(root0.sem, 1)

            def roots(it, n, b):
                k = slice(2 * b, 2 * b + 2)
                pool.wait_ge(ln_stats.sem, ln_stats.at(it, n + 1))
                G.tensor_tensor(ln_v[:, k, 0], mv[:, k, 1], W["eps"][:, 0:2], ALU.add).then_inc(ln_eps.sem, 1)
                pool.wait_ge(ln_eps.sem, ln_eps.at(it, n + 1))
                G.tensor_tensor(ln_r[:, k, 0], ln_v[:, k, 0], W["minus_half"][:, 0:2], ALU.pow).then_inc(ln_root.sem, 1)

            def one_pass(it, nxt):
                for n in range(2 * NB):
                    roots(it, n, n // 2)
                for l in range(L1):
                    for b in range(NB):
                        pool.wait_ge(q1_rot.sem, q1_rot.at(it, NB * l + b + 1))
                        G.tensor_tensor(Qh[:, half(b)], qr[:, b, 0, 0:T], qr[:, b, 0, T:2 * T], ALU.add).then_inc(q1_ready.sem, 1)
                    for b in range(NB):
                        pool.wait_ge(var_read.sem, var_read.at(it, NB * l + b + 1))
                        G.tensor_tensor(rr[:, b], rv[:, b], W["minus_half"][:, :], ALU.pow).then_inc(var_root.sem, 1)
                    for which in range(2):
                        if which and l == HEAD_LAYER and nxt is not None:
                            head_roots(nxt)
                        for b in range(NB):
                            n = NB * (2 + 2 * l + which) + b
                            if n < NLN:
                                roots(it, n, b)

            head_roots(0)
            with pool.Fori(0, passes - 1) as it:
                one_pass(it, it + 1)
            one_pass(passes - 1, None)

        @block.vector
        def _(dve):
            V = nc.vector
            dve.wait_ge(weights_in, 16 * len(w))
            dve.wait_ge(set_up, 3)
            steps = [0, 0]

            def head_link(p, ins):
                steps[0] += 1
                ins.then_inc(head_step.sem, 1)
                dve.wait_ge(head_step.sem, head_step.at(p, steps[0]))

            def body_link(p, ins):
                steps[1] += 1
                ins.then_inc(body_step.sem, 1)
                dve.wait_ge(body_step.sem, body_step.at(p, steps[1]))

            def settle():
                V.memset(settled[:, :], 0.0)

            def statistics(link, p, b, src, st, mv):
                for k in tiles(b):
                    last = V.bn_stats(st[:, k], src[:, k])
                link(p, last)
                settle()
                for k in tiles(b):
                    last = V.bn_aggr(mv[:, k], st[:, k])
                return last

            def scaled(b, src, dst, mv, ln_r):
                for k in tiles(b):
                    last = V.tensor_scalar(dst[:, k], src[:, k], mv[:, k, 0:1], ln_r[:, k], ALU.subtract, ALU.mult)
                return last

            def two_largest(link, p, n, gap):
                settle()
                for k in range(NT):
                    last = V.max(m8[:, k], lg[:, k, 0:n])
                link(p, last)
                settle()
                for k in range(NT):
                    V.max_index(i8[:, k], m8[:, k], lg[:, k, 0:n])
                V.tensor_tensor(gd[:, :], m8[:, :, 0], m8[:, :, 1], ALU.subtract).then_inc(gap.sem, 1)
                dve.wait_ge(gap.sem, gap.at(p, 1))
                link(p, V.tensor_copy(i2[:, :, :], i8[:, :, 0:2]))
                iota = W["iota"][:, :].rearrange("p (k e) -> p k e", k=NT)[:, :, 0:n]
                for j in range(2):
                    last = V.tensor_tensor(ge[:, j, :, 0:n], iota, i2[:, :, j:j + 1].to_broadcast([P, NT, n]), ALU.is_equal)
                link(p, last)

            def weights_of_experts(link, p, n, dst):
                V.tensor_scalar(gw[:, 0], gth[:, :], 0.5, 0.5, ALU.mult, ALU.add)
                link(p, V.tensor_scalar(gw[:, 1], gth[:, :], -0.5, 0.5, ALU.mult, ALU.add))
                for j in range(2):
                    last = V.tensor_tensor(ge[:, j, :, 0:n], ge[:, j, :, 0:n], gw[:, j].unsqueeze(2).to_broadcast([P, NT, n]), ALU.mult)
                link(p, last)
                link(p, V.tensor_tensor(dst[:, :, 0:n], ge[:, 0, :, 0:n], ge[:, 1, :, 0:n], ALU.add))

            def logits_of(n):
                return bank[6][:, 0:NT * 16].rearrange("p (k e) -> p k e", k=NT)[:, :, 0:n]

            def add0(p, e, b, dst):
                dve.wait_ge(down_ps.sem, down_ps.at(p, NB * e + b + 1))
                if e:
                    dve.wait_ge(down_added.sem, down_added.at(p, NB * e + b - 1))
                for k in tiles(b):
                    last = V.scalar_tensor_tensor(dst[:, k], bank[6][:, k * P:(k + 1) * P], comb0[:, k, e:e + 1], acc[:, k], ALU.mult, ALU.add)
                last.then_inc(down_added.sem, 1)

            def head_statistics(p):
                dve.wait_ge(x_loaded.sem, x_loaded.at(p, 16))
                steps[0] = 0
                for b in range(NB):
                    statistics(head_link, p, b, x_in, st0, mv0).then_inc(stats0.sem, 1)

            def head_normalise(p):
                for b in range(NB):
                    dve.wait_ge(stats0.sem, stats0.at(p, b + 1))
                    dve.wait_ge(root0.sem, root0.at(p, b + 1))
                    last = scaled(b, x_in, xn0, mv0, ln_r0)
                last.then_inc(xn0_ready.sem, 1)

            def run(piece, p, nxt):
                kind, a, c = piece
                if kind == "up":
                    dve.wait_ge(silu1_ready.sem, silu1_ready.at(p, a + 1))
                    dve.wait_ge(up1_ps.sem, up1_ps.at(p, a + 1))
                    V.tensor_tensor(hf[:, a % 4], th[:, a % 2], bank[5][:, :], ALU.mult).then_inc(hid1_ready.sem, 1)
                elif kind == "down":
                    dve.wait_ge(down1_ps.sem, down1_ps.at(p, NB * a + c + 1))
                    if a:
                        dve.wait_ge(down1_added.sem, down1_added.at(p, NB * a + c - 1))
                    for k in tiles(c):
                        s = comb[:, k, a:a + 1] if a < E1 else 1.0
                        last = V.scalar_tensor_tensor(x1[:, k], bank[6][:, k * P:(k + 1) * P], s, x1[:, k], ALU.mult, ALU.add)
                    last.then_inc(down1_added.sem, 1)
                elif nxt is None:
                    return
                elif kind == "logits0":
                    dve.wait_ge(logits0_ps.sem, logits0_ps.at(nxt, 1))
                    V.tensor_tensor(lg[:, :, 0:EALL0], logits_of(EALL0), W["bias0"][:, :].rearrange("p (k e) -> p k e", k=NT),
                                    ALU.add).then_inc(logits0_read.sem, 1)
                    dve.wait_ge(logits0_read.sem, logits0_read.at(nxt, 1))
                    two_largest(head_link, nxt, EALL0, gap0_ready)
                elif kind == "up0" and a == 1 and c == 0:
                    dve.wait_ge(tanh0_ready.sem, tanh0_ready.at(nxt, 1))
                    weights_of_experts(head_link, nxt, EALL0, comb0)
                    head_link(nxt, V.tensor_reduce(wz[:, :], comb0[:, :, E0:EALL0], AX.X, ALU.add))
                    for k in range(NT):
                        last = V.scalar_tensor_tensor(acc[:, k], xn0[:, k], wz[:, k:k + 1], x_in[:, k], ALU.mult, ALU.add)
                    last.then_inc(x_used.sem, 1)
                    dve.wait_ge(x_used.sem, x_used.at(nxt, 1))
                elif kind == "down0":
                    add0(nxt, a, c, acc)

            def by_half(t, b):
                return t[:, 2 * b:2 * b + 2].rearrange("p k c -> p (k c)")

            def stats(it, n, b, src):
                statistics(body_link, it, b, src, st, mv).then_inc(ln_stats.sem, 1)

            def normalise(it, n, b, src, dst, ready):
                dve.wait_ge(ln_stats.sem, ln_stats.at(it, n + 1))
                dve.wait_ge(ln_root.sem, ln_root.at(it, n + 1))
                scaled(b, src, dst, mv, ln_r).then_inc(ready.sem, 1)

            def first_block(it):
                steps[1] = 0
                for g in range(2):
                    dve.wait_ge(kk0_ps.sem, kk0_ps.at(it, 1 + g))
                    body_link(it, V.tensor_tensor(Kg[:, g], bank[2 * g][:, :], W["pos_k"][:, :], ALU.add))
                    for h in range(g * HG, (g + 1) * HG):
                        V.tensor_scalar(Km[:, h], Kg[:, g], W["head_mask"][:, h % HG:h % HG + 1], None, ALU.mult).then_inc(k_ready.sem, 1)
                for b in range(NB):
                    for i in range(NP1):
                        n = b * NP1 + i
                        dve.wait_ge(rows_ps.sem, rows_ps.at(it, n + 1))
                        if i == 0 and b:
                            dve.wait_ge(mpadT_ps.sem, mpadT_ps.at(it, b))
                        if i < 4:
                            g, h, cnt, k = i // 2, (i % 2) * 4, 4, 0
                        else:
                            g, h, cnt, k = (i - 4) // 4, ((i - 4) % 4) * 2, 2, 1
                        V.tensor_reduce(mpad[:, k, g, h:h + cnt, RM:RM + 1], bank[n % 3][:, :].rearrange("p (h s) -> p h s", h=cnt),
                                        AX.X, ALU.max).then_inc(rows_max.sem, 1)
                    dve.wait_ge(mpadT_ps.sem, mpadT_ps.at(it, b + 1))
                    for g in range(2):
                        last = V.tensor_tensor(Qg[:, g, half(b)], Qg[:, g, half(b)], bank[7][:, g * T:(g + 1) * T], ALU.subtract)
                    last.then_inc(q_shifted.sem, 1)
                for b in range(NB):
                    add0(it, EARLY, b, acc)

                def invert_sums(b, src):
                    dve.wait_ge(sums_ps.sem, sums_ps.at(it, b + 1))
                    V.reciprocal(rc[:, :], src[:, 0:T]).then_inc(sums_inv.sem, 1)

                def divide(b, banks):
                    for j in range(2):
                        dve.wait_ge(spread_ps.sem, spread_ps.at(it, 2 * b + j + 1))
                        V.tensor_tensor(On[:, 2 * j:2 * j + 2, half(b)], Osb[:, 2 * j:2 * j + 2, half(b)], pair_view(banks[j]), ALU.mult).then_inc(o_ready.sem, 1)

                invert_sums(0, bank[4])
                divide(0, [bank[5], bank[6]])
                dve.wait_ge(y0_ps.sem, y0_ps.at(it, 1))
                dve.wait_ge(down_added.sem, down_added.at(it, NB * (E0 - 1)))
                V.tensor_tensor(by_half(acc, 0), by_half(acc, 0), bank[4][:, 0:T], ALU.add).then_inc(y0_added.sem, 1)
                invert_sums(1, bank[0])
                dve.wait_ge(y0_added.sem, y0_added.at(it, 1))
                add0(it, E0 - 1, 0, x1)
                dve.wait_ge(down_added.sem, down_added.at(it, NB * E0 - 1))
                stats(it, 0, 0, x1)
                divide(1, [bank[1], bank[2]])
                normalise(it, 0, 0, x1, xn, xn_ready)
                dve.wait_ge(xn_ready.sem, xn_ready.at(it, 1))
                stats(it, 1, 0, xn)
                add0(it, E0 - 1, 1, acc)
                normalise(it, 1, 0, xn, xh, ln_ready)
                dve.wait_ge(y0_ps.sem, y0_ps.at(it, 2))
                dve.wait_ge(down_added.sem, down_added.at(it, NB * E0))
                body_link(it, V.tensor_tensor(by_half(x1, 1), by_half(acc, 1), bank[3][:, 0:T], ALU.add))
                stats(it, 2, 1, x1)
                normalise(it, 2, 1, x1, xn, xn_ready)
                dve.wait_ge(xn_ready.sem, xn_ready.at(it, 2))
                stats(it, 3, 1, xn)
                normalise(it, 3, 1, xn, xh, ln_ready)

            def second_block(it, nxt):
                def fill(l, s):
                    for piece in slot(l, s):
                        run(piece, it, nxt)

                for l in range(L1):
                    def rotate(b):
                        m = NB * l + b
                        dve.wait_ge(kk_ps.sem, kk_ps.at(it, m + 1))
                        body_link(it, V.tensor_tensor(qr[:, b, 1], B_bank[b][:, :], W["rope"][:, 2 * T:4 * T], ALU.mult))
                        V.tensor_tensor(Kh[:, half(b)], qr[:, b, 1, 0:T], qr[:, b, 1, T:2 * T], ALU.add).then_inc(k1_sum.sem, 1)
                        dve.wait_ge(qq_ps.sem, qq_ps.at(it, m + 1))
                        V.tensor_tensor(qr[:, b, 0], A_bank[b][:, :], W["rope"][:, 0:2 * T], ALU.mult).then_inc(q1_rot.sem, 1)
                        dve.wait_ge(k1_sum.sem, k1_sum.at(it, m + 1))
                        for h in range(KD):
                            V.tensor_scalar(Km[:, h, half(b)], Kh[:, half(b)], W["head_mask"][:, h:h + 1], None, ALU.mult).then_inc(k1_dve.sem, 1)

                    def causal(b, heads):
                        for h in heads:
                            n = (NB * l + b) * H1 + h
                            dve.wait_ge(att_ps.sem, att_ps.at(it, n + 1))
                            if b and h % 4 == 0:
                                dve.wait_ge(ret_ps.sem, ret_ps.at(it, 2 * NB * l + h // 4 + 1))
                            src = B_bank[b] if h % 2 == 0 else bank[7]
                            V.tensor_tensor(Pr[:, h], src[:, 0:BLK], W["causal"][:, :], ALU.mult).then_inc(att_ready.sem, 1)

                    def read_variances(b):
                        m = NB * l + b
                        dve.wait_ge(var_ps.sem, var_ps.at(it, m + 1))
                        V.tensor_scalar(rv[:, b], B_bank[b][:, 0:16], EPS, None, ALU.add).then_inc(var_read.sem, 1)

                    def widen_roots(b):
                        m = NB * l + b
                        dve.wait_ge(var_root.sem, var_root.at(it, m + 1))
                        V.tensor_copy(rsx[:, b], rr[:, b].unsqueeze(2).to_broadcast([P, 16, 32])).then_inc(roots_wide.sem, 1)

                    def weigh_gates(b):
                        m = NB * l + b
                        dve.wait_ge(g_scaled.sem, g_scaled.at(it, m + 1))
                        dve.wait_ge(ret_copied.sem, ret_copied.at(it, m + 1))
                        V.tensor_tensor(Z[:, :, half(b)], Osb[:, 0:2, half(b)], pair_view(qr[:, b, 0]), ALU.mult).then_inc(z_weighed.sem, 1)

                    def group_norm(b):
                        m = NB * l + b
                        dve.wait_ge(z_weighed.sem, z_weighed.at(it, m + 1))
                        dve.wait_ge(rootsT_ps.sem, rootsT_ps.at(it, m + 1))
                        body_link(it, V.tensor_tensor(Z[:, :, half(b)], Z[:, :, half(b)], pair_view(B_bank[b]), ALU.mult))
                        V.tensor_tensor(Z[:, :, half(b)], Z[:, :, half(b)], pair_view(qr[:, b, 1]), ALU.add).then_inc(z_ready.sem, 1)

                    def add_retention(b):
                        dve.wait_ge(wo_ps.sem, wo_ps.at(it, NB * l + b + 1))
                        body_link(it, V.tensor_tensor(by_half(Yr, b), by_half(xn if l == 0 else X, b), A_bank[b][:, 0:T], ALU.add))
                        stats(it, NB * (2 + 2 * l) + b, b, Yr)

                    def add_ffn(b):
                        if l == 0 and b == 0:
                            dve.wait_ge(out_free.sem, out_free.at(it, 1))
                        dve.wait_ge(w2_ps.sem, w2_ps.at(it, NB * l + b + 1))
                        body_link(it, V.tensor_tensor(by_half(X, b), by_half(Yr, b), B_bank[b][:, 0:T], ALU.add))
                        if l + 1 < L1:
                            stats(it, NB * (3 + 2 * l) + b, b, X)

                    fill(l, 0)
                    rotate(0)
                    fill(l, 1)
                    rotate(1)
                    if l == 0:
                        dve.wait_ge(logits_ps.sem, logits_ps.at(it, 1))
                        V.tensor_copy(lg[:, :, 0:E1], logits_of(E1)).then_inc(logits_read.sem, 1)
                        dve.wait_ge(logits_read.sem, logits_read.at(it, 1))
                        two_largest(body_link, it, E1, gap_ready)
                    fill(l, 2)
                    fill(l, 3)
                    causal(0, range(0, 8))
                    if l == 0:
                        dve.wait_ge(tanh_ready.sem, tanh_ready.at(it, 1))
                        weights_of_experts(body_link, it, E1, comb)
                    fill(l, 4)
                    causal(1, range(0, 6))
                    read_variances(0)
                    causal(1, range(6, 8))
                    weigh_gates(0)
                    fill(l, 5)
                    widen_roots(0)
                    fill(l, 6)
                    read_variances(1)
                    group_norm(0)
                    weigh_gates(1)
                    fill(l, 7)
                    widen_roots(1)
                    add_retention(0)
                    fill(l, 8)
                    group_norm(1)
                    normalise(it, NB * (2 + 2 * l), 0, Yr, xh, ln_ready)
                    fill(l, 9)
                    add_retention(1)
                    fill(l, 10)
                    normalise(it, NB * (2 + 2 * l) + 1, 1, Yr, xh, ln_ready)
                    fill(l, 11)
                    if l == HEAD_LAYER and nxt is not None:
                        head_statistics(nxt)
                    add_ffn(0)
                    fill(l, 12)
                    if l + 1 < L1:
                        normalise(it, NB * (3 + 2 * l), 0, X, xh, ln_ready)
                    add_ffn(1)
                    if l == HEAD_LAYER and nxt is not None:
                        head_normalise(nxt)
                    if l + 1 == L1:
                        dve.wait_ge(down1_added.sem, down1_added.at(it, NB * (E1 + 1)))
                        V.tensor_tensor(X[:].rearrange("p k c -> p (k c)"), x1[:].rearrange("p k c -> p (k c)"),
                                        X[:].rearrange("p k c -> p (k c)"), ALU.add).then_inc(out_ready.sem, 1)
                    fill(l, 13)
                    if l + 1 < L1:
                        normalise(it, NB * (3 + 2 * l) + 1, 1, X, xh, ln_ready)
                assert steps[1] == BODY_STEPS, steps

            head_statistics(0)
            head_normalise(0)
            for piece in head:
                run(piece, None, 0)
            assert steps[0] == HEAD_STEPS, steps
            with dve.Fori(0, passes - 1) as it:
                first_block(it)
                second_block(it, it + 1)
            first_block(passes - 1)
            second_block(passes - 1, None)


def laid_out(a):
    f = np.float32

    def z(*s):
        return np.zeros(s, f)

    w = {}
    wq, wk = z(P, 2, 8, 16), z(P, 2, 8, 16)
    wq[..., 0:8] = a["L0_attn_Wq"].T.reshape(P, 2, 8, 8)
    wk[..., 0:8] = a["L0_attn_Wk"].T.reshape(P, 2, 8, 8)
    w["wq"], w["wk"] = wq, wk
    w["wv"] = a["L0_attn_Wv"].T
    wo = z(4, 32, 4, P)
    wo[:, 0:8] = a["L0_attn_Wo"].T.reshape(4, 4, 8, P).transpose(1, 2, 0, 3)
    w["wo"] = wo
    w["gate0"] = a["L0_ffn_gate_w"].T
    w["bias0"] = np.broadcast_to(a["L0_ffn_expert_bias"][None, None], (P, NT, EALL0))
    w["w1"] = a["L0_ffn_w1"].transpose(2, 0, 1)
    w["w2"] = a["L0_ffn_w2"].reshape(E0, P, 2, P).transpose(3, 0, 2, 1)
    swap = np.arange(P) ^ 1
    for n in ("q", "k"):
        m = a[f"L1_attn_W{n}"].transpose(1, 0, 2)
        w[f"w{n}1"] = m
        w[f"w{n}s1"] = m[:, :, swap]
    w["wvT1"] = a["L1_attn_Wv"].transpose(2, 0, 1)
    wg = z(P, L1, 2, 4, 32)
    wg[..., 0:16] = a["L1_attn_Wg"].transpose(1, 0, 2).reshape(P, L1, 2, 4, 16)
    w["wg1"] = wg
    wo = z(4, 32, L1, 2, P)
    wo[:, 0:16] = a["L1_attn_Wo"].reshape(L1, 2, 4, 16, P).transpose(2, 3, 0, 1, 4)
    w["wo1"] = wo
    w["w11"] = a["L1_attn_W1"].transpose(1, 0, 2)
    w["w21"] = a["L1_attn_W2"].reshape(L1, 2, P, P).transpose(2, 0, 1, 3)
    w["ln_s"] = a["L1_attn_ln_scale"][:, None]
    w["ln_b"] = a["L1_attn_ln_bias"][:, None]
    for n, s in (("gn_s", "scale"), ("gn_b", "bias")):
        g = z(4, 32, L1, 2)
        g[:, 0:16] = a[f"L1_attn_gn_{s}"].reshape(L1, 2, 4, 16).transpose(2, 3, 0, 1)
        w[n] = g
    w["gate1"] = a["L1_ffn_gate_w"].T
    up, half = a["L1_ffn_w_up"], 192
    blocks = []
    for p in range(E1 // 2):
        for e in (2 * p, 2 * p + 1):
            blocks += [up[e, 0:P], up[e, half:half + P]]
        for o in (0, half):
            blocks.append(np.concatenate([up[2 * p, o + P:o + half], up[2 * p + 1, o + P:o + half]]))
    sg, su = a["L1_ffn_sg_gate"], a["L1_ffn_sg_up"]
    blocks += [sg[0:P], su[0:P]]
    blocks += [np.concatenate([s[P:half], z(64, P)]) for s in (sg, su)]
    w["wup"] = np.stack(blocks).transpose(2, 0, 1)
    dn = z(P, E1 + 1, 2, P)
    for e in range(E1 + 1):
        m = (a["L1_ffn_w_down"][e] if e < E1 else a["L1_ffn_sg_down"]).T
        o = 64 * (e % 2) if e < E1 else 0
        dn[:, e, 0] = m[0:P]
        dn[o:o + 64, e, 1] = m[P:half]
    w["wdn"] = dn
    return {n: np.ascontiguousarray(v.reshape(P, -1)) for n, v in w.items()}


def kernel(**inputs):
    import concourse.bacc as bacc
    from concourse.bass_utils import run_bass_kernel_spmd

    a = {n: np.asarray(v) for n, v in inputs.items()}
    shape = a["L0_attn_x"].shape
    arrays = laid_out(a)
    arrays.update(shape_constants())
    nc = bacc.Bacc("TRN2", target_bir_lowering=False, num_devices=1)
    w = {n: nc.dram_tensor("w_" + n, v.shape, mybir.dt.from_np(v.dtype), kind="ExternalInput").ap() for n, v in arrays.items()}
    x = np.ascontiguousarray(a["L0_attn_x"].reshape(-1, D))
    x_dram = nc.dram_tensor("x", x.shape, F32, kind="ExternalInput").ap()
    out = nc.dram_tensor("out", x.shape, F32, kind="ExternalOutput").ap()
    program(nc, x_dram, out, w)
    feed = {"w_" + n: v for n, v in arrays.items()}
    feed["x"] = x
    r = run_bass_kernel_spmd(nc, [feed], core_ids=[0])
    return r.results[0]["out"].reshape(shape)
```

```python
from contextlib import ExitStack

import numpy as np

import concourse.bass as bass
from concourse import mybir

P = 128
F32 = mybir.dt.float32
F32R = mybir.dt.float32r
BF16 = mybir.dt.bfloat16
I32 = mybir.dt.int32
U32 = mybir.dt.uint32
ALU = mybir.AluOpType
ACT = mybir.ActivationFunctionType
AX = mybir.AxisListType

T = 256
NB = 2
TOK = NB * T
NT = TOK // P
D = 128
H0, DH0 = 16, 8
H1, DH1, L1 = 8, 16, 4
HG, HR = 4, 32
RM, RS = 24, 26
SPLITS = [("k", 0), ("k", 1), ("q", 0), ("q", 1), ("k", 2), ("k", 3), ("q", 2), ("q", 3)]
SPLIT_BANK = [0, 2, 1, 3] * 2
E0, EALL0 = 8, 12
E1 = 8
BLK = 384
EPS = 1e-5
BIG = -1e30
EARLY = 5
HEAD_LAYER = 1
HEAD_STEPS = 9
BODY_STEPS = 57


class Sig:

    def __init__(self, sem, per_pass):
        self.sem, self.per_pass = sem, per_pass

    def at(self, it, n):
        return it * self.per_pass + n


def shape_constants():
    def bf16_bits(t):
        return (t.view(np.uint32) >> 16).astype(np.uint16)

    f = np.float32
    p = np.arange(P)
    c = {}
    slopes = np.power(f(2.0), (f(-8.0) * np.arange(1, H0 + 1, dtype=f) / f(H0))).astype(f)
    step = np.exp2(np.floor(np.log2(slopes)) - 10)
    slope_hi = (np.round(slopes / step) * step).astype(f)
    row = p % HR
    c["bias_q"] = np.where(row[:, None] == RS, slope_hi.reshape(4, HG)[:, p // HR].T, f(0)).astype(f)
    c["bias_q"] += np.where(row[:, None] == RS + 1, (slopes - slope_hi).reshape(4, HG)[:, p // HR].T, f(0)).astype(f)
    c["bias_k"] = ((row == RM) | (row == RM + 1)).astype(f)[:, None]
    def factors(high, low, scale=1.0):
        hi, lo = np.isin(row, high), np.isin(row, low)
        return (np.stack([hi * 1.0 - lo, lo * 1.0], 1) * scale).astype(f)
    dim = list(range(DH0))
    c["split_q"] = factors(dim + [16 + d for d in dim], [8 + d for d in dim], f(DH0) ** f(-0.5))
    c["split_k"] = factors(dim + [8 + d for d in dim] + [RS, RS + 1], [16 + d for d in dim])
    c["split_m"] = -factors([RM], [RM + 1])
    pos = np.zeros((P, T), f)
    pos[0] = np.arange(T) - 128.0
    c["pos"] = bf16_bits(pos)
    c["pos_rows"] = bf16_bits(((p[:, None] == 0) & (row[None] >= RS) & (row[None] < RS + 2)).astype(f))
    c["head_mask0"] = (p[:, None] // HR == np.arange(HG)[None]).astype(f)
    c["head_mask"] = (p[:, None] // 16 == np.arange(8)[None]).astype(f)
    c["ident"] = np.eye(P, dtype=f)
    c["ident_bf"] = bf16_bits(np.eye(P, dtype=f))
    later = np.where(p[None] > p[:, None], f(BIG), f(0))
    zero = np.zeros((P, P), f)
    c["mask_q"], c["mask_k"] = bf16_bits(later), bf16_bits(np.ascontiguousarray(later.T))
    c["sum_rows"] = (p[:, None] == 32 * (np.arange(32)[None] % 4) + DH0).astype(f)
    c["spread"] = np.concatenate([(p[:, None] == 32 * q + p[None] // 32) for q in range(4)], 1).astype(f)
    c["minus_half"] = np.full((P, 16), -0.5, f)
    c["eps"] = np.full((P, 2), EPS, f)
    c["mean_sq"] = ((p[:, None] // 32 == np.arange(4)[None]) & (p[:, None] % 32 < DH1)).astype(f) / f(DH1)
    c["centre"] = (np.eye(P) - (p[:, None] // DH1 == p[None] // DH1) / DH1).astype(f)
    keep = (p[None] >= p[:, None]).astype(f)
    c["causal"] = np.concatenate([keep, keep], 1).astype(f)
    c["iota"] = np.tile(np.arange(16, dtype=f)[None, None], (P, NT, 1)).reshape(P, NT * 16)
    gammas = (f(1.0) - np.exp(np.linspace(np.log(1 / 32), np.log(1 / 64), H1)).astype(f)).astype(f)
    log_g = np.log(gammas).astype(f).astype(np.float64)[p // DH1][:, None]
    inv_freq = (f(1.0) / np.power(f(10000.0), np.arange(0, DH1, 2, dtype=f) / f(DH1))).astype(f)
    ang = (np.arange(T, dtype=f)[None] * inv_freq[(p % DH1) // 2][:, None]).astype(f).astype(np.float64)
    sign = np.where(p % 2 == 0, -1.0, 1.0)[:, None]
    n = np.arange(T)[None] - 128.0
    dq, dk = np.exp(n * log_g), np.exp(-n * log_g)
    rope = [np.cos(ang) * dq, np.sin(ang) * sign * dq, np.cos(ang) * dk, -np.sin(ang) * sign * dk]
    c["rope"] = np.concatenate(rope, 1).astype(f)
    return c


def program(nc, x, out, w):
    passes = x.shape[0] // TOK
    with ExitStack() as ctx:
        def sb(name, shape, dt=F32):
            return ctx.enter_context(nc.sbuf_tensor(name, shape, dt))

        sigs = {}

        def sig(name, per_pass):
            sigs[name] = Sig(ctx.enter_context(nc.semaphore(name)), per_pass)
            return sigs[name]

        W = {n: sb("s_" + n, list(a.shape), a.dtype) for n, a in w.items()}
        wv_c = sb("wv_c", [P, L1 * P])
        ident_bf = W["ident_bf"][:, :].bitcast(BF16)

        x_in = sb("x_in", [P, NT, D])
        xn0 = sb("xn0", [P, NT, D])
        xnT0 = sb("xnT0", [P, TOK])
        xn = sb("xn", [P, NT, D])
        xnT = sb("xnT", [P, TOK])
        acc = sb("acc", [P, NT, D])
        settled = sb("settled", [P, 1])
        st0, st = sb("st0", [P, NT, 6]), sb("st", [P, NT, 6])
        mv0, mv = sb("mv0", [P, NT, 2]), sb("mv", [P, NT, 2])
        ln_v0, ln_v = sb("ln_v0", [P, NT, 1]), sb("ln_v", [P, NT, 1])
        ln_r0, ln_r = sb("ln_r0", [P, NT, 1]), sb("ln_r", [P, NT, 1])
        lg = sb("lg", [P, NT, 16])
        m8 = sb("m8", [P, NT, 8])
        i8 = sb("i8", [P, NT, 8], U32)
        i2 = sb("i2", [P, NT, 2])
        gd = sb("gd", [P, NT])
        gth = sb("gth", [P, NT])
        gw = sb("gw", [P, 2, NT])
        ge = sb("ge", [P, 2, NT, 16])
        comb0 = sb("comb0", [P, NT, 16])
        comb = sb("comb", [P, NT, 16])
        wz = sb("wz", [P, NT])
        Qg = sb("Qg", [P, 4, TOK], F32R)
        Kg = sb("Kg", [P, 2, TOK])
        with nc.sbuf_tensor("Kr", [P, H0, TOK], F32R) as Kr:
            pass
        Km = sb("Km", [P, H0, TOK])
        Vx = sb("Vx", [P, NT, H0, 32])
        mx = sb("mx", [P, NB, 2, H0, 1])
        NPR = 8
        Pr = sb("Pr", [P, NPR, BLK])
        Osb = sb("Osb", [P, 4, TOK])
        On = sb("On", [P, 4, TOK])
        rc = sb("rc", [P, T])
        th = sb("th", [P, 2, TOK])
        hf = sb("hf", [P, 4, TOK])
        x1 = sb("x1", [P, NT, D])
        X = sb("X", [P, NT, D])
        Yr = sb("Yr", [P, NT, D])
        xh = sb("xh", [P, NT, D])
        hT = sb("hT", [P, TOK])
        qr = On[:, :, :].rearrange("p (b j) t -> p b j t", b=NB)
        Qh, Kh = Km[:, H1], Km[:, H1 + 1]
        Gs, sq, Hh = (Km[:, H1 + j:H1 + j + 2] for j in (2, 4, 6))
        Z = Osb[:, 2:4]
        Vr = sb("Vr", [P, NT, H1, 32])
        St = sb("St", [P, NB, H1, 32])
        rsx = Kg[:, :, :].rearrange("p b (n c) -> p b n c", c=32)
        rv = sb("rv", [P, NB, 16])
        rr = sb("rr", [P, NB, 16])

        bank = [ctx.enter_context(nc.psum_tensor(f"bank{i}", [P, 512], F32)) for i in range(8)]

        FIRST = ("gate0", "bias0", "iota", "eps", "minus_half", "ident", "wvT1", "centre", "w1", "w2",
                 "wk", "wq", "wv", "pos", "pos_rows")
        first_in = ctx.enter_context(nc.semaphore("first_in"))
        rest_in = ctx.enter_context(nc.semaphore("rest_in"))
        set_up = ctx.enter_context(nc.semaphore("set_up"))
        fold_ps = ctx.enter_context(nc.semaphore("fold_ps"))
        x_loaded = sig("x_loaded", 16)
        x_used = sig("x_used", 1)
        stored = sig("stored", 16)
        out_ready = sig("out_ready", 1)
        out_free = sig("out_free", 1)
        head_step = sig("head_step", HEAD_STEPS)
        body_step = sig("body_step", BODY_STEPS)
        stats0 = sig("stats0", NB)
        eps0 = sig("eps0", NB)
        root0 = sig("root0", NB)
        xn0_ready = sig("xn0_ready", 1)
        xnT0_ps = sig("xnT0_ps", 1)
        xnT0_ready = sig("xnT0_ready", 1)
        logits0_ps = sig("logits0_ps", 1)
        logits0_read = sig("logits0_read", 1)
        gap0_ready = sig("gap0_ready", 1)
        tanh0_ready = sig("tanh0_ready", 1)
        NLN = NB * (1 + 2 * L1)
        ln_stats = sig("ln_stats", NLN)
        ln_eps = sig("ln_eps", NLN)
        ln_root = sig("ln_root", NLN)
        xn_ready = sig("xn_ready", NB)
        xnT_ps = sig("xnT_ps", NB)
        xnT_ready = sig("xnT_ready", NB)
        logits_ps = sig("logits_ps", 1)
        logits_read = sig("logits_read", 1)
        gap_ready = sig("gap_ready", 1)
        tanh_ready = sig("tanh_ready", 1)
        kq0_ps = sig("kq0_ps", len(SPLITS))
        high_ready = sig("high_ready", len(SPLITS))
        split_ready = sig("split_ready", len(SPLITS))
        v_ps = sig("v_ps", 1)
        k_ready = sig("k_ready", H0 - 4)
        k_ready_act = sig("k_ready_act", 4)
        v_ready = sig("v_ready", 1)
        NP1 = 12
        rows_ps = sig("rows_ps", NB * NP1)
        rows_max = sig("rows_max", NB * NP1)
        maxT_ps = sig("maxT_ps", NB)
        max_wide = sig("max_wide", NB)
        max_high = sig("max_high", 2 * NB)
        max_split = sig("max_split", 2 * NB)
        q_shifted = sig("q_shifted", 2 * NB)
        cols_ps = sig("cols_ps", NB * H0)
        exp_ready = sig("exp_ready", NB * H0)
        NG = NB * H0 // 4
        pv_ps = sig("pv_ps", NG)
        pv_copied = sig("pv_copied", NG // 2)
        sums_ps = sig("sums_ps", NB)
        sums_inv = sig("sums_inv", NB)
        spread_ps = sig("spread_ps", 2 * NB)
        o_ready = sig("o_ready", 2 * NB)
        y0_ps = sig("y0_ps", NB)
        y0_added = sig("y0_added", 1)
        up_ps = sig("up_ps", 2 * E0)
        hid_ready = sig("hid_ready", 2 * E0)
        down_ps = sig("down_ps", NB * E0)
        down_added = sig("down_added", NB * E0)
        C1 = 3 * (E1 // 2) + 2
        gate1_ps = sig("gate1_ps", C1)
        up1_ps = sig("up1_ps", C1)
        silu1_ready = sig("silu1_ready", C1)
        hid1_ready = sig("hid1_ready", C1)
        down1_ps = sig("down1_ps", NB * (E1 + 1))
        down1_added = sig("down1_added", NB * (E1 + 1))
        LB = L1 * NB
        ln_ready = sig("ln_ready", 2 * LB)
        lnT_ps = sig("lnT_ps", 2 * LB)
        lnT_ready = sig("lnT_ready", 2 * LB)
        qq_ps = sig("qq_ps", LB)
        kk_ps = sig("kk_ps", LB)
        v1_ps = sig("v1_ps", LB)
        v1_ready = sig("v1_ready", LB)
        q1_rot = sig("q1_rot", LB)
        q1_ready = sig("q1_ready", LB)
        k1_sum = sig("k1_sum", LB)
        KD, KA = 5, 3
        k1_dve = sig("k1_dve", LB * KD)
        k1_act = sig("k1_act", LB * KA)
        keysT_ps = sig("keysT_ps", LB)
        keysT_ready = sig("keysT_ready", LB)
        state_ps = sig("state_ps", LB)
        state_ready = sig("state_ready", LB)
        g_ps = sig("g_ps", LB)
        g_ready = sig("g_ready", LB)
        g_scaled = sig("g_scaled", LB)
        att_ps = sig("att_ps", H1 * LB)
        att_ready = sig("att_ready", H1 * LB)
        ret_ps = sig("ret_ps", 2 * LB)
        ret_copied = sig("ret_copied", LB)
        var_ps = sig("var_ps", LB)
        var_read = sig("var_read", LB)
        var_root = sig("var_root", LB)
        roots_wide = sig("roots_wide", LB)
        rootsT_ps = sig("rootsT_ps", LB)
        z_weighed = sig("z_weighed", LB)
        z_ready = sig("z_ready", LB)
        wo_ps = sig("wo_ps", LB)
        ffh_ps = sig("ffh_ps", LB)
        gelu_ready = sig("gelu_ready", LB)
        w2_ps = sig("w2_ps", LB)

        mx_wide = [On[:, 2 * b:2 * b + 2].rearrange("p n c -> p (n c)") for b in range(NB)]
        MAX_BANK = [(3, 7), (4, 5)]

        pieces = []

        def couple(a, c):
            return [("gate", a, c), ("up", a, c + 1)]

        base = 3 * (E1 // 2)
        for pair in range(E1 // 2):
            if pair == 0:
                pieces += couple(0, 0) + couple(1, 2)
            pieces += couple(3 * pair + 2, 6 * pair + 4)
            for odd in range(2):
                hidden = couple(3 * pair + 3 + odd, 6 * pair + 6 + 2 * odd)
                pieces += [hidden[0], ("down", 2 * pair + odd, 0), hidden[1], ("down", 2 * pair + odd, 1)]
        pieces += [("down", E1, b) for b in range(NB)]
        head = [("turn0", 0, 0), ("logits0", 0, 0), ("up0", 0, 0), ("up0", 0, 1)]
        for e in range(1, EARLY):
            head += [("up0", e, 0), ("down0", e - 1, 0), ("up0", e, 1), ("down0", e - 1, 1)]
        head += [("down0", EARLY - 1, b) for b in range(NB)]
        pieces += head
        plan = [[0, 1, 1, 0, 1, 1, 1, 2, 1, 2, 1, 0, 3, 3],
                [2, 1, 1, 0, 1, 1, 1, 2, 1, 2, 1, 0, 3, 3],
                [2, 1, 1, 0, 1, 1, 1, 2, 1, 2, 1, 0, 3, 3],
                [2, 1, 1, 0, 1, 1, 1, 2, 2, 1, 1, 0, 3, 3]]
        starts = np.cumsum([0] + [n for layer in plan for n in layer]).tolist()

        def slot(l, s):
            i = sum(len(layer) for layer in plan[:l]) + s
            last = l == L1 - 1 and s == len(plan[l]) - 1
            return pieces[starts[i]:len(pieces) if last else starts[i + 1]]

        def down_blocks(e):
            pair, odd = (e // 2, e % 2)
            a = 3 * pair + odd
            b = 3 * pair + 2 if e < E1 else base + 1
            return [(a, 2 * e), (b, 2 * e + 1)]

        A_bank = [bank[0], bank[2]]
        B_bank = [bank[1], bank[3]]

        late = [(-2, "up", EARLY, 0),
                (-2, "up", EARLY, 1),
                (-1, "down", EARLY, 0),
                (2, "up", EARLY + 1, 0),
                (5, "down", EARLY, 1),
                (10, "up", EARLY + 1, 1),
                (12, "down", EARLY + 1, 0),
                (18, "down", EARLY + 1, 1)]

        def late_pieces(n):
            return [piece for at, *piece in late if at == n]

        def item(n):
            b, i = n // NP1, n % NP1
            g, j = i // 3, i % 3
            return (b, 0, g, HG * g, HG) if j == 0 else (b, 1, g, HG * g + 2 * (j - 1), 2)

        def half(b):
            return slice(b * T, (b + 1) * T)

        def tiles(b):
            return range(2 * b, 2 * b + 2)

        def pair_view(t):
            return t[:, 0:TOK].rearrange("p (q t) -> p q t", q=2)

        block = ctx.enter_context(nc.Block())

        @block.sync
        def _(sp):
            for n in w:
                if n in FIRST:
                    sp.dma_start(W[n][:, :], w[n]).then_inc(first_in, 16)

            def load(p):
                sp.dma_start(x_in[:], x[bass.ds(p * TOK, TOK), :].rearrange("(k p) c -> p k c", p=P)).then_inc(x_loaded.sem, 16)

            def store(p):
                sp.wait_ge(out_ready.sem, out_ready.at(p, 1))
                sp.dma_start(out[bass.ds(p * TOK, TOK), :].rearrange("(k p) c -> p k c", p=P), X[:]).then_inc(stored.sem, 16)
                sp.wait_ge(stored.sem, stored.at(p, 16))
                sp.sem_inc(out_free.sem, 1)

            sp.sem_inc(out_free.sem, 1)
            load(0)
            for n in w:
                if n not in FIRST:
                    sp.dma_start(W[n][:, :], w[n]).then_inc(rest_in, 16)
            with sp.Fori(0, passes - 1) as it:
                sp.wait_ge(x_used.sem, x_used.at(it, 1))
                load(it + 1)
                store(it)
            store(passes - 1)

        @block.tensor
        def _(pe):
            mm = nc.tensor.matmul
            pe.wait_ge(first_in, 16 * len(FIRST))
            for l in range(L1):
                mm(bank[l][:, 0:P], W["wvT1"][:, l * P:(l + 1) * P], W["centre"][:, :], start=True, stop=True).then_inc(fold_ps, 1)
            pe.wait_ge(set_up, 3)

            def transposes(dst, col, src, tiles):
                for j, k in enumerate(tiles):
                    last = nc.tensor.transpose(dst[:, col + j * P:col + (j + 1) * P], src[:, k, :], W["ident"][:, :])
                return last

            def by_token(dst, lhs, rhs_blocks, tiles, col=0):
                for i, k in enumerate(tiles):
                    n = len(rhs_blocks)
                    for j in range(n):
                        last = mm(dst[:, col + i * P:col + (i + 1) * P], lhs[j][:, k * P:(k + 1) * P], rhs_blocks[j],
                                  start=(j == 0), stop=(j == n - 1))
                return last

            def four_heads(dst, col, values, probs, first, second, n=T):
                for r in range(4):
                    mm(dst[32 * r:32 * r + 32, col:col + n], values[r][0], probs[r][:, first:first + n], start=True, stop=False, skip_group_check=True)
                for r in range(4):
                    last = mm(dst[32 * r:32 * r + 32, col + P:col + T], values[r][1], probs[r][:, second:second + P], start=False, stop=True,
                              skip_group_check=True)
                return last

            def up0(p, e, m):
                if e:
                    pe.wait_ge(hid_ready.sem, hid_ready.at(p, 2 * e + m - 1))
                c = (2 * e + m) * P
                mm(bank[4 + m][:, :], W["w1"][:, c:c + P], xnT0[:, :], start=True, stop=True).then_inc(up_ps.sem, 1)

            def down0(p, e, b):
                pe.wait_ge(hid_ready.sem, hid_ready.at(p, 2 * e + 2))
                if e or b:
                    pe.wait_ge(down_added.sem, down_added.at(p, NB * e + b))
                else:
                    pe.wait_ge(logits0_read.sem, logits0_read.at(p, 1))
                by_token(bank[6], [hf[:, 2 * (e % 2) + m] for m in range(2)],
                         [W["w2"][:, (2 * e + m) * P:(2 * e + m + 1) * P] for m in range(2)], tiles(b), b * T).then_inc(down_ps.sem, 1)

            def run(piece, p, nxt):
                kind, a, c = piece
                if kind == "gate":
                    if a:
                        pe.wait_ge(silu1_ready.sem, silu1_ready.at(p, a))
                    mm(bank[4][:, :], W["wup"][:, c * P:(c + 1) * P], xnT[:, :], start=True, stop=True).then_inc(gate1_ps.sem, 1)
                elif kind == "up":
                    if a:
                        pe.wait_ge(hid1_ready.sem, hid1_ready.at(p, a))
                    mm(bank[5][:, :], W["wup"][:, c * P:(c + 1) * P], xnT[:, :], start=True, stop=True).then_inc(up1_ps.sem, 1)
                elif kind == "down":
                    blocks = down_blocks(a)
                    pe.wait_ge(hid1_ready.sem, hid1_ready.at(p, blocks[1][0] + 1))
                    if a or c:
                        pe.wait_ge(down1_added.sem, down1_added.at(p, NB * a + c))
                    else:
                        pe.wait_ge(logits_read.sem, logits_read.at(p, 1))
                    by_token(bank[6], [hf[:, j[0] % 4] for j in blocks],
                             [W["wdn"][:, j[1] * P:(j[1] + 1) * P] for j in blocks], tiles(c), c * T).then_inc(down1_ps.sem, 1)
                elif nxt is None:
                    return
                elif kind == "turn0":
                    pe.wait_ge(xn0_ready.sem, xn0_ready.at(nxt, 1))
                    if p is not None:
                        pe.wait_ge(down1_added.sem, down1_added.at(p, NB * (E1 + 1)))
                    transposes(bank[6], 0, xn0, range(NT)).then_inc(xnT0_ps.sem, 1)
                elif kind == "logits0":
                    pe.wait_ge(xnT0_ready.sem, xnT0_ready.at(nxt, 1))
                    for k in range(NT):
                        last = mm(bank[6][:, k * 16:k * 16 + EALL0], xnT0[:, k * P:(k + 1) * P], W["gate0"][:, :], start=True, stop=True)
                    last.then_inc(logits0_ps.sem, 1)
                elif kind == "up0":
                    if a == 0 and p is not None:
                        pe.wait_ge(hid1_ready.sem, hid1_ready.at(p, C1))
                    up0(nxt, a, c)
                else:
                    down0(nxt, a, c)

            def project0(p, parts):
                for j in parts:
                    kind, g = SPLITS[j]
                    if j == 4:
                        for what, e, c in late_pieces(-2):
                            up0(p, e, c)
                    if j >= 4:
                        pe.wait_ge(split_ready.sem, split_ready.at(p, j - 3))
                    dst = bank[SPLIT_BANK[j]]
                    if kind == "k":
                        for b in range(NB):
                            mm(dst[:, half(b)], W["pos_rows"][:, :].bitcast(BF16), W["pos"][:, :].bitcast(BF16), start=(b == 0), stop=False,
                               skip_group_check=True)
                    mm(dst[:, :], W["w" + kind][:, g * P:(g + 1) * P], xnT0[:, :], start=(kind == "q"), stop=True,
                       skip_group_check=True).then_inc(kq0_ps.sem, 1)
                if 7 in parts:
                    by_token(bank[7], [xnT0], [W["wv"][:, :]], range(NT)).then_inc(v_ps.sem, 1)

            def first_block(it):
                def run_late(n):
                    for kind, e, c in late_pieces(n):
                        (up0 if kind == "up" else down0)(it, e, c)

                def turn_maxima(b):
                    pe.wait_ge(max_wide.sem, max_wide.at(it, b + 1))
                    if b == 0:
                        pe.wait_ge(v_ready.sem, v_ready.at(it, 1))
                        pe.wait_ge(split_ready.sem, split_ready.at(it, len(SPLITS)))
                    else:
                        pe.wait_ge(hid_ready.sem, hid_ready.at(it, 2 * (E0 - 1)))
                    for g in range(4):
                        for k in range(2):
                            c = (2 * (g % 2) + k) * P
                            last = nc.tensor.transpose(bank[MAX_BANK[b][g // 2]][:, c:c + P],
                                                       mx_wide[b][:, (4 * k + g) * P:(4 * k + g + 1) * P], W["ident"][:, :])
                    last.then_inc(maxT_ps.sem, 1)

                run_late(-1)
                for n in range(NB * NP1):
                    b, t_tile, g, h, cnt = item(n)
                    if n < NP1:
                        pe.wait_ge(k_ready.sem, k_ready.at(it, (HG - 1) * (g + 1)))
                        pe.wait_ge(k_ready_act.sem, k_ready_act.at(it, g + 1))
                        pe.wait_ge(split_ready.sem, split_ready.at(it, 5 if n == 0 else 7 if g < 3 else 8))
                    if n >= 3:
                        pe.wait_ge(rows_max.sem, rows_max.at(it, n - 2))
                    dst = bank[n % 3][:, :].rearrange("p (h s) -> p h s", h=cnt)
                    width = P * (1 + t_tile)
                    mm(dst, Qg[:, g, b * T + t_tile * P:b * T + (t_tile + 1) * P],
                       Kr[:, h:h + cnt, b * T:b * T + width], start=True, stop=False, skip_group_check=True)
                    mm(dst[:, :, width - P:width], ident_bf, W["mask_q"][:, :].bitcast(BF16).unsqueeze(1).to_broadcast([P, cnt, P]),
                       start=False, stop=True, skip_group_check=True).then_inc(rows_ps.sem, 1)
                    run_late(n)
                    if n == NP1 + 1:
                        turn_maxima(0)

                def weigh(G):
                    b, q = G // 4, G % 4
                    pe.wait_ge(exp_ready.sem, exp_ready.at(it, 4 * G + 4))
                    if G == 0:
                        pe.wait_ge(max_split.sem, max_split.at(it, 2))
                    if b and q % 2 == 0:
                        pe.wait_ge(pv_copied.sem, pv_copied.at(it, 1 + q // 2))
                    heads = range(4 * q, 4 * q + 4)
                    four_heads(bank[3 if q < 2 else 7], (q % 2) * T,
                               [(Vx[:, 2 * b, h, :], Vx[:, 2 * b + 1, h, :]) for h in heads],
                               [Pr[:, h % NPR] for h in heads], P, 0).then_inc(pv_ps.sem, 1)

                def sum_rows(b, dst):
                    pe.wait_ge(pv_copied.sem, pv_copied.at(it, 2 * b + 2))
                    for q in range(4):
                        last = mm(dst[32 * q:32 * q + 32, 0:T], W["sum_rows"][:, :], Osb[:, q, half(b)], start=True, stop=True)
                    last.then_inc(sums_ps.sem, 1)

                def spread(b, banks):
                    pe.wait_ge(sums_inv.sem, sums_inv.at(it, b + 1))
                    for q in range(4):
                        last = mm(banks[q // 2][:, (q % 2) * T:(q % 2 + 1) * T], W["spread"][:, q * P:(q + 1) * P], rc[:, :], start=True, stop=True)
                        if q % 2:
                            last.then_inc(spread_ps.sem, 1)

                def project(b, dst):
                    pe.wait_ge(o_ready.sem, o_ready.at(it, 2 * b + 2))
                    by_token(dst, [On[:, q] for q in range(4)], [W["wo"][:, q * P:(q + 1) * P] for q in range(4)],
                             tiles(b)).then_inc(y0_ps.sem, 1)

                for G in range(NG):
                    for h in range(4 * (G % 4), 4 * (G % 4) + 4):
                        b = G // 4
                        n = b * H0 + h
                        dst = bank[n % 3]
                        if n >= 3:
                            pe.wait_ge(exp_ready.sem, exp_ready.at(it, n - 2))
                        else:
                            pe.wait_ge(rows_max.sem, rows_max.at(it, NB * NP1 - 2 + n))
                        if n % H0 == 0:
                            pe.wait_ge(q_shifted.sem, q_shifted.at(it, 2 * b + 2))
                        for j in range(2):
                            k0 = b * T + (1 - j) * P
                            mm(dst[:, j * T:(j + 1) * T], Kr[:, h, k0:k0 + P], Qg[:, h // HG, half(b)],
                               start=(j == 0), stop=False, skip_group_check=True)
                        mm(dst[:, P:P + T].rearrange("p (k t) -> p k t", k=2), ident_bf,
                           W["mask_k"][:, :].bitcast(BF16).unsqueeze(1).to_broadcast([P, 2, P]), start=False, stop=True,
                           skip_group_check=True).then_inc(cols_ps.sem, 1)
                    if G == 0:
                        turn_maxima(1)
                    else:
                        weigh(G - 1)
                    if G == 1:
                        run_late(NB * NP1)
                    if G == 5:
                        sum_rows(0, bank[4])
                    if G == 6:
                        pe.wait_ge(down_added.sem, down_added.at(it, NB * (E0 - 1)))
                        spread(0, [bank[5], bank[6]])
                    if G == 7:
                        project(0, bank[4])
                weigh(NG - 1)
                pe.wait_ge(y0_added.sem, y0_added.at(it, 1))
                up0(it, E0 - 1, 0)
                up0(it, E0 - 1, 1)
                sum_rows(1, bank[0])
                down0(it, E0 - 1, 0)
                spread(1, [bank[1], bank[2]])
                down0(it, E0 - 1, 1)
                project(1, bank[3])

            def second_block(it, nxt):
                def turn_input(b):
                    pe.wait_ge(xn_ready.sem, xn_ready.at(it, b + 1))
                    transposes(bank[7 - b], 0, xn, tiles(b)).then_inc(xnT_ps.sem, 1)

                def fill(l, s):
                    for piece in slot(l, s):
                        run(piece, it, nxt)

                turn_input(0)
                for l in range(L1):
                    def turn(which, b, dst):
                        n = (2 * l + which) * NB + b + 1
                        pe.wait_ge(ln_ready.sem, ln_ready.at(it, n))
                        transposes(dst, 0, xh, tiles(b)).then_inc(lnT_ps.sem, 1)

                    def project(b):
                        m = NB * l + b
                        pe.wait_ge(lnT_ready.sem, lnT_ready.at(it, 2 * NB * l + b + 1))
                        for j, name in enumerate(("wk1", "wks1")):
                            last = mm(B_bank[b][:, j * T:(j + 1) * T], W[name][:, l * P:(l + 1) * P], hT[:, half(b)], start=True, stop=True)
                        last.then_inc(kk_ps.sem, 1)
                        for j, name in enumerate(("wq1", "wqs1")):
                            last = mm(A_bank[b][:, j * T:(j + 1) * T], W[name][:, l * P:(l + 1) * P], hT[:, half(b)], start=True, stop=True)
                        last.then_inc(qq_ps.sem, 1)
                        if b:
                            pe.wait_ge(v1_ready.sem, v1_ready.at(it, m))
                        elif l == 0:
                            pe.wait_ge(xnT_ready.sem, xnT_ready.at(it, 1))
                        by_token(bank[7], [hT], [wv_c[:, l * P:(l + 1) * P]], tiles(b)).then_inc(v1_ps.sem, 1)

                    def turn_keys(b):
                        pe.wait_ge(k1_sum.sem, k1_sum.at(it, NB * l + b + 1))
                        nc.tensor.transpose(B_bank[b][:, 0:P], Kh[:, b * T:b * T + P], W["ident"][:, :]).then_inc(keysT_ps.sem, 1)

                    def state(b):
                        pe.wait_ge(keysT_ready.sem, keysT_ready.at(it, NB * l + b + 1))
                        pe.wait_ge(v1_ready.sem, v1_ready.at(it, NB * l + b + 1))
                        mm(B_bank[b][:, P:2 * P], xh[:, 2 * b], Vr[:, 2 * b, :, 0:DH1], start=True, stop=True).then_inc(state_ps.sem, 1)

                    def gates(b):
                        m = NB * l + b
                        pe.wait_ge(q1_rot.sem, q1_rot.at(it, m + 1))
                        for q in range(2):
                            last = mm(A_bank[b][:, q * T:(q + 1) * T], W["wg1"][:, (2 * l + q) * P:(2 * l + q + 1) * P], hT[:, half(b)], start=True, stop=True)
                        last.then_inc(g_ps.sem, 1)

                    def scores(b, heads):
                        m = NB * l + b
                        for h in heads:
                            n = m * H1 + h
                            if h == 0:
                                pe.wait_ge(state_ready.sem, state_ready.at(it, m + 1))
                            if h < KD:
                                pe.wait_ge(k1_dve.sem, k1_dve.at(it, m * KD + h + 1))
                            else:
                                pe.wait_ge(k1_act.sem, k1_act.at(it, m * KA + h - KD + 1))
                            if h >= 2 or (b and h == 1):
                                pe.wait_ge(att_ready.sem, att_ready.at(it, n - 1))
                            dst = B_bank[b] if h % 2 == 0 else bank[7]
                            for k in range(2):
                                t = slice(b * T + k * P, b * T + (k + 1) * P)
                                last = mm(dst[:, k * P:(k + 1) * P], Km[:, h, t], Qh[:, t], start=True, stop=True)
                            last.then_inc(att_ps.sem, 1)

                    def retain(b, q):
                        m = NB * l + b
                        pe.wait_ge(att_ready.sem, att_ready.at(it, m * H1 + 4 * q + 4))
                        heads = range(4 * q, 4 * q + 4)
                        four_heads(A_bank[b], q * T, [(Vr[:, 2 * b, h, :], Vr[:, 2 * b + 1, h, :]) for h in heads],
                                   [Pr[:, h] for h in heads], 0, P, n=P)
                        mm(A_bank[b][:, q * T + P:(q + 1) * T], St[:, b, 4 * q:4 * q + 4].rearrange("p h d -> p (h d)"),
                           Qh[:, b * T + P:(b + 1) * T], start=False, stop=True, skip_group_check=True).then_inc(ret_ps.sem, 1)

                    def variances(b):
                        m = NB * l + b
                        pe.wait_ge(ret_copied.sem, ret_copied.at(it, m + 1))
                        for k in range(2):
                            for q in range(2):
                                c = (2 * k + q) * 4
                                last = mm(B_bank[b][:, c:c + 4], sq[:, q, (2 * b + k) * P:(2 * b + k + 1) * P], W["mean_sq"][:, :], start=True, stop=True)
                        last.then_inc(var_ps.sem, 1)

                    def spread_roots(b):
                        m = NB * l + b
                        pe.wait_ge(roots_wide.sem, roots_wide.at(it, m + 1))
                        for q in range(2):
                            for k in range(2):
                                last = nc.tensor.transpose(B_bank[b][:, (2 * q + k) * P:(2 * q + k + 1) * P],
                                                           rsx[:, b, (2 * k + q) * 4:(2 * k + q) * 4 + 4, :].rearrange("p r c -> p (r c)"),
                                                           W["ident"][:, :])
                        last.then_inc(rootsT_ps.sem, 1)

                    def out_project(b):
                        m = NB * l + b
                        pe.wait_ge(z_ready.sem, z_ready.at(it, m + 1))
                        by_token(A_bank[b], [Z[:, q] for q in range(2)],
                                 [W["wo1"][:, (2 * l + q) * P:(2 * l + q + 1) * P] for q in range(2)], tiles(b)).then_inc(wo_ps.sem, 1)

                    def hidden(b):
                        pe.wait_ge(lnT_ready.sem, lnT_ready.at(it, (2 * l + 1) * NB + b + 1))
                        for j in range(2):
                            last = mm(A_bank[b][:, j * T:(j + 1) * T], W["w11"][:, (2 * l + j) * P:(2 * l + j + 1) * P], hT[:, half(b)], start=True, stop=True)
                        last.then_inc(ffh_ps.sem, 1)

                    def last_product(b):
                        pe.wait_ge(gelu_ready.sem, gelu_ready.at(it, NB * l + b + 1))
                        by_token(B_bank[b], [Hh[:, j] for j in range(2)],
                                 [W["w21"][:, (2 * l + j) * P:(2 * l + j + 1) * P] for j in range(2)], tiles(b)).then_inc(w2_ps.sem, 1)

                    turn(0, 0, A_bank[0])
                    fill(l, 0)
                    project(0)
                    if l == 0:
                        turn_input(1)
                        pe.wait_ge(xnT_ready.sem, xnT_ready.at(it, 2))
                        for k in range(NT):
                            last = mm(bank[6][:, k * 16:k * 16 + E1], xnT[:, k * P:(k + 1) * P], W["gate1"][:, :], start=True, stop=True)
                        last.then_inc(logits_ps.sem, 1)
                    turn(0, 1, A_bank[1])
                    fill(l, 1)
                    turn_keys(0)
                    project(1)
                    state(0)
                    fill(l, 2)
                    turn_keys(1)
                    gates(0)
                    gates(1)
                    state(1)
                    pe.wait_ge(v1_ready.sem, v1_ready.at(it, NB * l + NB))
                    pe.wait_ge(q1_ready.sem, q1_ready.at(it, NB * l + 1))
                    fill(l, 3)
                    scores(0, range(0, 6))
                    pe.wait_ge(g_ready.sem, g_ready.at(it, NB * l + 1))
                    retain(0, 0)
                    scores(0, range(6, 8))
                    fill(l, 4)
                    pe.wait_ge(q1_ready.sem, q1_ready.at(it, NB * l + 2))
                    scores(1, range(0, 2))
                    retain(0, 1)
                    scores(1, range(2, 6))
                    variances(0)
                    pe.wait_ge(g_ready.sem, g_ready.at(it, NB * l + 2))
                    retain(1, 0)
                    scores(1, range(6, 8))
                    fill(l, 5)
                    retain(1, 1)
                    fill(l, 6)
                    spread_roots(0)
                    variances(1)
                    fill(l, 7)
                    out_project(0)
                    fill(l, 8)
                    spread_roots(1)
                    fill(l, 9)
                    out_project(1)
                    turn(1, 0, B_bank[0])
                    fill(l, 10)
                    hidden(0)
                    turn(1, 1, B_bank[1])
                    fill(l, 11)
                    last_product(0)
                    hidden(1)
                    fill(l, 12)
                    last_product(1)
                    fill(l, 13)
                if nxt is not None:
                    project0(nxt, range(0, 2))
                    pe.wait_ge(out_ready.sem, out_ready.at(it, 1))
                    project0(nxt, range(2, 8))

            for piece in head:
                run(piece, None, 0)
            pe.wait_ge(rest_in, 16 * (len(w) - len(FIRST)))
            project0(0, range(8))
            with pe.Fori(0, passes - 1) as it:
                first_block(it)
                second_block(it, it + 1)
            first_block(passes - 1)
            second_block(passes - 1, None)

        @block.scalar
        def _(act):
            A = nc.scalar.activation
            act.wait_ge(first_in, 16 * len(FIRST))
            act.wait_ge(fold_ps, L1)
            for l in range(L1):
                last = A(wv_c[:, l * P:(l + 1) * P], bank[l][:, 0:P], ACT.Copy)
            last.then_inc(set_up, 1)

            def silu0(p, e, m):
                act.wait_ge(up_ps.sem, up_ps.at(p, 2 * e + m + 1))
                A(hf[:, 2 * (e % 2) + m], bank[4 + m][:, :], ACT.Silu).then_inc(hid_ready.sem, 1)

            def run(piece, p, nxt):
                kind, a, c = piece
                if kind == "gate":
                    act.wait_ge(gate1_ps.sem, gate1_ps.at(p, a + 1))
                    if a >= 2:
                        act.wait_ge(hid1_ready.sem, hid1_ready.at(p, a - 1))
                    A(th[:, a % 2], bank[4][:, :], ACT.Silu).then_inc(silu1_ready.sem, 1)
                elif nxt is None:
                    return
                elif kind == "turn0":
                    act.wait_ge(xnT0_ps.sem, xnT0_ps.at(nxt, 1))
                    A(xnT0[:, :], bank[6][:, :], ACT.Copy).then_inc(xnT0_ready.sem, 1)
                elif kind == "up0":
                    silu0(nxt, a, c)
                    if a == 0 and c == 1:
                        act.wait_ge(gap0_ready.sem, gap0_ready.at(nxt, 1))
                        A(gth[:, :], gd[:, :], ACT.Tanh, scale=0.5).then_inc(tanh0_ready.sem, 1)

            def first_block(it):
                def silu_late(parts):
                    for n in parts:
                        for kind, e, c in late_pieces(n):
                            if kind == "up":
                                silu0(it, e, c)

                for j in range(len(SPLITS)):
                    kind, g = SPLITS[j]
                    if j == 4:
                        silu_late([-2])
                    act.wait_ge(kq0_ps.sem, kq0_ps.at(it, j + 1))
                    if j >= 2:
                        act.wait_ge(split_ready.sem, split_ready.at(it, j - 1))
                    bias = W["bias_q"][:, g:g + 1] if kind == "q" else W["bias_k"][:, 0:1]
                    A(th[:, j % 2].bitcast(F32R), bank[SPLIT_BANK[j]][:, :], ACT.Identity, bias=bias,
                      scale=W["split_" + kind][:, 0:1]).then_inc(high_ready.sem, 1)
                    if j in (2, 3, 6, 7):
                        act.wait_ge(split_ready.sem, split_ready.at(it, j - 1))
                        g = SPLITS[j - 2][1]
                        A(Kr[:, HG * g + HG - 1], Kg[:, g % 2].bitcast(F32R), ACT.Copy,
                          scale=W["head_mask0"][:, HG - 1:HG]).then_inc(k_ready_act.sem, 1)
                act.wait_ge(v_ps.sem, v_ps.at(it, 1))
                A(Vx[:, :, :, 0:DH0], bank[7][:, :].rearrange("p (k h d) -> p k h d", k=NT, h=H0), ACT.Copy).then_inc(v_ready.sem, 1)

                def max_highs(b):
                    act.wait_ge(maxT_ps.sem, maxT_ps.at(it, b + 1))
                    for j in range(2):
                        if b == 0:
                            act.wait_ge(split_ready.sem, split_ready.at(it, 7 + j))
                        else:
                            act.wait_ge(q_shifted.sem, q_shifted.at(it, j + 1))
                        A(th[:, j].bitcast(F32R), bank[MAX_BANK[b][j]][:, :], ACT.Copy, scale=W["split_m"][:, 0:1]).then_inc(max_high.sem, 1)

                silu_late(range(-1, NP1 + 1 + 1))
                max_highs(0)
                silu_late(range(NP1 + 1 + 1, NB * NP1))

                def copy_o(i):
                    act.wait_ge(pv_ps.sem, pv_ps.at(it, 2 * i + 2))
                    b, q = i // 2, 2 * (i % 2)
                    A(Osb[:, q:q + 2, half(b)], pair_view(bank[3 if q == 0 else 7]), ACT.Copy).then_inc(pv_copied.sem, 1)

                for G in range(NG):
                    for n in range(4 * G, 4 * G + 4):
                        act.wait_ge(cols_ps.sem, cols_ps.at(it, n + 1))
                        if n % 4 == 0 and n >= NPR:
                            act.wait_ge(pv_ps.sem, pv_ps.at(it, G - 1))
                        A(Pr[:, n % NPR], bank[n % 3][:, P:P + BLK], ACT.Exp).then_inc(exp_ready.sem, 1)
                    if G == 0:
                        max_highs(1)
                    if G in (2, 4, 6):
                        copy_o(G // 2 - 1)
                copy_o(3)
                for m in range(2):
                    silu0(it, E0 - 1, m)

            def second_block(it, nxt):
                def turned_input(b):
                    act.wait_ge(xnT_ps.sem, xnT_ps.at(it, b + 1))
                    A(xnT[:, half(b)], bank[7 - b][:, 0:T], ACT.Copy).then_inc(xnT_ready.sem, 1)

                def fill(l, s):
                    for piece in slot(l, s):
                        run(piece, it, nxt)

                turned_input(0)
                for l in range(L1):
                    def turned(which, b, src):
                        act.wait_ge(lnT_ps.sem, lnT_ps.at(it, (2 * l + which) * NB + b + 1))
                        A(hT[:, half(b)], src[:, 0:T], ACT.Identity, bias=W["ln_b"][:, 0:1], scale=W["ln_s"][:, 0:1]).then_inc(lnT_ready.sem, 1)

                    def values(b):
                        act.wait_ge(v1_ps.sem, v1_ps.at(it, NB * l + b + 1))
                        A(Vr[:, 2 * b:2 * b + 2, :, 0:DH1], bank[7][:, 0:T].rearrange("p (k h d) -> p k h d", k=2, h=H1), ACT.Copy).then_inc(v1_ready.sem, 1)

                    def copy_keys(b):
                        act.wait_ge(keysT_ps.sem, keysT_ps.at(it, NB * l + b + 1))
                        A(xh[:, 2 * b], B_bank[b][:, 0:P], ACT.Copy).then_inc(keysT_ready.sem, 1)

                    def mask_keys(b):
                        act.wait_ge(k1_sum.sem, k1_sum.at(it, NB * l + b + 1))
                        for h in range(KD, H1):
                            A(Km[:, h, half(b)], Kh[:, half(b)], ACT.Copy, scale=W["head_mask"][:, h:h + 1]).then_inc(k1_act.sem, 1)

                    def gates(b):
                        act.wait_ge(g_ps.sem, g_ps.at(it, NB * l + b + 1))
                        A(Gs[:, :, half(b)], pair_view(A_bank[b]), ACT.Silu).then_inc(g_ready.sem, 1)

                    def scale_gates(b):
                        m = NB * l + b
                        act.wait_ge(g_ready.sem, g_ready.at(it, m + 1))
                        act.wait_ge(q1_ready.sem, q1_ready.at(it, m + 1))
                        act.wait_ge(k1_sum.sem, k1_sum.at(it, m + 1))
                        for j, name in enumerate(("gn_s", "gn_b")):
                            for q in range(2):
                                c = 2 * l + q
                                last = A(qr[:, b, j, q * T:(q + 1) * T], Gs[:, q, half(b)], ACT.Copy, scale=W[name][:, c:c + 1])
                        last.then_inc(g_scaled.sem, 1)

                    def retained(b):
                        act.wait_ge(ret_ps.sem, ret_ps.at(it, 2 * (NB * l + b) + 2))
                        A(sq[:, :, half(b)], pair_view(A_bank[b]), ACT.Square)
                        A(Osb[:, 0:2, half(b)], pair_view(A_bank[b]), ACT.Copy).then_inc(ret_copied.sem, 1)

                    def gelu(b):
                        act.wait_ge(ffh_ps.sem, ffh_ps.at(it, NB * l + b + 1))
                        A(Hh[:, :, half(b)], pair_view(A_bank[b]), ACT.Gelu_apprx_tanh).then_inc(gelu_ready.sem, 1)

                    turned(0, 0, A_bank[0])
                    fill(l, 0)
                    values(0)
                    if l == 0:
                        turned_input(1)
                    turned(0, 1, A_bank[1])
                    fill(l, 1)
                    copy_keys(0)
                    mask_keys(0)
                    values(1)
                    fill(l, 2)
                    copy_keys(1)
                    gates(0)
                    mask_keys(1)
                    gates(1)
                    scale_gates(0)
                    scale_gates(1)
                    fill(l, 3)
                    if l == 0:
                        act.wait_ge(gap_ready.sem, gap_ready.at(it, 1))
                        A(gth[:, :], gd[:, :], ACT.Tanh, scale=0.5).then_inc(tanh_ready.sem, 1)
                    fill(l, 4)
                    retained(0)
                    fill(l, 5)
                    retained(1)
                    for s in range(6, 10):
                        fill(l, s)
                    turned(1, 0, B_bank[0])
                    fill(l, 10)
                    gelu(0)
                    turned(1, 1, B_bank[1])
                    gelu(1)
                    fill(l, 11)
                    fill(l, 12)
                    fill(l, 13)

            for piece in head:
                run(piece, None, 0)
            act.wait_ge(rest_in, 16 * (len(w) - len(FIRST)))
            with act.Fori(0, passes - 1) as it:
                first_block(it)
                second_block(it, it + 1)
            first_block(passes - 1)
            second_block(passes - 1, None)

        @block.gpsimd
        def _(pool):
            G = nc.gpsimd
            G.memset(Vx[:], 0.0).then_inc(set_up, 1)
            G.memset(Vr[:], 0.0)
            G.memset(St[:], 0.0)
            pool.wait_ge(set_up, 2)
            G.memset(Vx[:, :, :, DH0:DH0 + 1], 1.0).then_inc(set_up, 1)
            pool.wait_ge(first_in, 16 * len(FIRST))

            def head_roots(p):
                for b in range(NB):
                    pool.wait_ge(stats0.sem, stats0.at(p, b + 1))
                    k = slice(2 * b, 2 * b + 2)
                    G.tensor_tensor(ln_v0[:, k, 0], mv0[:, k, 1], W["eps"][:, 0:2], ALU.add).then_inc(eps0.sem, 1)
                    pool.wait_ge(eps0.sem, eps0.at(p, b + 1))
                    G.tensor_tensor(ln_r0[:, k, 0], ln_v0[:, k, 0], W["minus_half"][:, 0:2], ALU.pow).then_inc(root0.sem, 1)

            def roots(it, n, b):
                pool.wait_ge(ln_stats.sem, ln_stats.at(it, n + 1))
                k = slice(2 * b, 2 * b + 2)
                G.tensor_tensor(ln_v[:, k, 0], mv[:, k, 1], W["eps"][:, 0:2], ALU.add).then_inc(ln_eps.sem, 1)
                pool.wait_ge(ln_eps.sem, ln_eps.at(it, n + 1))
                G.tensor_tensor(ln_r[:, k, 0], ln_v[:, k, 0], W["minus_half"][:, 0:2], ALU.pow).then_inc(ln_root.sem, 1)

            def one_pass(it, nxt):
                for b in range(NB):
                    for j in range(2):
                        pool.wait_ge(max_split.sem, max_split.at(it, 2 * b + j + 1))
                        q = Qg[:, 2 * j:2 * j + 2, half(b)]
                        G.tensor_tensor(q, q, pair_view(th[:, j]).bitcast(F32R), ALU.add).then_inc(q_shifted.sem, 1)
                for n in range(2 * NB):
                    roots(it, n, n // 2)
                for l in range(L1):
                    for b in range(NB):
                        pool.wait_ge(q1_rot.sem, q1_rot.at(it, NB * l + b + 1))
                        G.tensor_tensor(Qh[:, half(b)], qr[:, b, 0, 0:T], qr[:, b, 0, T:2 * T], ALU.add).then_inc(q1_ready.sem, 1)
                    for b in range(NB):
                        pool.wait_ge(var_read.sem, var_read.at(it, NB * l + b + 1))
                        G.tensor_tensor(rr[:, b], rv[:, b], W["minus_half"][:, :], ALU.pow).then_inc(var_root.sem, 1)
                    for which in range(2):
                        if which and l == HEAD_LAYER and nxt is not None:
                            head_roots(nxt)
                        for b in range(NB):
                            n = NB * (2 + 2 * l + which) + b
                            if n < NLN:
                                roots(it, n, b)

            head_roots(0)
            pool.wait_ge(rest_in, 16 * (len(w) - len(FIRST)))
            with pool.Fori(0, passes - 1) as it:
                one_pass(it, it + 1)
            one_pass(passes - 1, None)

        @block.vector
        def _(dve):
            V = nc.vector
            dve.wait_ge(first_in, 16 * len(FIRST))
            dve.wait_ge(set_up, 3)
            steps = [0, 0]

            def head_link(p, ins):
                steps[0] += 1
                ins.then_inc(head_step.sem, 1)
                dve.wait_ge(head_step.sem, head_step.at(p, steps[0]))

            def body_link(p, ins):
                steps[1] += 1
                ins.then_inc(body_step.sem, 1)
                dve.wait_ge(body_step.sem, body_step.at(p, steps[1]))

            def settle():
                V.memset(settled[:, :], 0.0)

            def statistics(link, p, b, src, st, mv):
                for k in tiles(b):
                    last = V.bn_stats(st[:, k], src[:, k])
                link(p, last)
                settle()
                for k in tiles(b):
                    last = V.bn_aggr(mv[:, k], st[:, k])
                return last

            def scaled(b, src, dst, mv, ln_r):
                for k in tiles(b):
                    last = V.tensor_scalar(dst[:, k], src[:, k], mv[:, k, 0:1], ln_r[:, k], ALU.subtract, ALU.mult)
                return last

            def two_largest(link, p, n, gap):
                settle()
                for k in range(NT):
                    last = V.max(m8[:, k], lg[:, k, 0:n])
                link(p, last)
                settle()
                for k in range(NT):
                    V.max_index(i8[:, k], m8[:, k], lg[:, k, 0:n])
                V.tensor_tensor(gd[:, :], m8[:, :, 0], m8[:, :, 1], ALU.subtract).then_inc(gap.sem, 1)
                dve.wait_ge(gap.sem, gap.at(p, 1))
                link(p, V.tensor_copy(i2[:, :, :], i8[:, :, 0:2]))
                iota = W["iota"][:, :].rearrange("p (k e) -> p k e", k=NT)[:, :, 0:n]
                for j in range(2):
                    last = V.tensor_tensor(ge[:, j, :, 0:n], iota, i2[:, :, j:j + 1].to_broadcast([P, NT, n]), ALU.is_equal)
                link(p, last)

            def weights_of_experts(link, p, n, dst):
                V.tensor_scalar(gw[:, 0], gth[:, :], 0.5, 0.5, ALU.mult, ALU.add)
                link(p, V.tensor_scalar(gw[:, 1], gth[:, :], -0.5, 0.5, ALU.mult, ALU.add))
                for j in range(2):
                    last = V.tensor_tensor(ge[:, j, :, 0:n], ge[:, j, :, 0:n], gw[:, j].unsqueeze(2).to_broadcast([P, NT, n]), ALU.mult)
                link(p, last)
                link(p, V.tensor_tensor(dst[:, :, 0:n], ge[:, 0, :, 0:n], ge[:, 1, :, 0:n], ALU.add))

            def logits_of(n):
                return bank[6][:, 0:NT * 16].rearrange("p (k e) -> p k e", k=NT)[:, :, 0:n]

            def add0(p, e, b, dst):
                dve.wait_ge(down_ps.sem, down_ps.at(p, NB * e + b + 1))
                if e:
                    dve.wait_ge(down_added.sem, down_added.at(p, NB * e + b - 1))
                for k in tiles(b):
                    last = V.scalar_tensor_tensor(dst[:, k], bank[6][:, k * P:(k + 1) * P], comb0[:, k, e:e + 1], acc[:, k], ALU.mult, ALU.add)
                last.then_inc(down_added.sem, 1)

            def head_statistics(p):
                dve.wait_ge(x_loaded.sem, x_loaded.at(p, 16))
                steps[0] = 0
                for b in range(NB):
                    statistics(head_link, p, b, x_in, st0, mv0).then_inc(stats0.sem, 1)

            def head_normalise(p):
                for b in range(NB):
                    dve.wait_ge(stats0.sem, stats0.at(p, b + 1))
                    dve.wait_ge(root0.sem, root0.at(p, b + 1))
                    last = scaled(b, x_in, xn0, mv0, ln_r0)
                last.then_inc(xn0_ready.sem, 1)

            def run(piece, p, nxt):
                kind, a, c = piece
                if kind == "up":
                    dve.wait_ge(silu1_ready.sem, silu1_ready.at(p, a + 1))
                    dve.wait_ge(up1_ps.sem, up1_ps.at(p, a + 1))
                    V.tensor_tensor(hf[:, a % 4], th[:, a % 2], bank[5][:, :], ALU.mult).then_inc(hid1_ready.sem, 1)
                elif kind == "down":
                    dve.wait_ge(down1_ps.sem, down1_ps.at(p, NB * a + c + 1))
                    if a:
                        dve.wait_ge(down1_added.sem, down1_added.at(p, NB * a + c - 1))
                    for k in tiles(c):
                        s = comb[:, k, a:a + 1] if a < E1 else 1.0
                        last = V.scalar_tensor_tensor(x1[:, k], bank[6][:, k * P:(k + 1) * P], s, x1[:, k], ALU.mult, ALU.add)
                    last.then_inc(down1_added.sem, 1)
                elif nxt is None:
                    return
                elif kind == "logits0":
                    dve.wait_ge(logits0_ps.sem, logits0_ps.at(nxt, 1))
                    V.tensor_tensor(lg[:, :, 0:EALL0], logits_of(EALL0), W["bias0"][:, :].rearrange("p (k e) -> p k e", k=NT),
                                    ALU.add).then_inc(logits0_read.sem, 1)
                    dve.wait_ge(logits0_read.sem, logits0_read.at(nxt, 1))
                    two_largest(head_link, nxt, EALL0, gap0_ready)
                elif kind == "up0" and a == 1 and c == 0:
                    dve.wait_ge(tanh0_ready.sem, tanh0_ready.at(nxt, 1))
                    weights_of_experts(head_link, nxt, EALL0, comb0)
                    head_link(nxt, V.tensor_reduce(wz[:, :], comb0[:, :, E0:EALL0], AX.X, ALU.add))
                    for k in range(NT):
                        last = V.scalar_tensor_tensor(acc[:, k], xn0[:, k], wz[:, k:k + 1], x_in[:, k], ALU.mult, ALU.add)
                    last.then_inc(x_used.sem, 1)
                    dve.wait_ge(x_used.sem, x_used.at(nxt, 1))
                elif kind == "down0":
                    add0(nxt, a, c, acc)

            def by_half(t, b):
                return t[:, 2 * b:2 * b + 2].rearrange("p k c -> p (k c)")

            def stats(it, n, b, src):
                statistics(body_link, it, b, src, st, mv).then_inc(ln_stats.sem, 1)

            def normalise(it, n, b, src, dst, ready):
                dve.wait_ge(ln_stats.sem, ln_stats.at(it, n + 1))
                dve.wait_ge(ln_root.sem, ln_root.at(it, n + 1))
                scaled(b, src, dst, mv, ln_r).then_inc(ready.sem, 1)

            def first_block(it):
                steps[1] = 0
                for j in range(len(SPLITS)):
                    kind, g = SPLITS[j]
                    dst = Kg[:, g % 2].bitcast(F32R) if kind == "k" else Qg[:, g]
                    dve.wait_ge(high_ready.sem, high_ready.at(it, j + 1))
                    if kind == "k" and g >= 2:
                        dve.wait_ge(k_ready_act.sem, k_ready_act.at(it, g - 1))
                    V.scalar_tensor_tensor(dst, bank[SPLIT_BANK[j]][:, :], W["split_" + kind][:, 1:2],
                                           th[:, j % 2].bitcast(F32R), ALU.mult, ALU.add).then_inc(split_ready.sem, 1)
                    if kind == "k":
                        dve.wait_ge(split_ready.sem, split_ready.at(it, j + 1))
                        for h in range(g * HG, (g + 1) * HG - 1):
                            V.tensor_scalar(Kr[:, h], dst, W["head_mask0"][:, h % HG:h % HG + 1], None,
                                            ALU.mult).then_inc(k_ready.sem, 1)

                def add_late(n):
                    for kind, e, c in late_pieces(n):
                        if kind == "down":
                            add0(it, e, c, acc)

                def split_max(b):
                    for j in range(2):
                        dve.wait_ge(max_high.sem, max_high.at(it, 2 * b + j + 1))
                        V.scalar_tensor_tensor(th[:, j].bitcast(F32R), bank[MAX_BANK[b][j]][:, :], W["split_m"][:, 1:2],
                                               th[:, j].bitcast(F32R), ALU.mult, ALU.add).then_inc(max_split.sem, 1)

                add_late(-1)
                for n in range(NB * NP1):
                    b, k, g, h, cnt = item(n)
                    dve.wait_ge(rows_ps.sem, rows_ps.at(it, n + 1))
                    V.tensor_reduce(mx[:, b, k, h:h + cnt], bank[n % 3][:, :].rearrange("p (h s) -> p h s", h=cnt),
                                    AX.X, ALU.max).then_inc(rows_max.sem, 1)
                    if n % NP1 == NP1 - 1:
                        dve.wait_ge(rows_max.sem, rows_max.at(it, n + 1))
                        V.tensor_copy(mx_wide[b].rearrange("p (h r) -> p h r", r=HR), mx[:, b].rearrange("p k h r -> p (k h) r").to_broadcast([P, 2 * H0, HR])).then_inc(max_wide.sem, 1)
                    if n:
                        add_late(n - 1)
                    if n == NP1 + 1 + 3:
                        split_max(0)
                add_late(NB * NP1 - 1)
                split_max(1)
                add_late(NB * NP1)

                def invert_sums(b, src):
                    dve.wait_ge(sums_ps.sem, sums_ps.at(it, b + 1))
                    V.reciprocal(rc[:, :], src[:, 0:T]).then_inc(sums_inv.sem, 1)

                def divide(b, banks):
                    for j in range(2):
                        dve.wait_ge(spread_ps.sem, spread_ps.at(it, 2 * b + j + 1))
                        V.tensor_tensor(On[:, 2 * j:2 * j + 2, half(b)], Osb[:, 2 * j:2 * j + 2, half(b)], pair_view(banks[j]), ALU.mult).then_inc(o_ready.sem, 1)

                invert_sums(0, bank[4])
                divide(0, [bank[5], bank[6]])
                dve.wait_ge(y0_ps.sem, y0_ps.at(it, 1))
                dve.wait_ge(down_added.sem, down_added.at(it, NB * (E0 - 1)))
                V.tensor_tensor(by_half(acc, 0), by_half(acc, 0), bank[4][:, 0:T], ALU.add).then_inc(y0_added.sem, 1)
                invert_sums(1, bank[0])
                dve.wait_ge(y0_added.sem, y0_added.at(it, 1))
                add0(it, E0 - 1, 0, x1)
                dve.wait_ge(down_added.sem, down_added.at(it, NB * E0 - 1))
                stats(it, 0, 0, x1)
                divide(1, [bank[1], bank[2]])
                normalise(it, 0, 0, x1, xn, xn_ready)
                dve.wait_ge(xn_ready.sem, xn_ready.at(it, 1))
                stats(it, 1, 0, xn)
                add0(it, E0 - 1, 1, acc)
                normalise(it, 1, 0, xn, xh, ln_ready)
                dve.wait_ge(y0_ps.sem, y0_ps.at(it, 2))
                dve.wait_ge(down_added.sem, down_added.at(it, NB * E0))
                body_link(it, V.tensor_tensor(by_half(x1, 1), by_half(acc, 1), bank[3][:, 0:T], ALU.add))
                stats(it, 2, 1, x1)
                normalise(it, 2, 1, x1, xn, xn_ready)
                dve.wait_ge(xn_ready.sem, xn_ready.at(it, 2))
                stats(it, 3, 1, xn)
                normalise(it, 3, 1, xn, xh, ln_ready)

            def second_block(it, nxt):
                def fill(l, s):
                    for piece in slot(l, s):
                        run(piece, it, nxt)

                for l in range(L1):
                    def rotate(b):
                        m = NB * l + b
                        dve.wait_ge(kk_ps.sem, kk_ps.at(it, m + 1))
                        body_link(it, V.tensor_tensor(qr[:, b, 1], B_bank[b][:, :], W["rope"][:, 2 * T:4 * T], ALU.mult))
                        V.tensor_tensor(Kh[:, half(b)], qr[:, b, 1, 0:T], qr[:, b, 1, T:2 * T], ALU.add).then_inc(k1_sum.sem, 1)
                        dve.wait_ge(qq_ps.sem, qq_ps.at(it, m + 1))
                        V.tensor_tensor(qr[:, b, 0], A_bank[b][:, :], W["rope"][:, 0:2 * T], ALU.mult).then_inc(q1_rot.sem, 1)
                        dve.wait_ge(k1_sum.sem, k1_sum.at(it, m + 1))
                        for h in range(KD):
                            V.tensor_scalar(Km[:, h, half(b)], Kh[:, half(b)], W["head_mask"][:, h:h + 1], None, ALU.mult).then_inc(k1_dve.sem, 1)

                    def mask_state(b):
                        dve.wait_ge(state_ps.sem, state_ps.at(it, NB * l + b + 1))
                        V.tensor_tensor(St[:, b, :, 0:DH1], B_bank[b][:, P:2 * P].rearrange("p (h d) -> p h d", h=H1),
                                        W["head_mask"][:, :].unsqueeze(2).to_broadcast([P, H1, DH1]), ALU.mult).then_inc(state_ready.sem, 1)

                    def causal(b, heads):
                        for h in heads:
                            n = (NB * l + b) * H1 + h
                            dve.wait_ge(att_ps.sem, att_ps.at(it, n + 1))
                            if b and h % 4 == 0:
                                dve.wait_ge(ret_ps.sem, ret_ps.at(it, 2 * NB * l + h // 4 + 1))
                            src = B_bank[b] if h % 2 == 0 else bank[7]
                            V.tensor_tensor(Pr[:, h, 0:2 * P], src[:, 0:2 * P], W["causal"][:, :], ALU.mult).then_inc(att_ready.sem, 1)

                    def read_variances(b):
                        m = NB * l + b
                        dve.wait_ge(var_ps.sem, var_ps.at(it, m + 1))
                        V.tensor_scalar(rv[:, b], B_bank[b][:, 0:16], EPS, None, ALU.add).then_inc(var_read.sem, 1)

                    def widen_roots(b):
                        m = NB * l + b
                        dve.wait_ge(var_root.sem, var_root.at(it, m + 1))
                        V.tensor_copy(rsx[:, b], rr[:, b].unsqueeze(2).to_broadcast([P, 16, 32])).then_inc(roots_wide.sem, 1)

                    def weigh_gates(b):
                        m = NB * l + b
                        dve.wait_ge(g_scaled.sem, g_scaled.at(it, m + 1))
                        dve.wait_ge(ret_copied.sem, ret_copied.at(it, m + 1))
                        V.tensor_tensor(Z[:, :, half(b)], Osb[:, 0:2, half(b)], pair_view(qr[:, b, 0]), ALU.mult).then_inc(z_weighed.sem, 1)

                    def group_norm(b):
                        m = NB * l + b
                        dve.wait_ge(z_weighed.sem, z_weighed.at(it, m + 1))
                        dve.wait_ge(rootsT_ps.sem, rootsT_ps.at(it, m + 1))
                        body_link(it, V.tensor_tensor(Z[:, :, half(b)], Z[:, :, half(b)], pair_view(B_bank[b]), ALU.mult))
                        V.tensor_tensor(Z[:, :, half(b)], Z[:, :, half(b)], pair_view(qr[:, b, 1]), ALU.add).then_inc(z_ready.sem, 1)

                    def add_retention(b):
                        dve.wait_ge(wo_ps.sem, wo_ps.at(it, NB * l + b + 1))
                        body_link(it, V.tensor_tensor(by_half(Yr, b), by_half(xn if l == 0 else X, b), A_bank[b][:, 0:T], ALU.add))
                        stats(it, NB * (2 + 2 * l) + b, b, Yr)

                    def add_ffn(b):
                        if l == 0 and b == 0:
                            dve.wait_ge(out_free.sem, out_free.at(it, 1))
                        dve.wait_ge(w2_ps.sem, w2_ps.at(it, NB * l + b + 1))
                        body_link(it, V.tensor_tensor(by_half(X, b), by_half(Yr, b), B_bank[b][:, 0:T], ALU.add))
                        if l + 1 < L1:
                            stats(it, NB * (3 + 2 * l) + b, b, X)

                    fill(l, 0)
                    rotate(0)
                    fill(l, 1)
                    rotate(1)
                    mask_state(0)
                    if l == 0:
                        dve.wait_ge(logits_ps.sem, logits_ps.at(it, 1))
                        V.tensor_copy(lg[:, :, 0:E1], logits_of(E1)).then_inc(logits_read.sem, 1)
                        dve.wait_ge(logits_read.sem, logits_read.at(it, 1))
                        two_largest(body_link, it, E1, gap_ready)
                    fill(l, 2)
                    mask_state(1)
                    fill(l, 3)
                    causal(0, range(0, 8))
                    if l == 0:
                        dve.wait_ge(tanh_ready.sem, tanh_ready.at(it, 1))
                        weights_of_experts(body_link, it, E1, comb)
                    fill(l, 4)
                    causal(1, range(0, 6))
                    read_variances(0)
                    causal(1, range(6, 8))
                    weigh_gates(0)
                    fill(l, 5)
                    widen_roots(0)
                    fill(l, 6)
                    read_variances(1)
                    group_norm(0)
                    weigh_gates(1)
                    fill(l, 7)
                    widen_roots(1)
                    add_retention(0)
                    fill(l, 8)
                    group_norm(1)
                    normalise(it, NB * (2 + 2 * l), 0, Yr, xh, ln_ready)
                    fill(l, 9)
                    add_retention(1)
                    fill(l, 10)
                    normalise(it, NB * (2 + 2 * l) + 1, 1, Yr, xh, ln_ready)
                    fill(l, 11)
                    if l == HEAD_LAYER and nxt is not None:
                        head_statistics(nxt)
                    add_ffn(0)
                    fill(l, 12)
                    if l + 1 < L1:
                        normalise(it, NB * (3 + 2 * l), 0, X, xh, ln_ready)
                    add_ffn(1)
                    if l == HEAD_LAYER and nxt is not None:
                        head_normalise(nxt)
                    if l + 1 == L1:
                        dve.wait_ge(down1_added.sem, down1_added.at(it, NB * (E1 + 1)))
                        V.tensor_tensor(X[:].rearrange("p k c -> p (k c)"), x1[:].rearrange("p k c -> p (k c)"),
                                        X[:].rearrange("p k c -> p (k c)"), ALU.add).then_inc(out_ready.sem, 1)
                    fill(l, 13)
                    if l + 1 < L1:
                        normalise(it, NB * (3 + 2 * l) + 1, 1, X, xh, ln_ready)
                assert steps[1] == BODY_STEPS, steps

            head_statistics(0)
            head_normalise(0)
            for piece in head:
                run(piece, None, 0)
            assert steps[0] == HEAD_STEPS, steps
            dve.wait_ge(rest_in, 16 * (len(w) - len(FIRST)))
            with dve.Fori(0, passes - 1) as it:
                first_block(it)
                second_block(it, it + 1)
            first_block(passes - 1)
            second_block(passes - 1, None)


def laid_out(a):
    f = np.float32

    def z(*s):
        return np.zeros(s, f)

    w = {}
    wq, wk = z(P, 4, HG, HR), z(P, 4, HG, HR)
    for r in (0, 8, 16):
        wq[..., r:r + 8] = a["L0_attn_Wq"].T.reshape(P, 4, HG, DH0)
        wk[..., r:r + 8] = a["L0_attn_Wk"].T.reshape(P, 4, HG, DH0)
    w["wq"], w["wk"] = wq, wk
    w["wv"] = a["L0_attn_Wv"].T
    wo = z(4, 32, 4, P)
    wo[:, 0:8] = a["L0_attn_Wo"].T.reshape(4, 4, 8, P).transpose(1, 2, 0, 3)
    w["wo"] = wo
    w["gate0"] = a["L0_ffn_gate_w"].T
    w["bias0"] = np.broadcast_to(a["L0_ffn_expert_bias"][None, None], (P, NT, EALL0))
    w["w1"] = a["L0_ffn_w1"].transpose(2, 0, 1)
    w["w2"] = a["L0_ffn_w2"].reshape(E0, P, 2, P).transpose(3, 0, 2, 1)
    swap = np.arange(P) ^ 1
    for n in ("q", "k"):
        m = a[f"L1_attn_W{n}"].transpose(1, 0, 2)
        w[f"w{n}1"] = m
        w[f"w{n}s1"] = m[:, :, swap]
    w["wvT1"] = a["L1_attn_Wv"].transpose(2, 0, 1)
    wg = z(P, L1, 2, 4, 32)
    wg[..., 0:16] = a["L1_attn_Wg"].transpose(1, 0, 2).reshape(P, L1, 2, 4, 16)
    w["wg1"] = wg
    wo = z(4, 32, L1, 2, P)
    wo[:, 0:16] = a["L1_attn_Wo"].reshape(L1, 2, 4, 16, P).transpose(2, 3, 0, 1, 4)
    w["wo1"] = wo
    w["w11"] = a["L1_attn_W1"].transpose(1, 0, 2)
    w["w21"] = a["L1_attn_W2"].reshape(L1, 2, P, P).transpose(2, 0, 1, 3)
    w["ln_s"] = a["L1_attn_ln_scale"][:, None]
    w["ln_b"] = a["L1_attn_ln_bias"][:, None]
    for n, s in (("gn_s", "scale"), ("gn_b", "bias")):
        g = z(4, 32, L1, 2)
        g[:, 0:16] = a[f"L1_attn_gn_{s}"].reshape(L1, 2, 4, 16).transpose(2, 3, 0, 1)
        w[n] = g
    w["gate1"] = a["L1_ffn_gate_w"].T
    up, half = a["L1_ffn_w_up"], 192
    blocks = []
    for p in range(E1 // 2):
        for e in (2 * p, 2 * p + 1):
            blocks += [up[e, 0:P], up[e, half:half + P]]
        for o in (0, half):
            blocks.append(np.concatenate([up[2 * p, o + P:o + half], up[2 * p + 1, o + P:o + half]]))
    sg, su = a["L1_ffn_sg_gate"], a["L1_ffn_sg_up"]
    blocks += [sg[0:P], su[0:P]]
    blocks += [np.concatenate([s[P:half], z(64, P)]) for s in (sg, su)]
    w["wup"] = np.stack(blocks).transpose(2, 0, 1)
    dn = z(P, E1 + 1, 2, P)
    for e in range(E1 + 1):
        m = (a["L1_ffn_w_down"][e] if e < E1 else a["L1_ffn_sg_down"]).T
        o = 64 * (e % 2) if e < E1 else 0
        dn[:, e, 0] = m[0:P]
        dn[o:o + 64, e, 1] = m[P:half]
    w["wdn"] = dn
    return {n: np.ascontiguousarray(v.reshape(P, -1)) for n, v in w.items()}


def kernel(**inputs):
    import concourse.bacc as bacc
    from concourse.bass_utils import run_bass_kernel_spmd

    a = {n: np.asarray(v) for n, v in inputs.items()}
    shape = a["L0_attn_x"].shape
    arrays = laid_out(a)
    arrays.update(shape_constants())
    nc = bacc.Bacc("TRN2", target_bir_lowering=False, num_devices=1)
    w = {n: nc.dram_tensor("w_" + n, v.shape, mybir.dt.from_np(v.dtype), kind="ExternalInput").ap() for n, v in arrays.items()}
    x = np.ascontiguousarray(a["L0_attn_x"].reshape(-1, D))
    x_dram = nc.dram_tensor("x", x.shape, F32, kind="ExternalInput").ap()
    out = nc.dram_tensor("out", x.shape, F32, kind="ExternalOutput").ap()
    program(nc, x_dram, out, w)
    feed = {"w_" + n: v for n, v in arrays.items()}
    feed["x"] = x
    r = run_bass_kernel_spmd(nc, [feed], core_ids=[0])
    return r.results[0]["out"].reshape(shape)
```
